# Optimizing a Trainium2 kernel written in Bass

```python
import numpy as np
import jax
import jax.numpy as jnp

def _softmax(x, axis=-1):
    return jax.nn.softmax(x, axis=axis)

def _gelu(x):
    return jax.nn.gelu(x, approximate=True)

def _silu(x):
    return jax.nn.silu(x)

def _sigmoid(x):
    return jax.nn.sigmoid(x)

def _layernorm(x, axis=-1, eps=1e-05):
    m = jnp.mean(x, axis=axis, keepdims=True)
    v = jnp.var(x, axis=axis, keepdims=True)
    return (x - m) / jnp.sqrt(v + eps)

def _scatter_add(tgt, idx, src, axis=0):
    return tgt.at[idx].add(src)

def _segment_sum(src, seg, n):
    return jax.ops.segment_sum(src, seg, n)
kernel_name = 'mk_flamingo_gated_d4_seqx_r8_1a2d3a'

def setup_inputs(seed: int=0):
    np.random.seed(seed)
    _w = jnp.asarray

    def _rec_inputs():
        import jax
        import jax.numpy as jnp
        _rk = jax.random.key(seed)
        x = 7.22e-05 + 1 * jax.random.normal(jax.random.fold_in(_rk, 1), (128, 64, 128), jnp.float32)
        _lenS = 64 - jax.random.randint(jax.random.fold_in(_rk, 7), (128,), 0, max(1, 64 // 4) + 1, jnp.int32)
        _lenS2 = 64 - jax.random.randint(jax.random.fold_in(_rk, 8), (128,), 0, max(1, 64 // 4) + 1, jnp.int32)
        _ctx_768P = jax.random.normal(jax.random.fold_in(_rk, 11), (128, 16, 96), jnp.float32)
        _ctx_768c = jax.random.dirichlet(jax.random.fold_in(_rk, 511), 0.3 * jnp.ones((16,), jnp.float32), (128, 64))
        _ctx_768t = jnp.einsum('bsk,bkd->bsd', _ctx_768c, _ctx_768P)
        _ctx_768t = _ctx_768t * jax.lax.rsqrt(jnp.mean(jnp.square(_ctx_768t)) + 1e-12) * 0.953939
        ctx_768 = -0.000191848 + 0.999787 * (_ctx_768t + 0.3 * jax.random.normal(jax.random.fold_in(_rk, 611), (128, 64, 96), jnp.float32))
        _validS = jnp.arange(64)[None, :] < _lenS[:, None]
        _validS2 = jnp.arange(64)[None, :] < _lenS2[:, None]
        _causal = jnp.tril(jnp.ones((64, 64), dtype=bool))
        mask_BxS2_bk0 = jnp.logical_not(jnp.broadcast_to(_validS2[:, :], (128, 64)))
        mask_BxS2_bf1 = jnp.ones((128, 64), dtype=bool)
        _g = jax.random.normal(jax.random.fold_in(_rk, 9001), (2, 4), jnp.float32)
        _g = jnp.sign(_g) * jnp.maximum(jnp.abs(_g), 1.0) + (_g == 0) * 1.0
        g_xattn = _g[0]
        g_ffn = _g[1]
        return (x, ctx_768, mask_BxS2_bk0, mask_BxS2_bf1, g_xattn, g_ffn)
    x, ctx_768, mask_BxS2_bk0, mask_BxS2_bf1, g_xattn, g_ffn = _rec_inputs()

    def _L0_xattn_setup():
        import jax, jax.numpy as jnp
        import numpy as np
        HEADS = 8
        DIM_HEAD = 64
        QUERY_DIM = 128
        CONTEXT_DIM = 96
        INNER = HEADS * DIM_HEAD
        key = jax.random.key(seed)
        ks = jax.random.split(key, 8)
        b, n, j = (4, 256, 256)
        x = jax.random.normal(ks[0], (b, n, QUERY_DIM), dtype=jnp.float32)
        context = jax.random.normal(ks[1], (b, j, CONTEXT_DIM), dtype=jnp.float32)
        mask = jax.random.randint(ks[2], (b, j), 0, 2).astype(jnp.bool_)
        W_q = jax.random.normal(ks[3], (QUERY_DIM, INNER), dtype=jnp.float32) / np.sqrt(QUERY_DIM)
        W_k = jax.random.normal(ks[4], (CONTEXT_DIM, INNER), dtype=jnp.float32) / np.sqrt(CONTEXT_DIM)
        W_v = jax.random.normal(ks[5], (CONTEXT_DIM, INNER), dtype=jnp.float32) / np.sqrt(CONTEXT_DIM)
        W_o = jax.random.normal(ks[6], (INNER, QUERY_DIM), dtype=jnp.float32) / np.sqrt(INNER)
        b_o = jax.random.normal(ks[7], (QUERY_DIM,), dtype=jnp.float32) * 0.01
        return {'x': x, 'context': context, 'mask': mask, 'W_q': W_q, 'W_k': W_k, 'W_v': W_v, 'W_o': W_o, 'b_o': b_o}
    _L0_xattn_all = _L0_xattn_setup()
    _L0_xattn_in = {k: v for k, v in _L0_xattn_all.items() if k in ('W_q', 'W_k', 'W_v', 'W_o', 'b_o')}
    del _L0_xattn_all

    def _L0_ffn_setup():
        import jax, jax.numpy as jnp
        import numpy as np
        HIDDEN = 128
        HEAD_DIM = 64
        N_EXPERTS = 16
        MIN_EXPERTS = 2
        B, T = (4, 256)

        def _normalize(x, axis):
            n = jnp.sqrt(jnp.sum(x * x, axis=axis, keepdims=True))
            return x / jnp.maximum(n, 1e-12)

        def _ste(x):
            hard = jax.lax.stop_gradient((x > 0).astype(x.dtype))
            return hard + x - jax.lax.stop_gradient(x)

        def _gating(hidden_states, sim_matrix, gates):
            b, t, c = hidden_states.shape
            flat = hidden_states.reshape(b * t, c)
            logits = _normalize(flat, -1) @ _normalize(sim_matrix, 0) - jax.nn.sigmoid(gates)
            gated = jax.nn.relu(logits)
            mask = _ste(gated)
            inactive = jnp.sum(mask, axis=1) == 0
            _, fb_idx = jax.lax.top_k(logits, MIN_EXPERTS)
            fb = jnp.zeros_like(mask).at[jnp.arange(b * t)[:, None], fb_idx].set(1.0)
            fb_applied = inactive[:, None] & (fb > 0)
            mask = jnp.where(fb_applied, 1.0, mask)
            masked_logits = jnp.where(mask > 0, gated, -jnp.inf)
            return jax.nn.softmax(masked_logits, axis=-1).reshape(b, t, -1)
        key = jax.random.key(seed)
        ks = jax.random.split(key, 6)
        xav_qkv = float(np.sqrt(6.0 / (HIDDEN + HEAD_DIM)))
        return {'hidden_states': jax.random.normal(ks[0], (B, T, HIDDEN), dtype=jnp.float32), 'sim_matrix': jax.random.normal(ks[1], (HIDDEN, N_EXPERTS), dtype=jnp.float32), 'gates': jnp.zeros((N_EXPERTS,), dtype=jnp.float32), 'q_proj': jax.random.uniform(ks[2], (N_EXPERTS, HIDDEN, HEAD_DIM), jnp.float32, -xav_qkv, xav_qkv), 'k_proj': jax.random.uniform(ks[3], (N_EXPERTS, HIDDEN, HEAD_DIM), jnp.float32, -xav_qkv, xav_qkv), 'v_proj': jax.random.uniform(ks[4], (N_EXPERTS, HIDDEN, HEAD_DIM), jnp.float32, -xav_qkv, xav_qkv), 'o_proj': jax.random.uniform(ks[5], (N_EXPERTS, HEAD_DIM, HIDDEN), jnp.float32, -xav_qkv, xav_qkv)}
    _L0_ffn_all = _L0_ffn_setup()
    _L0_ffn_in = {k: v for k, v in _L0_ffn_all.items() if k in ('sim_matrix', 'gates', 'q_proj', 'k_proj', 'v_proj', 'o_proj')}
    del _L0_ffn_all

    def _L1_xattn_setup():
        import jax, jax.numpy as jnp
        import numpy as np
        QUERY_DIM = 128
        CONTEXT_DIM = 96
        HEADS = 8
        DIM_HEAD = 64
        INNER = HEADS * DIM_HEAD
        key = jax.random.key(seed)
        ks = jax.random.split(key, 7)
        B, S, L = (8, 512, 77)
        x = jax.random.normal(ks[0], (B, S, QUERY_DIM), dtype=jnp.float32)
        context = jax.random.normal(ks[1], (B, L, CONTEXT_DIM), dtype=jnp.float32)
        Wq = jax.random.normal(ks[2], (QUERY_DIM, INNER), dtype=jnp.float32) * QUERY_DIM ** (-0.5)
        Wk = jax.random.normal(ks[3], (CONTEXT_DIM, INNER), dtype=jnp.float32) * CONTEXT_DIM ** (-0.5)
        Wv = jax.random.normal(ks[4], (CONTEXT_DIM, INNER), dtype=jnp.float32) * CONTEXT_DIM ** (-0.5)
        Wo = jax.random.normal(ks[5], (INNER, QUERY_DIM), dtype=jnp.float32) * INNER ** (-0.5)
        bo = jax.random.normal(ks[6], (QUERY_DIM,), dtype=jnp.float32) * 0.01
        return {'x': x, 'context': context, 'Wq': Wq, 'Wk': Wk, 'Wv': Wv, 'Wo': Wo, 'bo': bo}
    _L1_xattn_all = _L1_xattn_setup()
    _L1_xattn_in = {k: v for k, v in _L1_xattn_all.items() if k in ('Wq', 'Wk', 'Wv', 'Wo', 'bo')}
    del _L1_xattn_all

    def _L1_ffn_setup():
        import jax, jax.numpy as jnp
        import numpy as np
        B, N, D = (4, 256, 128)
        SPARSITY = 0.01
        key = jax.random.key(seed)
        k1, k2, k3 = jax.random.split(key, 3)
        x = jax.random.normal(k1, (B, N, D), dtype=jnp.float32)
        spatial = jax.random.normal(k2, (D, D), dtype=jnp.float32) * 0.02
        freq = jnp.fft.fft(spatial, axis=-1)
        k = int(D * SPARSITY)
        mag = jnp.abs(freq)
        kth = jax.lax.top_k(mag, k)[0][:, -1:]
        w_sparse = jnp.where(mag >= kth, freq, 0.0 + 0j)
        bias = jax.random.normal(k3, (D,), dtype=jnp.float32) * 0.01
        return {'x': x, 'w_freq_real': jnp.real(w_sparse).astype(jnp.float32), 'w_freq_imag': jnp.imag(w_sparse).astype(jnp.float32), 'bias': bias}
    _L1_ffn_all = _L1_ffn_setup()
    _L1_ffn_in = {k: v for k, v in _L1_ffn_all.items() if k in ('w_freq_real', 'w_freq_imag', 'bias')}
    del _L1_ffn_all

    def _L2_xattn_setup():
        import jax, jax.numpy as jnp
        import numpy as np
        NUM_HEADS = 16
        CLAMP = 10000.0
        key = jax.random.key(seed)
        ks = jax.random.split(key, 8)
        B, Nq, Nkv, Cq, Ckv = (4, 256, 256, 128, 96)
        s_q = 1.0 / np.sqrt(Cq)
        s_kv = 1.0 / np.sqrt(Ckv)
        return {'query': jax.random.normal(ks[0], (B, Nq, Cq), jnp.float32), 'key_value': jax.random.normal(ks[1], (B, Nkv, Ckv), jnp.float32), 'Wq': jax.random.normal(ks[2], (Cq, Cq), jnp.float32) * s_q, 'bq': jnp.zeros((Cq,), jnp.float32), 'Wk': jax.random.normal(ks[3], (Ckv, Cq), jnp.float32) * s_kv, 'bk': jnp.zeros((Cq,), jnp.float32), 'Wv': jax.random.normal(ks[4], (Ckv, Cq), jnp.float32) * s_kv, 'bv': jnp.zeros((Cq,), jnp.float32), 'Wo': jax.random.normal(ks[5], (Cq, Cq), jnp.float32) * s_q, 'bo': jnp.zeros((Cq,), jnp.float32)}
    _L2_xattn_all = _L2_xattn_setup()
    _L2_xattn_in = {k: v for k, v in _L2_xattn_all.items() if k in ('Wq', 'bq', 'Wk', 'bk', 'Wv', 'bv', 'Wo', 'bo')}
    del _L2_xattn_all

    def _L2_ffn_setup():
        import jax, jax.numpy as jnp
        import numpy as np
        N_EXPERTS = 32
        TOP_K = 8
        N_GROUP = 4
        TOPK_GROUP = 2
        ROUTED_SCALING = 2.5

        def _gate(x, gate_w, gate_bias):
            T, E = (x.shape[0], gate_w.shape[0])
            logits = jnp.einsum('th,eh->te', x, gate_w)
            scores = jax.nn.sigmoid(logits)
            scores_choice = scores + gate_bias[None, :]
            grp = scores_choice.reshape(T, N_GROUP, E // N_GROUP)
            top2, _ = jax.lax.top_k(grp, 2)
            group_scores = top2.sum(-1)
            _, grp_idx = jax.lax.top_k(group_scores, TOPK_GROUP)
            group_mask = jax.nn.one_hot(grp_idx, N_GROUP, dtype=scores.dtype).sum(1)
            expert_mask = jnp.repeat(group_mask, E // N_GROUP, axis=1)
            masked = jnp.where(expert_mask > 0, scores_choice, 0.0)
            _, topk_idx = jax.lax.top_k(masked, TOP_K)
            topk_w = jnp.take_along_axis(scores, topk_idx, axis=1)
            topk_w = topk_w / (topk_w.sum(-1, keepdims=True) + 1e-20)
            topk_w = topk_w * ROUTED_SCALING
            return (topk_idx, topk_w)

        def _mlp(x, wg, wu, wd):
            return jnp.einsum('...i,hi->...h', jax.nn.silu(jnp.einsum('...h,ih->...i', x, wg)) * jnp.einsum('...h,ih->...i', x, wu), wd)
        key = jax.random.key(seed)
        ks = jax.random.split(key, 9)
        B, S, H, I = (2, 64, 128, 64)
        w = 0.02
        return {'hidden_states': jax.random.normal(ks[0], (B, S, H), jnp.float32), 'gate_w': jax.random.normal(ks[1], (N_EXPERTS, H), jnp.float32) * w, 'gate_bias': jax.random.normal(ks[2], (N_EXPERTS,), jnp.float32) * w, 'expert_gate': jax.random.normal(ks[3], (N_EXPERTS, I, H), jnp.float32) * w, 'expert_up': jax.random.normal(ks[4], (N_EXPERTS, I, H), jnp.float32) * w, 'expert_down': jax.random.normal(ks[5], (N_EXPERTS, H, I), jnp.float32) * w, 'shared_gate': jax.random.normal(ks[6], (2 * I, H), jnp.float32) * w, 'shared_up': jax.random.normal(ks[7], (2 * I, H), jnp.float32) * w, 'shared_down': jax.random.normal(ks[8], (H, 2 * I), jnp.float32) * w}
    _L2_ffn_all = _L2_ffn_setup()
    _L2_ffn_in = {k: v for k, v in _L2_ffn_all.items() if k in ('gate_w', 'gate_bias', 'expert_gate', 'expert_up', 'expert_down', 'shared_gate', 'shared_up', 'shared_down')}
    del _L2_ffn_all

    def _L3_xattn_setup():
        import jax, jax.numpy as jnp
        import numpy as np
        import math
        B, N, M = (4, 128, 128)
        DIM, CTX_DIM = (128, 96)
        HEADS, DIM_HEAD = (16, 64)
        INNER = HEADS * DIM_HEAD

        def layer_norm(t, g, eps=1e-05):
            mean = jnp.mean(t, axis=-1, keepdims=True)
            var = jnp.mean((t - mean) ** 2, axis=-1, keepdims=True)
            return (t - mean) * jax.lax.rsqrt(var + eps) * g
        key = jax.random.key(seed)
        ks = jax.random.split(key, 8)
        return {'x': jax.random.normal(ks[0], (B, N, DIM), jnp.float32), 'context': jax.random.normal(ks[1], (B, M, CTX_DIM), jnp.float32), 'mask': jnp.ones((B, M), dtype=bool), 'g_norm': jnp.ones((DIM,), jnp.float32), 'null_kv': jax.random.normal(ks[2], (2, DIM_HEAD), jnp.float32), 'Wq': jax.random.normal(ks[3], (DIM, INNER), jnp.float32) * DIM ** (-0.5), 'Wkv': jax.random.normal(ks[4], (CTX_DIM, 2 * INNER), jnp.float32) * CTX_DIM ** (-0.5), 'Wout': jax.random.normal(ks[5], (INNER, DIM), jnp.float32) * INNER ** (-0.5), 'g_out': jnp.ones((DIM,), jnp.float32)}
    _L3_xattn_all = _L3_xattn_setup()
    _L3_xattn_in = {k: v for k, v in _L3_xattn_all.items() if k in ('g_norm', 'null_kv', 'Wq', 'Wkv', 'Wout', 'g_out')}
    del _L3_xattn_all

    def _L3_ffn_setup():
        import jax, jax.numpy as jnp
        import numpy as np
        D_MODEL, D_FF, RANK = (128, 512, 32)
        B, S = (4, 512)
        key = jax.random.key(seed)
        ks = jax.random.split(key, 7)
        return {'x': jax.random.normal(ks[0], (B, S, D_MODEL), dtype=jnp.float32), 'U1': jax.random.normal(ks[1], (D_MODEL, RANK), dtype=jnp.float32) * 0.02, 'V1': jax.random.normal(ks[2], (RANK, D_FF), dtype=jnp.float32) * 0.02, 'b1': jnp.zeros((D_FF,), dtype=jnp.float32), 'U2': jax.random.normal(ks[3], (D_FF, RANK), dtype=jnp.float32) * 0.02, 'V2': jax.random.normal(ks[4], (RANK, D_MODEL), dtype=jnp.float32) * 0.02, 'b2': jnp.zeros((D_MODEL,), dtype=jnp.float32)}
    _L3_ffn_all = _L3_ffn_setup()
    _L3_ffn_in = {k: v for k, v in _L3_ffn_all.items() if k in ('U1', 'V1', 'b1', 'U2', 'V2', 'b2')}
    del _L3_ffn_all
    return {'x': x, 'ctx_768': ctx_768, 'mask_BxS2_bk0': mask_BxS2_bk0, 'mask_BxS2_bf1': mask_BxS2_bf1, 'g_xattn': g_xattn, 'g_ffn': g_ffn, 'L0_xattn_W_q': _L0_xattn_in['W_q'], 'L0_xattn_W_k': _L0_xattn_in['W_k'], 'L0_xattn_W_v': _L0_xattn_in['W_v'], 'L0_xattn_W_o': _L0_xattn_in['W_o'], 'L0_xattn_b_o': _L0_xattn_in['b_o'], 'L0_ffn_sim_matrix': _L0_ffn_in['sim_matrix'], 'L0_ffn_gates': _L0_ffn_in['gates'], 'L0_ffn_q_proj': _L0_ffn_in['q_proj'], 'L0_ffn_k_proj': _L0_ffn_in['k_proj'], 'L0_ffn_v_proj': _L0_ffn_in['v_proj'], 'L0_ffn_o_proj': _L0_ffn_in['o_proj'], 'L1_xattn_Wq': _L1_xattn_in['Wq'], 'L1_xattn_Wk': _L1_xattn_in['Wk'], 'L1_xattn_Wv': _L1_xattn_in['Wv'], 'L1_xattn_Wo': _L1_xattn_in['Wo'], 'L1_xattn_bo': _L1_xattn_in['bo'], 'L1_ffn_w_freq_real': _L1_ffn_in['w_freq_real'], 'L1_ffn_w_freq_imag': _L1_ffn_in['w_freq_imag'], 'L1_ffn_bias': _L1_ffn_in['bias'], 'L2_xattn_Wq': _L2_xattn_in['Wq'], 'L2_xattn_bq': _L2_xattn_in['bq'], 'L2_xattn_Wk': _L2_xattn_in['Wk'], 'L2_xattn_bk': _L2_xattn_in['bk'], 'L2_xattn_Wv': _L2_xattn_in['Wv'], 'L2_xattn_bv': _L2_xattn_in['bv'], 'L2_xattn_Wo': _L2_xattn_in['Wo'], 'L2_xattn_bo': _L2_xattn_in['bo'], 'L2_ffn_gate_w': _L2_ffn_in['gate_w'], 'L2_ffn_gate_bias': _L2_ffn_in['gate_bias'], 'L2_ffn_expert_gate': _L2_ffn_in['expert_gate'], 'L2_ffn_expert_up': _L2_ffn_in['expert_up'], 'L2_ffn_expert_down': _L2_ffn_in['expert_down'], 'L2_ffn_shared_gate': _L2_ffn_in['shared_gate'], 'L2_ffn_shared_up': _L2_ffn_in['shared_up'], 'L2_ffn_shared_down': _L2_ffn_in['shared_down'], 'L3_xattn_g_norm': _L3_xattn_in['g_norm'], 'L3_xattn_null_kv': _L3_xattn_in['null_kv'], 'L3_xattn_Wq': _L3_xattn_in['Wq'], 'L3_xattn_Wkv': _L3_xattn_in['Wkv'], 'L3_xattn_Wout': _L3_xattn_in['Wout'], 'L3_xattn_g_out': _L3_xattn_in['g_out'], 'L3_ffn_U1': _L3_ffn_in['U1'], 'L3_ffn_V1': _L3_ffn_in['V1'], 'L3_ffn_b1': _L3_ffn_in['b1'], 'L3_ffn_U2': _L3_ffn_in['U2'], 'L3_ffn_V2': _L3_ffn_in['V2'], 'L3_ffn_b2': _L3_ffn_in['b2']}

def reference(x, ctx_768, mask_BxS2_bk0, mask_BxS2_bf1, g_xattn, g_ffn, L0_xattn_W_q, L0_xattn_W_k, L0_xattn_W_v, L0_xattn_W_o, L0_xattn_b_o, L0_ffn_sim_matrix, L0_ffn_gates, L0_ffn_q_proj, L0_ffn_k_proj, L0_ffn_v_proj, L0_ffn_o_proj, L1_xattn_Wq, L1_xattn_Wk, L1_xattn_Wv, L1_xattn_Wo, L1_xattn_bo, L1_ffn_w_freq_real, L1_ffn_w_freq_imag, L1_ffn_bias, L2_xattn_Wq, L2_xattn_bq, L2_xattn_Wk, L2_xattn_bk, L2_xattn_Wv, L2_xattn_bv, L2_xattn_Wo, L2_xattn_bo, L2_ffn_gate_w, L2_ffn_gate_bias, L2_ffn_expert_gate, L2_ffn_expert_up, L2_ffn_expert_down, L2_ffn_shared_gate, L2_ffn_shared_up, L2_ffn_shared_down, L3_xattn_g_norm, L3_xattn_null_kv, L3_xattn_Wq, L3_xattn_Wkv, L3_xattn_Wout, L3_xattn_g_out, L3_ffn_U1, L3_ffn_V1, L3_ffn_b1, L3_ffn_U2, L3_ffn_V2, L3_ffn_b2):
    import jax
    import jax.numpy as jnp

    def _L0_xattn_ref(x, context, mask, W_q, W_k, W_v, W_o, b_o):
        import jax, jax.numpy as jnp
        import numpy as np
        HEADS = 8
        DIM_HEAD = 64
        QUERY_DIM = 128
        CONTEXT_DIM = 96
        INNER = HEADS * DIM_HEAD
        b, n, _ = x.shape
        j = context.shape[1]
        scale = DIM_HEAD ** (-0.5)
        q = (x @ W_q).reshape(b, n, HEADS, DIM_HEAD)
        k = (context @ W_k).reshape(b, j, HEADS, DIM_HEAD)
        v = (context @ W_v).reshape(b, j, HEADS, DIM_HEAD)
        sim = jnp.einsum('bihd,bjhd->bhij', q, k) * scale
        max_neg = -jnp.finfo(sim.dtype).max
        sim = jnp.where(mask[:, None, None, :], sim, max_neg)
        attn = jax.nn.softmax(sim, axis=-1)
        out = jnp.einsum('bhij,bjhd->bihd', attn, v).reshape(b, n, INNER)
        return out @ W_o + b_o

    def _L0_ffn_ref(hidden_states, sim_matrix, gates, q_proj, k_proj, v_proj, o_proj):
        import jax, jax.numpy as jnp
        import numpy as np
        HIDDEN = 128
        HEAD_DIM = 64
        N_EXPERTS = 16
        MIN_EXPERTS = 2
        B, T = (4, 256)

        def _normalize(x, axis):
            n = jnp.sqrt(jnp.sum(x * x, axis=axis, keepdims=True))
            return x / jnp.maximum(n, 1e-12)

        def _ste(x):
            hard = jax.lax.stop_gradient((x > 0).astype(x.dtype))
            return hard + x - jax.lax.stop_gradient(x)

        def _gating(hidden_states, sim_matrix, gates):
            b, t, c = hidden_states.shape
            flat = hidden_states.reshape(b * t, c)
            logits = _normalize(flat, -1) @ _normalize(sim_matrix, 0) - jax.nn.sigmoid(gates)
            gated = jax.nn.relu(logits)
            mask = _ste(gated)
            inactive = jnp.sum(mask, axis=1) == 0
            _, fb_idx = jax.lax.top_k(logits, MIN_EXPERTS)
            fb = jnp.zeros_like(mask).at[jnp.arange(b * t)[:, None], fb_idx].set(1.0)
            fb_applied = inactive[:, None] & (fb > 0)
            mask = jnp.where(fb_applied, 1.0, mask)
            masked_logits = jnp.where(mask > 0, gated, -jnp.inf)
            return jax.nn.softmax(masked_logits, axis=-1).reshape(b, t, -1)
        b, t, c = hidden_states.shape
        rw = _gating(hidden_states, sim_matrix, gates)
        q = jnp.einsum('bte,bted->btd', rw, jnp.einsum('btc,ecd->bted', hidden_states, q_proj))
        k = jnp.einsum('bte,bted->btd', rw, jnp.einsum('btc,ecd->bted', hidden_states, k_proj))
        v = jnp.einsum('bte,bted->btd', rw, jnp.einsum('btc,ecd->bted', hidden_states, v_proj))
        scale = 1.0 / jnp.sqrt(jnp.asarray(HEAD_DIM, dtype=q.dtype))
        scores = jnp.einsum('bqd,bkd->bqk', q, k) * scale
        causal = jnp.tril(jnp.ones((t, t), dtype=bool))
        scores = jnp.where(causal, scores, -jnp.inf)
        attn = jnp.einsum('bqk,bkd->bqd', jax.nn.softmax(scores, axis=-1), v)
        mixed = attn[:, :, None, :] * rw[..., None]
        return jnp.einsum('bted,edc->btc', mixed, o_proj)

    def _L1_xattn_ref(x, context, Wq, Wk, Wv, Wo, bo):
        import jax, jax.numpy as jnp
        import numpy as np
        QUERY_DIM = 128
        CONTEXT_DIM = 96
        HEADS = 8
        DIM_HEAD = 64
        INNER = HEADS * DIM_HEAD
        B, S, _ = x.shape
        L = context.shape[1]
        scale = DIM_HEAD ** (-0.5)
        q = (x @ Wq).reshape(B, S, HEADS, DIM_HEAD).transpose(0, 2, 1, 3)
        k = (context @ Wk).reshape(B, L, HEADS, DIM_HEAD).transpose(0, 2, 1, 3)
        v = (context @ Wv).reshape(B, L, HEADS, DIM_HEAD).transpose(0, 2, 1, 3)
        attn = jnp.einsum('bhsd,bhld->bhsl', q, k) * scale
        attn = jax.nn.softmax(attn, axis=-1)
        out = jnp.einsum('bhsl,bhld->bhsd', attn, v)
        out = out.transpose(0, 2, 1, 3).reshape(B, S, INNER)
        return out @ Wo + bo

    def _L1_ffn_ref(x, w_freq_real, w_freq_imag, bias):
        import jax, jax.numpy as jnp
        import numpy as np
        B, N, D = (4, 256, 128)
        SPARSITY = 0.01
        w = jax.lax.complex(w_freq_real, w_freq_imag)
        x_freq = jnp.fft.fft(x, axis=-1)
        y_freq = jnp.einsum('bnd,do->bno', x_freq, w)
        y = jnp.real(jnp.fft.ifft(y_freq, axis=-1))
        return y + bias

    def _L2_xattn_ref(query, key_value, Wq, bq, Wk, bk, Wv, bv, Wo, bo):
        import jax, jax.numpy as jnp
        import numpy as np
        NUM_HEADS = 16
        CLAMP = 10000.0
        B, Nq, Cq = query.shape
        Nkv = key_value.shape[1]
        H = NUM_HEADS
        D = Cq // H
        scale = D ** (-0.5)
        q = (query @ Wq + bq).reshape(B, Nq, H, D).transpose(0, 2, 1, 3)
        k = (key_value @ Wk + bk).reshape(B, Nkv, H, D).transpose(0, 2, 1, 3)
        v = (key_value @ Wv + bv).reshape(B, Nkv, H, D).transpose(0, 2, 1, 3)
        attn = jnp.einsum('bhqd,bhkd->bhqk', q, k) * scale
        attn = jnp.clip(attn, -CLAMP, CLAMP)
        attn = jax.nn.softmax(attn, axis=-1)
        attn = jnp.where(jnp.any(jnp.isnan(attn)), jnp.asarray(1.0 / Nkv, attn.dtype), attn)
        x = jnp.einsum('bhqk,bhkd->bqhd', attn, v).reshape(B, Nq, Cq)
        return x @ Wo + bo

    def _L2_ffn_ref(hidden_states, gate_w, gate_bias, expert_gate, expert_up, expert_down, shared_gate, shared_up, shared_down):
        import jax, jax.numpy as jnp
        import numpy as np
        N_EXPERTS = 32
        TOP_K = 8
        N_GROUP = 4
        TOPK_GROUP = 2
        ROUTED_SCALING = 2.5

        def _gate(x, gate_w, gate_bias):
            T, E = (x.shape[0], gate_w.shape[0])
            logits = jnp.einsum('th,eh->te', x, gate_w)
            scores = jax.nn.sigmoid(logits)
            scores_choice = scores + gate_bias[None, :]
            grp = scores_choice.reshape(T, N_GROUP, E // N_GROUP)
            top2, _ = jax.lax.top_k(grp, 2)
            group_scores = top2.sum(-1)
            _, grp_idx = jax.lax.top_k(group_scores, TOPK_GROUP)
            group_mask = jax.nn.one_hot(grp_idx, N_GROUP, dtype=scores.dtype).sum(1)
            expert_mask = jnp.repeat(group_mask, E // N_GROUP, axis=1)
            masked = jnp.where(expert_mask > 0, scores_choice, 0.0)
            _, topk_idx = jax.lax.top_k(masked, TOP_K)
            topk_w = jnp.take_along_axis(scores, topk_idx, axis=1)
            topk_w = topk_w / (topk_w.sum(-1, keepdims=True) + 1e-20)
            topk_w = topk_w * ROUTED_SCALING
            return (topk_idx, topk_w)

        def _mlp(x, wg, wu, wd):
            return jnp.einsum('...i,hi->...h', jax.nn.silu(jnp.einsum('...h,ih->...i', x, wg)) * jnp.einsum('...h,ih->...i', x, wu), wd)
        orig_shape = hidden_states.shape
        H = orig_shape[-1]
        residuals = hidden_states
        x = hidden_states.reshape(-1, H)
        topk_idx, topk_w = _gate(x, gate_w, gate_bias)
        g = jnp.einsum('th,eih->eti', x, expert_gate)
        u = jnp.einsum('th,eih->eti', x, expert_up)
        outs = jnp.einsum('eti,ehi->eth', jax.nn.silu(g) * u, expert_down)
        outs_t = jnp.transpose(outs, (1, 0, 2))
        gathered = jnp.take_along_axis(outs_t, topk_idx[:, :, None], axis=1)
        final = (gathered * topk_w[:, :, None]).sum(1)
        shared = _mlp(residuals, shared_gate, shared_up, shared_down)
        return final.reshape(orig_shape) + shared

    def _L3_xattn_ref(x, context, mask, g_norm, null_kv, Wq, Wkv, Wout, g_out):
        import jax, jax.numpy as jnp
        import numpy as np
        import math
        B, N, M = (4, 128, 128)
        DIM, CTX_DIM = (128, 96)
        HEADS, DIM_HEAD = (16, 64)
        INNER = HEADS * DIM_HEAD

        def layer_norm(t, g, eps=1e-05):
            mean = jnp.mean(t, axis=-1, keepdims=True)
            var = jnp.mean((t - mean) ** 2, axis=-1, keepdims=True)
            return (t - mean) * jax.lax.rsqrt(var + eps) * g
        b = x.shape[0]
        scale = DIM_HEAD ** (-0.5)
        sqrt_scale = math.sqrt(scale)
        x = layer_norm(x, g_norm)
        q = x @ Wq
        kv = context @ Wkv
        k, v = jnp.split(kv, 2, axis=-1)

        def to_heads(t):
            return t.reshape(b, t.shape[1], HEADS, DIM_HEAD).transpose(0, 2, 1, 3)
        q, k, v = (to_heads(q), to_heads(k), to_heads(v))
        nk = jnp.broadcast_to(null_kv[0], (b, HEADS, 1, DIM_HEAD))
        nv = jnp.broadcast_to(null_kv[1], (b, HEADS, 1, DIM_HEAD))
        k = jnp.concatenate([nk, k], axis=2)
        v = jnp.concatenate([nv, v], axis=2)
        q = q * sqrt_scale
        k = k * sqrt_scale
        sim = jnp.einsum('bhid,bhjd->bhij', q, k)
        max_neg = -jnp.finfo(sim.dtype).max
        full_mask = jnp.pad(mask, ((0, 0), (1, 0)), constant_values=True)
        sim = jnp.where(full_mask[:, None, None, :], sim, max_neg)
        attn = jax.nn.softmax(sim.astype(jnp.float32), axis=-1).astype(sim.dtype)
        out = jnp.einsum('bhij,bhjd->bhid', attn, v)
        out = out.transpose(0, 2, 1, 3).reshape(b, -1, INNER)
        out = out @ Wout
        return layer_norm(out, g_out)

    def _L3_ffn_ref(x, U1, V1, b1, U2, V2, b2):
        import jax, jax.numpy as jnp
        import numpy as np
        D_MODEL, D_FF, RANK = (128, 512, 32)
        B, S = (4, 512)
        P = jnp.einsum('bsd,dr->bsr', x, U1)
        H = jax.nn.gelu(jnp.einsum('bsr,rf->bsf', P, V1) + b1)
        Q = jnp.einsum('bsf,fr->bsr', H, U2)
        return jnp.einsum('bsr,rd->bsd', Q, V2) + b2
    x = x + jnp.tanh(g_xattn[0]) * _L0_xattn_ref(_layernorm(x, axis=-1), ctx_768, mask_BxS2_bk0, L0_xattn_W_q, L0_xattn_W_k, L0_xattn_W_v, L0_xattn_W_o, L0_xattn_b_o)
    x = x + jnp.tanh(g_ffn[0]) * _L0_ffn_ref(_layernorm(x, axis=-1), L0_ffn_sim_matrix, L0_ffn_gates, L0_ffn_q_proj, L0_ffn_k_proj, L0_ffn_v_proj, L0_ffn_o_proj)
    x = x + jnp.tanh(g_xattn[1]) * _L1_xattn_ref(_layernorm(x, axis=-1), ctx_768, L1_xattn_Wq, L1_xattn_Wk, L1_xattn_Wv, L1_xattn_Wo, L1_xattn_bo)
    x = x + jnp.tanh(g_ffn[1]) * _L1_ffn_ref(_layernorm(x, axis=-1), L1_ffn_w_freq_real, L1_ffn_w_freq_imag, L1_ffn_bias)
    x = x + jnp.tanh(g_xattn[2]) * _L2_xattn_ref(_layernorm(x, axis=-1), ctx_768, L2_xattn_Wq, L2_xattn_bq, L2_xattn_Wk, L2_xattn_bk, L2_xattn_Wv, L2_xattn_bv, L2_xattn_Wo, L2_xattn_bo)
    x = x + jnp.tanh(g_ffn[2]) * _L2_ffn_ref(_layernorm(x, axis=-1), L2_ffn_gate_w, L2_ffn_gate_bias, L2_ffn_expert_gate, L2_ffn_expert_up, L2_ffn_expert_down, L2_ffn_shared_gate, L2_ffn_shared_up, L2_ffn_shared_down)
    x = x + jnp.tanh(g_xattn[3]) * _L3_xattn_ref(_layernorm(x, axis=-1), ctx_768, mask_BxS2_bf1, L3_xattn_g_norm, L3_xattn_null_kv, L3_xattn_Wq, L3_xattn_Wkv, L3_xattn_Wout, L3_xattn_g_out)
    x = x + jnp.tanh(g_ffn[3]) * _L3_ffn_ref(_layernorm(x, axis=-1), L3_ffn_U1, L3_ffn_V1, L3_ffn_b1, L3_ffn_U2, L3_ffn_V2, L3_ffn_b2)
    return x

_drawn_inputs = setup_inputs


def setup_inputs(seed=0):
    import zlib

    import numpy as np

    out = dict(_drawn_inputs(seed))
    spreads = {'L0_ffn_gates': (0.0, 0.1),
     'L2_xattn_bq': (0.0, 0.679),
     'L2_xattn_bk': (0.0, 2.0),
     'L2_xattn_bv': (0.0, 0.1),
     'L2_xattn_bo': (0.0, 0.1),
     'L3_xattn_g_norm': (1.0, 0.6),
     'L3_xattn_g_out': (1.0, 0.2),
     'L3_ffn_b1': (0.0, 0.8),
     'L3_ffn_b2': (0.0, 0.523)}
    factors = {'g_ffn': 43.064,
     'L0_xattn_b_o': 4.935,
     'L1_xattn_bo': 8.0,
     'L1_ffn_bias': 8.0,
     'L2_ffn_gate_w': 8.0,
     'L2_ffn_gate_bias': 8.0,
     'L2_ffn_expert_gate': 8.0,
     'L2_ffn_expert_up': 8.0,
     'L2_ffn_expert_down': 8.0,
     'L2_ffn_shared_gate': 8.0,
     'L2_ffn_shared_up': 8.0,
     'L2_ffn_shared_down': 8.0,
     'L3_ffn_U1': 8.0,
     'L3_ffn_V1': 8.0,
     'L3_ffn_U2': 8.0,
     'L3_ffn_V2': 8.0,
     'L3_xattn_null_kv': 5.348}
    for name, (base, spread) in spreads.items():
        noise = np.random.default_rng([zlib.crc32(name.encode()), seed]).standard_normal(out[name].shape)
        drawn = base * np.exp(spread * noise) if base else spread * noise
        out[name] = jnp.asarray(drawn.astype(out[name].dtype))
    for name, factor in factors.items():
        out[name] = (out[name] * factor).astype(out[name].dtype)
    return out
```

```python
import concourse.bass as bass
from concourse import mybir
from contextlib import ExitStack
import numpy as np

FP = mybir.dt.float32
U8 = mybir.dt.uint8
ALU = mybir.AluOpType
ACT = mybir.ActivationFunctionType
AX = mybir.AxisListType

P = 128
S = 64
D = 128
DC = 96
TG = 4
GT = TG * P
HP = 8
DH = 64
NE0 = 16
QKV = 3 * DH
NE2, I2 = 32, 64
W2N = NE2 * I2 + P
NEG = -3.0e38
LN_EPS = 1e-5


def bc(ap, axis, n):
    shape = list(ap.shape)
    shape.insert(axis, n)
    return ap.unsqueeze(axis).broadcast_to(shape)


class Chip:

    def __init__(self, nc, ctx):
        self.nc, self.ctx, self.own, self.w = nc, ctx, [], {}

    def sbuf(self, name, shape, dt=FP):
        return self.ctx.enter_context(self.nc.sbuf_tensor(name, shape, dt))

    def sem(self, name):
        s = self.nc.alloc_semaphore(name=name)
        self.own.append(s)
        return s

    def carve(self):
        at = [0]

        def take(shape):
            n = int(np.prod(shape))
            t = self.work[:, at[0]:at[0] + n]
            at[0] += n
            assert at[0] <= self.work.shape[1], at
            names = "abcd"[:len(shape)]
            if len(shape) == 1:
                return t
            sizes = {m: k for m, k in zip(names[1:], shape[1:])}
            return t.rearrange(f"p ({' '.join(names)}) -> p {' '.join(names)}", **sizes)
        return take


def setup(c, d):
    nc = c.nc
    V, A, T, G = nc.vector, nc.scalar, nc.tensor, nc.gpsimd
    names = []

    def res(name, shape, dt=FP):
        t = c.sbuf(name, shape, dt)
        c.w[name] = t
        return t

    ntile = c.ntile
    res("x", [P, ntile, D])
    res("ident", [P, P])
    res("tg", [P, 8])
    early = res("early", [P, 8 * 4 * D + NE0 * QKV + NE0 * DH // P * D])
    at = [0]

    def place(name, shape, parts=P):
        n = int(np.prod(shape))
        t = early[0:parts, at[0]:at[0] + n]
        c.w[name] = t if len(shape) == 1 else t.rearrange("p (a b) -> p a b", b=shape[-1])
        at[0] += n

    for n in ("l0", "l1"):
        place(n + "_wq", [HP * DH]), place(n + "_wk", [HP * DH], DC), place(n + "_wv", [HP * DH], DC)
        place(n + "_wo", [4, D])
    place("l0f_w", [NE0 * QKV]), place("l0f_o", [NE0 * DH // P, D])
    at[0] = 0
    place("l2f_g", [W2N]), place("l2f_u", [W2N]), place("l2f_d", [W2N // P, D])
    res("l3_wq", [P, 2 * HP * DH])
    res("l3_wk", [DC, 2 * HP * DH])
    res("l3_wv", [DC, 2 * HP * DH])
    res("l3_wo", [P, 8, D])
    res("l2_wq", [P, D]), res("l2_wk", [DC, D]), res("l2_wv", [DC, D]), res("l2_wo", [P, D])
    for n in ("l2_wq", "l2_wk", "l2_wv", "l2_wo", "l3_wk", "l3_wv"):
        c.w[n] = c.w[n][:, :]
    res("l2_bcol", [P, 2])
    res("rows", [P, 7, D])
    res("hm", [P, 16])
    res("nullk", [P, DH])
    res("nvsel", [P, 8, 16])
    res("nvcol", [P, 1])
    res("gncol", [P, 1])
    res("l3_wnull", [P, 16])
    res("l3_nwo", [16, D])
    res("l1f_g", [P, D])
    res("l3f_w1", [P, 512])
    res("l3f_w2", [P, 4, D])
    res("l3f_b1", [P, 4])
    res("eps", [P, TG])
    res("half", [P, 16])
    res("l0f_sim", [P, NE0])
    res("l0f_sig", [P, NE0])
    res("causal", [P, P])
    res("iota16", [P, NE0])
    res("l2f_wr", [P, NE2])
    res("l2f_bias", [P, NE2])
    res("tri4", [P, 4, 4])
    scr = c.work[:, 0:9 * 512].rearrange("p (n w) -> p n w", w=512)
    dftc, dfts, wr, wi = (scr[:, i, 0:D] for i in range(4))
    a1, a2, cn, sn = (scr[:, 4 + i, 0:D] for i in range(4))
    nsc = scr[:, 8, 0:D]
    u1t = c.work[0:32, 9 * 512:9 * 512 + D]
    v1 = c.work[0:32, 10 * 512:11 * 512]
    u2t = c.work[0:32, 11 * 512:12 * 512]
    v2 = c.work[0:32, 12 * 512:12 * 512 + D]
    nkprod = c.work[:, 13 * 512:15 * 512]
    simsq = c.work[:, 15 * 512:15 * 512 + 16]
    simn2 = c.work[:, 15 * 512 + 16:15 * 512 + 32]
    ones = c.work[:, 15 * 512 + 128:15 * 512 + 256]

    loads_small, loads_x, loads_big = [], [], []
    loads_small += [(c.w["ident"][:, :], d["ident"]), (c.w["tg"][:, :], d["gates"]), (c.w["rows"][:, :, :], d["rows"]),
                    (c.w["hm"][:, :], d["hm"]), (c.w["nullk"][:, :], d["nullk"]), (c.w["nvsel"][:, :, :], d["nvsel"]),
                    (c.w["nvcol"][:, :], d["nvcol"]), (c.w["gncol"][:, :], d["gncol"]), (c.w["l2_bcol"][:, :], d["l2_bcol"]),
                    (c.w["l3f_b1"][:, :], d["l3f_b1"]),
                    (dftc, d["dftc"]), (dfts, d["dfts"]), (wr, d["wr"]), (wi, d["wi"]),
                    (u1t, d["u1t"]), (v1, d["v1"]), (u2t, d["u2t"]), (v2, d["v2"]),
                    (c.w["l0f_sim"][:, :], d["sim"]), (c.w["l0f_sig"][:, :], d["gates0"]),
                    (c.w["causal"][:, :], d["causal"]), (c.w["iota16"][:, :], d["iota16"]),
                    (c.w["l2f_wr"][:, :], d["l2f_wr"]), (c.w["l2f_bias"][:, :], d["l2f_bias"]), (c.w["tri4"][:, :, :], d["tri4"]),
                    (c.w["l3_wq"][:, :], d["l3_wq"]), (c.w["l3_wo"][:, :, :], d["l3_wo"])]
    for n in ("l0_wq", "l0_wk", "l0_wv"):
        loads_big.append((c.w[n], d[n]))
    loads_big.append((c.w["l0_wo"], d["l0_wo"]))
    loads_big += [(c.w["l0f_w"], d["l0f_w"]), (c.w["l0f_o"], d["l0f_o"])]
    for n in ("l1_wq", "l1_wk", "l1_wv", "l2_wq", "l2_wk", "l2_wv", "l2_wo", "l3_wk", "l3_wv"):
        loads_big.append((c.w[n], d[n]))
    loads_big += [(c.w["l1_wo"], d["l1_wo"])]

    ld_small, ld_x, ld_big = c.sem("ld_small"), c.sem("ld_x"), c.sem("ld_big")
    xv = d["x"].rearrange("(n p) c -> p n c", p=P)
    consts, chain, pe, evac, ppow, vchain = (c.sem("su_" + n) for n in ("consts", "act", "pe", "evac", "pow", "dve"))
    with nc.Block() as block:
        @block.sync
        def _(sp):
            for dst, src in loads_small:
                sp.dma_start(dst, src).then_inc(ld_small, 16)
            sp.wait_ge(ld_small, 16 * len(loads_small))
            sp.wait_ge(ld_x, 16)
            sp.wait_ge(ld_big, 16 * len(loads_big))

        @block.scalar
        def _(act):
            act.dma_start(c.w["x"][:, :, :], xv).then_inc(ld_x, 16)
            for dst, src in loads_big:
                act.dma_start(dst, src).then_inc(ld_big, 16)
            act.wait_ge(ld_small, 16 * len(loads_small))
            A.activation(c.w["tg"][:, :], c.w["tg"][:, :], ACT.Tanh).then_inc(chain, 1)
            A.activation(c.w["l0f_sig"][:, :], c.w["l0f_sig"][:, :], ACT.Exp, scale=-1.0).then_inc(chain, 1)

        @block.gpsimd
        def _(pool):
            G.memset(ones, 1.0).then_inc(consts, 1)
            G.memset(c.w["half"][:, :], -0.5).then_inc(consts, 1)
            G.memset(c.zero[:, :], 0.0)
            G.memset(c.w["eps"][:, :], LN_EPS)
            pool.wait_ge(consts, 2)
            pool.wait_ge(vchain, 2)
            G.tensor_tensor(simn2, simn2, c.w["half"][:, :], ALU.pow).then_inc(ppow, 1)

        @block.tensor
        def _(te):
            te.wait_ge(ld_small, 16 * len(loads_small))
            te.wait_ge(vchain, 1)
            te.wait_ge(consts, 1)
            pa, pb, pw, pn = c.ps[:, 0, :], c.ps[:, 1, :], c.ps[:, 2, :], c.ps[:, 3, :]
            T.matmul(c.ps[:, 6, 0:16], ones, simsq, start=True, stop=True).then_inc(pe, 1)
            te.wait_ge(evac, 1)
            T.matmul(pa[:, 0:D], wr, dftc, start=True, stop=False)
            T.matmul(pa[:, 0:D], wi, dfts, start=False, stop=True)
            T.matmul(pb[:, 0:D], wr, dfts, start=True, stop=False)
            T.matmul(pb[:, 0:D], wi, nsc, start=False, stop=True).then_inc(pe, 1)
            T.matmul(pw, u1t, v1, start=True, stop=True)
            for j in range(4):
                T.matmul(pn[:, j * D:(j + 1) * D], u2t[:, j * P:(j + 1) * P], v2, start=True, stop=True)
            te.wait_ge(evac, 2)
            for j in range(8):
                last = T.matmul(c.ps[0:16, 4, 0:D], c.w["nvsel"][:, j, :], c.w["l3_wo"][:, j, :], start=(j == 0), stop=(j == 7))
            last.then_inc(pe, 1)
            te.wait_ge(evac, 4)
            T.matmul(c.ps[:, 5, 0:D], a1, cn, start=True, stop=False)
            T.matmul(c.ps[:, 5, 0:D], a2, sn, start=False, stop=True).then_inc(pe, 1)

        @block.vector
        def _(ve):
            ve.wait_ge(ld_small, 16 * len(loads_small))
            V.tensor_tensor(simsq, c.w["l0f_sim"][:, :], c.w["l0f_sim"][:, :], ALU.mult).then_inc(vchain, 1)
            V.tensor_scalar(nsc, dftc, -1.0, None, ALU.mult).then_inc(evac, 1)
            V.tensor_scalar(c.w["nvsel"][:, :, :], c.w["nvsel"][:, :, :], c.w["nvcol"][:, 0:1], None, ALU.mult).then_inc(evac, 1)
            V.tensor_scalar(cn, dftc, 1.0 / D, None, ALU.mult).then_inc(evac, 1)
            V.tensor_scalar(sn, dfts, 1.0 / D, None, ALU.mult)
            ve.wait_ge(pe, 1)
            V.tensor_scalar(simn2, c.ps[:, 6, 0:16], 1e-24, None, ALU.max).then_inc(vchain, 1)
            V.tensor_scalar(c.w["l3_wq"][:, :], c.w["l3_wq"][:, :], c.w["gncol"][:, 0:1], None, ALU.mult).then_inc(vchain, 1)
            ve.wait_ge(vchain, 3)
            V.tensor_tensor(nkprod.rearrange("p (h d) -> p h d", d=DH), c.w["l3_wq"][:, :].rearrange("p (h d) -> p h d", d=DH),
                            bc(c.w["nullk"][:, :], 1, 16), ALU.mult).then_inc(vchain, 1)
            ve.wait_ge(vchain, 4)
            V.tensor_reduce(c.w["l3_wnull"][:, :], nkprod.rearrange("p (h d) -> p h d", d=DH), AX.X, ALU.add)
            ve.wait_ge(ppow, 1)
            V.tensor_tensor(c.w["l0f_sim"][:, :], c.w["l0f_sim"][:, :], simn2, ALU.mult)
            ve.wait_ge(chain, 2)
            V.tensor_scalar(c.w["l0f_sig"][:, :], c.w["l0f_sig"][:, :], 1.0, None, ALU.add).then_inc(vchain, 1)
            ve.wait_ge(vchain, 5)
            V.reciprocal(c.w["l0f_sig"][:, :], c.w["l0f_sig"][:, :])
            for row, gate in ((0, 0), (1, 1), (2, 5), (3, 2), (4, 7), (5, 3)):
                V.tensor_scalar(c.w["rows"][:, row, :], c.w["rows"][:, row, :], c.w["tg"][:, gate:gate + 1], None, ALU.mult)
            ve.wait_ge(pe, 2)
            V.tensor_copy(a1, c.ps[:, 0, 0:D])
            V.tensor_copy(a2, c.ps[:, 1, 0:D]).then_inc(evac, 1)
            ve.wait_ge(pe, 3)
            V.tensor_copy(c.w["l3f_w1"][:, :], c.ps[:, 2, :])
            V.tensor_copy(c.w["l3f_w2"][:, :, :].rearrange("p j c -> p (j c)"), c.ps[:, 3, :])
            V.tensor_copy(c.w["l3_nwo"][:, :], c.ps[0:16, 4, 0:D])
            ve.wait_ge(pe, 4)
            V.tensor_copy(c.w["l1f_g"][:, :], c.ps[:, 5, 0:D])


class Norm:

    def __init__(self, c, name, hn, bias_row=None, twice=False):
        self.c, self.hn, self.bias_row, self.twice = c, hn, bias_row, twice
        self.n = 2 if twice else 1
        self.stats = c.st
        self.moments, self.rstd_ready, self.eps_added, self.biased, self.ready, self.bn = (
            c.sem(f"{name}_{n}") for n in ("moments", "rstd", "eps", "biased", "hn", "bn"))
        self.mid = c.sem(f"{name}_mid") if twice else None

    def xg(self, g):
        return self.c.w["x"][:, bass.ds(g * TG, TG), :]

    def vector(self, ve, g):
        for r in range(self.n):
            self.take_moments(ve, g, r), self.scale(ve, g, r)

    def take_moments(self, ve, g, r=0):
        c, V = self.c, self.c.nc.vector
        e = g * self.n + r
        if r:
            ve.wait_ge(self.mid, g + 1)
        for t in range(TG):
            src = c.w["x"][:, bass.ds(g * TG + t, 1), :] if r == 0 else self.hn[:, t, :]
            last = V.bn_stats(c.st[:, t, :], src[:, 0, :] if r == 0 else src)
        last.then_inc(self.bn, 1)
        ve.wait_ge(self.bn, e + 1)
        V.memset(c.pause[:, 0:1], 0.0)
        for t in range(TG):
            last = V.bn_aggr(c.mv[:, t, :], c.st[:, t, :])
        last.then_inc(self.moments, 1)

    def scale(self, ve, g, r=0):
        c, V = self.c, self.c.nc.vector
        e = g * self.n + r
        ve.wait_ge(self.rstd_ready, e + 1)
        for t in range(TG):
            src = c.w["x"][:, bass.ds(g * TG + t, 1), :][:, 0, :] if r == 0 else self.hn[:, t, :]
            last = V.tensor_scalar(self.hn[:, t, :], src, c.mv[:, t, 0:1], c.rstd[:, t:t + 1],
                                   ALU.subtract, ALU.mult)
        last.then_inc(self.mid if self.twice and r == 0 else self.ready, 1)

    def pool(self, pool, g):
        c, G = self.c, self.c.nc.gpsimd
        for r in range(self.n):
            e = g * self.n + r
            pool.wait_ge(self.moments, e + 1)
            G.tensor_tensor(c.rstd[:, 0:TG], c.mv[:, :, 1], c.w["eps"][:, 0:TG], ALU.add).then_inc(self.eps_added, 1)
            pool.wait_ge(self.eps_added, e + 1)
            G.tensor_tensor(c.rstd[:, 0:TG], c.rstd[:, 0:TG], c.w["half"][:, 0:TG], ALU.pow).then_inc(self.rstd_ready, 1)
        if self.bias_row is not None:
            pool.wait_ge(self.ready, g + 1)
            G.tensor_tensor(self.xg(g), self.xg(g), bc(c.w["rows"][:, self.bias_row, :], 1, TG), ALU.add).then_inc(self.biased, 1)


class Unit:

    def __init__(self, it, u, passes):
        self.it, self.u, self.passes = it, u, passes
        self.k = it * 2 + u
        self.p = u if passes == 2 else 0
        self.g = it if passes == 2 else self.k

    def next(self):
        return Unit(self.it + 1, 0, self.passes) if self.u else Unit(self.it, 1, self.passes)


def attention(c, d, layer):
    nc = c.nc
    V, A, T, G = nc.vector, nc.scalar, nc.tensor, nc.gpsimd
    narrow = layer == 2
    null = layer == 3
    masked = layer in (0, 3)
    passes = 2 if layer >= 2 else 1
    units = c.ngroup * passes
    pre = f"a{layer}_"
    scale = 8 ** -0.5 if narrow else DH ** -0.5
    wq, wk, wv, wo = (c.w[f"l{layer}_w{n}"] for n in "qkvo")
    bias_row = {0: 0, 1: 1, 2: 3, 3: None}[layer]

    w = c.carve()
    hn, hT = w([TG, P]), w([GT])
    ctx = [w([GT]), w([GT])]
    qz = [w([HP, GT]), w([HP, GT])]
    kT = [w([1 if narrow else HP // 2, GT]) for _ in range(2)]
    vv = [w([TG, HP, P] if narrow else [TG, HP * DH]) for _ in range(2)]
    sc = w([HP, S])
    pr = [w([HP, S]), w([HP, S])]
    pbd = w([HP, P])
    ptT = w([HP, P])
    oT = w([1 if narrow else HP // 2, P])
    mx, den, rec = w([HP]), w([HP]), w([HP])
    if masked:
        mask = c.mask
        nm = [w([TG, S]), w([TG, S])]
    if narrow:
        qs = w([GT])
    if null:
        s0 = [w([TG, HP]), w([TG, HP])]
        e0, r0, r0T, y = [w([HP]), w([HP])], w([TG, 2 * HP]), w([GT]), w([TG, D])

    bank = {"A": c.ps[:, 0, :], "B": c.ps[:, 1, :]}
    ps_s = c.ps[:, 2:4, :].rearrange("p a (h k) -> p (a h) k", k=P)
    ps_t = c.ps[:, 4:6, :].rearrange("p a (h k) -> p (a h) k", k=P)
    ps_o = c.ps[:, 6, :].rearrange("p (j q) -> p j q", q=P)
    acc = c.ps[:, 7, :].rearrange("p (t c) -> p t c", c=D)

    norm = Norm(c, pre + "ln", hn, bias_row, twice=null)
    sem = lambda n: c.sem(pre + n)
    zeroed, mask_in = sem("zeroed"), sem("mask_in")
    ctx_in = [sem("ctx0"), sem("ctx1")]
    full = {"A": sem("fullA"), "B": sem("fullB")}
    done = {"A": sem("doneA"), "B": sem("doneB")}
    s_ready, s_out, max_ready, sub_ready, exp_ready = (sem(n) for n in ("s", "s_out", "max", "sub", "exp"))
    sum_ready, rec_ready, pbd_ready, pt_ready, pt_out = (sem(n) for n in ("sum", "rec", "pbd", "pt", "pt_out"))
    o_ready, o_out, acc_ready, added = (sem(n) for n in ("o", "o_out", "acc", "added"))
    nm_ready = sem("nm") if masked else None
    if narrow:
        qs_ready, qz_ready, clipped = sem("qs"), sem("qz"), sem("clip")
    if null:
        null_max, e0_ready, den_ready, r0_ready, fin_bn, fin_mv, fin_eps, fin_rstd, fin_y, fin_yg = (
            sem(n) for n in ("nmax", "e0", "den", "r0", "fbn", "fmv", "feps", "frstd", "fy", "fyg"))

    def steps_of(u):
        t = [("T", 0)] if u % passes == 0 else []
        if narrow:
            return [t + [("q", 0)], [("k", 0)], [("v", 0)], []]
        qk = [(kind, j) for j in range(4) for kind in "qk"]
        v = [("v", j) for j in range(TG)]
        return [t + qk[0:4], qk[4:8] + ([("z", 0)] if null else []), v[0:2], v[2:4]]

    def banked(steps):
        count, out = {"A": 0, "B": 0}, []
        for jobs in steps:
            row = []
            for kind, j in jobs:
                b = {"T": "A", "z": "B", "r": "A"}.get(kind) or (
                    {"q": "B", "k": "A"}.get(kind) or ("B" if narrow else "BA"[j % 2]))
                row.append((kind, j, b, count[b]))
                count[b] += 1
            out.append((row, dict(count)))
        return out, count

    r = [("r", 0)] if null else []
    table_first, base = banked([sum(steps_of(0), [])])
    s1, s2 = steps_of(1), steps_of(2)
    table, per = banked(s1 + s2[:3] + [r + s2[3]])
    table_last, _ = banked(s1 + [[], [], [], r])

    def before(b, i, it):
        return i if it is None else base[b] + it * per[b] + i

    def takes(kind, j):
        if kind == "z" or (narrow and kind in "qv"):
            return V
        if kind == "v" and not masked:
            return V
        return A

    def te_job(te, job, it, un):
        kind, j, b, i = job
        u, p, out = un.u, un.p, bank[job[2]]
        te.wait_ge(done[b], before(b, i, it))
        if kind == "T":
            te.wait_ge(norm.ready, un.g + 1)
            for t in range(TG):
                last = T.transpose(out[:, t * P:(t + 1) * P], hn[:, t, :], c.w["ident"][:, :])
        elif kind == "q":
            if j == 0 and un.p == 0:
                te.wait_ge(done["A"], before("A", i_T(it, un), it) + 1)
            col = j * P + (0 if narrow else p * HP * DH)
            last = T.matmul(out, wq[:, col:col + P], hT, start=True, stop=True)
        elif kind == "k":
            if j == 0:
                te.wait_ge(ctx_in[u], (un.it + 1) * 16)
            col = j * P + (0 if narrow else p * HP * DH)
            last = T.matmul(out, wk[:, col:col + P], ctx[u][0:DC, :], start=True, stop=True)
        elif kind == "z":
            for t in range(TG):
                last = T.matmul(out[:, t * HP:(t + 1) * HP], hT[:, t * P:(t + 1) * P],
                                c.w["l3_wnull"][:, p * HP:(p + 1) * HP], start=True, stop=True)
        elif kind == "v" and narrow:
            for t in range(TG):
                last = T.matmul(out[:, t * P:(t + 1) * P], ctx[u][0:DC, t * P:(t + 1) * P], wv, start=True, stop=True)
        elif kind == "v":
            last = T.matmul(out, ctx[u][0:DC, j * P:(j + 1) * P], wv[:, p * HP * DH:(p + 1) * HP * DH],
                            start=True, stop=True)
        elif kind == "r":
            te.wait_ge(r0_ready, un.g * 2 * TG + 2 * TG)
            for t in range(TG):
                last = T.transpose(out[0:2 * HP, t * P:(t + 1) * P], r0[:, t, :], c.w["ident"][:, :])
        last.then_inc(full[b], 1)

    def i_T(it, un):
        rows = table_first if it is None else table
        s = 0 if it is None else (TG if un.u == 0 else 0)
        return next(i for kind, _, _, i in rows[s][0] if kind == "T")

    def te_scores(te, n, un, t):
        te.wait_ge(s_out, n)
        for h in range(HP):
            k_h = kT[un.u][:, 0 if narrow else h // 2, t * P:(t + 1) * P]
            last = T.matmul(ps_s[:, h, :], qz[un.u][:, h, t * P:(t + 1) * P], k_h, start=True, stop=True)
        last.then_inc(s_ready, 1)

    def te_wait_unit(te, it, un, row):
        cnt = (table_first if it is None else table)[row][1]
        for b in "AB":
            te.wait_ge(done[b], before(b, cnt[b], it))
        if narrow:
            te.wait_ge(qz_ready, un.k + 1)

    def two_on(un, t):
        return (un, t + 2) if t < 2 else (un.next(), t - 2)

    def te_step(te, it, un, t, last_pair):
        rows = table_last if last_pair else table
        n = it * 8 + (4 * un.u + t)
        end = last_pair and un.u == 1
        te.wait_ge(pbd_ready, n + 1)
        te.wait_ge(pt_out, n * 2 + 1)
        for h in range(HP):
            tr = T.transpose(ps_t[:, h, :], pbd[:, h, :], c.w["ident"][:, :])
            if h % 4 == 3:
                tr.then_inc(pt_ready, 1)
        jobs = rows[4 * un.u + t][0]
        if jobs and jobs[0][0] in "Tr":
            te_job(te, jobs[0], it, un if jobs[0][0] == "r" else un.next())
            jobs = jobs[1:]
        if t < 2 or not end:
            if t == 2:
                te_wait_unit(te, it, un.next(), 4 * un.u + 1)
            te_scores(te, n + 2, *two_on(un, t))
        te.wait_ge(pt_out, n * 2 + 3)
        te.wait_ge(o_out, n + 1)
        for h in range(HP):
            if narrow:
                last = T.matmul(ps_o[:, 0, :], vv[un.u][:, t, h, :], ptT[:, h, :], start=(h == 0), stop=(h == HP - 1))
            else:
                half = slice(DH * (h % 2), DH * (h % 2) + DH)
                last = T.matmul(ps_o[half, h // 2, :], vv[un.u][:, t, h * DH:(h + 1) * DH], ptT[:, h, :],
                                start=True, stop=True)
        last.then_inc(o_ready, 1)
        for job in jobs:
            te_job(te, job, it, un.next())
        if t == TG - 1 and not end:
            cnt = rows[4 * un.u + t][1]
            te_v_wait = [(b, before(b, cnt[b], it)) for b in "AB"]
        te.wait_ge(o_out, n + 2)
        if t == 0 and un.p == 0:
            te.wait_ge(added, un.g + 1)
        chunks = 1 if narrow else HP // 2
        for j in range(chunks):
            wo_j = wo if narrow else wo[:, un.p * 4 + j, :]
            last = T.matmul(acc[:, t, :], oT[:, j, :], wo_j, start=(un.p == 0 and t == 0 and j == 0),
                            stop=(j == chunks - 1 and un.p == passes - 1), skip_group_check=True)
        if null and un.p == 1 and t == TG - 1:
            _, _, b, i = rows[4 * un.u + t][0][0]
            te.wait_ge(done[b], before(b, i, it) + 1)
            for tt in range(TG):
                last = T.matmul(acc[:, tt, :], r0T[0:2 * HP, tt * P:(tt + 1) * P], c.w["l3_nwo"][:, :],
                                start=False, stop=True, skip_group_check=True)
        last.then_inc(acc_ready, 1)
        if t == TG - 1 and not end:
            for b, v in te_v_wait:
                te.wait_ge(done[b], v)

    def take(eng, who, job, it, un):
        kind, j, b, i = job
        src, u, p = bank[b], un.u, un.p
        on_act = who is A
        copy = (lambda o, s: A.activation(o, s, ACT.Copy)) if on_act else (lambda o, s: V.tensor_copy(o, s))
        eng.wait_ge(full[b], before(b, i, it) + 1)
        if kind == "T":
            last = copy(hT, src)
        elif kind == "q" and narrow:
            last = V.tensor_scalar(qs, src, c.w["l2_bcol"][:, 0:1], None, ALU.add)
        elif kind == "q":
            copy(qz[u][0:DH, 2 * j, :], src[0:DH, :])
            last = copy(qz[u][DH:P, 2 * j + 1, :], src[DH:P, :])
        elif kind == "k" and narrow:
            last = A.activation(kT[u][:, 0, :], src, ACT.Identity, bias=c.w["l2_bcol"][:, 1:2])
        elif kind == "k":
            last = copy(kT[u][:, j, :], src)
        elif kind == "z":
            last = V.tensor_scalar(s0[u].rearrange("p t h -> p (t h)"), src[:, 0:TG * HP], scale, None, ALU.mult)
        elif kind == "v" and narrow:
            sv = src.rearrange("p (t f) -> p t f", f=P)
            for s in range(HP):
                col = (p * HP + s) * 8
                last = V.tensor_tensor(vv[u][:, :, s, col:col + 8], sv[:, :, col:col + 8],
                                       bc(c.w["rows"][:, 6, col:col + 8], 1, TG), ALU.add)
        elif kind == "v":
            last = copy(vv[u][:, j, :], src)
        elif kind == "r":
            last = copy(r0T[0:2 * HP, :], src[0:2 * HP, :])
        last.then_inc(done[b], 1)
        if kind == "q" and narrow:
            eng.wait_ge(done[b], before(b, i, it) + 1)
            for h in range(HP):
                last = V.tensor_scalar(qz[u][:, h, :], qs, c.w["hm"][:, p * HP + h:p * HP + h + 1], None, ALU.mult)
            last.then_inc(qz_ready, 1)

    def act_scores(act, n, un, t):
        if not masked:
            act.wait_ge(s_ready, n + 1)
            if not (isinstance(n, int) and n == 0):
                act.wait_ge(exp_ready, n)
            for b in range(2):
                half = slice(b * S, b * S + S)
                last = A.activation(sc[half, :, :], ps_s[half, :, half], ACT.Copy, scale=scale)
            last.then_inc(s_out, 1)

    def act_exp(act, n, t):
        act.wait_ge(sub_ready, n + 1)
        if null:
            A.activation(e0[t % 2], e0[t % 2], ACT.Exp)
        A.activation(pr[t % 2], sc, ACT.Exp).then_inc(exp_ready, 1)

    def ve_max(ve, n, un, t):
        if masked:
            if t == 0:
                ve.wait_ge(nm_ready, un.k + 1)
            ve.wait_ge(s_ready, n + 1)
            ve.wait_ge(exp_ready, n)
            for b in range(2):
                half = slice(b * S, b * S + S)
                last = V.scalar_tensor_tensor(out=sc[half, :, :], in0=ps_s[half, :, half], scalar=scale,
                                              in1=bc(nm[un.u][half, t, :], 1, HP), op0=ALU.mult, op1=ALU.add)
            last.then_inc(s_out, 1)
        ve.wait_ge(s_out, n + 1)
        if narrow:
            V.tensor_scalar(sc, sc, 1e4, -1e4, ALU.min, ALU.max).then_inc(clipped, 1)
            ve.wait_ge(clipped, n + 1)
        V.tensor_reduce(mx, sc, AX.X, ALU.max).then_inc(max_ready, 1)
        ve.wait_ge(max_ready, n + 1)
        if null:
            V.tensor_tensor(mx, mx, s0[un.u][:, t, :], ALU.max).then_inc(null_max, 1)
            ve.wait_ge(null_max, n + 1)
            V.tensor_tensor(e0[t % 2], s0[un.u][:, t, :], mx, ALU.subtract)
        V.tensor_tensor(sc, sc, bc(mx, 2, S), ALU.subtract).then_inc(sub_ready, 1)

    def ve_probs(ve, n, un, t, it=None):
        ve.wait_ge(exp_ready, n + 1)
        V.tensor_reduce(den, pr[t % 2], AX.X, ALU.add).then_inc(sum_ready, 1)
        ve.wait_ge(sum_ready, n + 1)
        if null:
            V.tensor_tensor(den, den, e0[t % 2], ALU.add).then_inc(den_ready, 1)
            ve.wait_ge(den_ready, n + 1)
        V.reciprocal(rec, den).then_inc(rec_ready, 1)
        ve.wait_ge(rec_ready, n + 1)
        ve.wait_ge(pt_ready, n * 2)
        for b in range(2):
            half = slice(b * S, b * S + S)
            last = V.tensor_tensor(pbd[half, :, half], pr[t % 2][half, :, :], bc(rec[half, :], 2, S), ALU.mult)
        last.then_inc(pbd_ready, 1)
        if null:
            if it is not None and t == 0 and un.p == 0:
                ve.wait_ge(full["A"], before("A", table[7][0][0][3], it) + 1)
            V.tensor_tensor(r0[:, t, un.p * HP:(un.p + 1) * HP], e0[t % 2], rec, ALU.mult).then_inc(r0_ready, 1)

    def ve_mask(ve, un):
        tiles = mask[:, bass.ds(un.g * TG, TG), :]
        V.tensor_scalar(nm[un.u], tiles, 1.0, -NEG, ALU.subtract, ALU.mult).then_inc(nm_ready, 1)

    def pairs(eng, body, n=units // 2):
        if n > 1:
            with eng.Fori(0, n - 1) as it:
                body(it, False)
        body(n - 1, True)

    with nc.Block() as block:
        @block.sync
        def _(sp):
            def load(un):
                sp.dma_start(ctx[un.u][0:DC, :], d["ctxT"][:, bass.ds(un.g * GT, GT)]).then_inc(ctx_in[un.u], 16)

            def vdone(it, row):
                kind, j, b, i = (table_first if it is None else table)[row][0][-1]
                sp.wait_ge(full[b], before(b, i, it) + 1)

            if layer == 0:
                sp.dma_start(mask[:, :, :], d["mask0"]).then_inc(mask_in, 16)
            elif layer == 3:
                sp.dma_start(mask[:, :, :], d["mask1"]).then_inc(mask_in, 16)
            if layer == 2:
                for dst, src in ((c.w["l2f_g"], d["l2f_g"]), (c.w["l2f_u"], d["l2f_u"]), (c.w["l2f_d"], d["l2f_d"])):
                    sp.dma_start(dst, src).then_inc(c.l2f_in, 16)
            load(Unit(0, 0, passes)), load(Unit(0, 1, passes))
            vdone(None, 0)
            load(Unit(1, 0, passes))

            def reload(it, u):
                vdone(it, 4 * u + (2 if narrow else 3))
                load(Unit(it, u, passes).next().next().next())

            if units > 4:
                with sp.Fori(0, (units - 4) // 2) as it:
                    reload(it, 0), reload(it, 1)
            reload((units - 4) // 2, 0)

        @block.gpsimd
        def _(pool):
            norm.pool(pool, 0)
            if passes == 1:
                norm.pool(pool, 1)

            def body(it, last_pair):
                for u in range(2):
                    if passes == 1 and not last_pair:
                        norm.pool(pool, it * 2 + u + 2)
                    if passes == 2 and u == 0 and not last_pair:
                        norm.pool(pool, it + 1)
                if null:
                    pool.wait_ge(fin_mv, it + 1)
                    G.tensor_tensor(c.rstd[:, TG:2 * TG], c.mv[:, :, 1], c.w["eps"][:, 0:TG], ALU.add).then_inc(fin_eps, 1)
                    pool.wait_ge(fin_eps, it + 1)
                    G.tensor_tensor(c.rstd[:, TG:2 * TG], c.rstd[:, TG:2 * TG], c.w["half"][:, 0:TG], ALU.pow)\
                        .then_inc(fin_rstd, 1)

            pairs(pool, body)

        @block.tensor
        def _(te):
            te.wait_ge(zeroed, 2)
            for job in table_first[0][0]:
                te_job(te, job, None, Unit(0, 0, passes))
            te_wait_unit(te, None, Unit(0, 0, passes), 0)
            te_scores(te, 0, Unit(0, 0, passes), 0)
            te_scores(te, 1, Unit(0, 0, passes), 1)

            def body(it, last_pair):
                for u in range(2):
                    for t in range(TG):
                        te_step(te, it, Unit(it, u, passes), t, last_pair)

            pairs(te, body)

        @block.scalar
        def _(act):
            act.sem_inc(pt_out, 1), act.sem_inc(o_out, 1), act.sem_inc(added, 1)
            A.activation(qz[0], bc(c.zero[:, 0:GT], 1, HP), ACT.Copy)
            A.activation(qz[1], bc(c.zero[:, 0:GT], 1, HP), ACT.Copy).then_inc(zeroed, 1)
            act.wait_ge(zeroed, 2)
            for job in table_first[0][0]:
                if takes(*job[:2]) is A:
                    take(act, A, job, None, Unit(0, 0, passes))
            for t in range(2):
                act_scores(act, t, Unit(0, 0, passes), t), act_exp(act, t, t)

            def body(it, last_pair):
                rows = table_last if last_pair else table
                for u in range(2):
                    for t in range(TG):
                        un, n = Unit(it, u, passes), it * 8 + (4 * u + t)
                        for a in range(2):
                            act.wait_ge(pt_ready, n * 2 + a + 1)
                            A.activation(ptT[:, 4 * a:4 * a + 4, :], ps_t[:, 4 * a:4 * a + 4, :], ACT.Copy).then_inc(pt_out, 1)
                        more = t < 2 or not (last_pair and u)
                        if more:
                            act_scores(act, n + 2, *two_on(un, t))
                        mine = [job for job in rows[4 * u + t][0] if takes(*job[:2]) is A]
                        if mine and mine[0][0] in "Tr":
                            take(act, A, mine[0], it, un if mine[0][0] == "r" else un.next())
                            mine = mine[1:]
                        act.wait_ge(o_ready, n + 1)
                        A.activation(oT, ps_o[:, 0:oT.shape[1], :], ACT.Copy).then_inc(o_out, 1)
                        for job in mine:
                            take(act, A, job, it, un.next())
                        if more:
                            act_exp(act, n + 2, t)

            pairs(act, body)

        @block.vector
        def _(ve):
            V.memset(pbd, 0.0)
            if narrow:
                V.memset(vv[0], 0.0)
                V.memset(vv[1], 0.0).then_inc(zeroed, 1)
            else:
                V.memset(mx, 0.0).then_inc(zeroed, 1)
            norm.vector(ve, 0)
            ve.wait_ge(zeroed, 2)
            if masked:
                ve.wait_ge(mask_in, 16)
                ve_mask(ve, Unit(0, 0, passes))
            for job in table_first[0][0]:
                if takes(*job[:2]) is V:
                    take(ve, V, job, None, Unit(0, 0, passes))
            if passes == 1:
                ve.wait_ge(full["A"], 1)
                norm.vector(ve, 1)
            ve_max(ve, 0, Unit(0, 0, passes), 0), ve_max(ve, 1, Unit(0, 0, passes), 1)
            ve_probs(ve, 0, Unit(0, 0, passes), 0)

            def body(it, last_pair):
                rows = table_last if last_pair else table
                for u in range(2):
                    for t in range(TG):
                        un, n = Unit(it, u, passes), it * 8 + (4 * u + t)
                        end = last_pair and u == 1
                        mine = [job for job in rows[4 * u + t][0] if takes(*job[:2]) is V]
                        if t < TG - 1:
                            ve_probs(ve, n + 1, un, t + 1, it)
                        elif not end:
                            ve_probs(ve, n + 1, un.next(), 0, it)
                        if t < 2 or not end:
                            if t == 2 and masked:
                                ve_mask(ve, un.next())
                            ve_max(ve, n + 2, *two_on(un, t))
                        for job in mine:
                            take(ve, V, job, it, un.next())
                        if not last_pair and (passes == 1 or u == 0):
                            g = it * 2 + u + 2 if passes == 1 else it + 1
                            if t == 1:
                                norm.take_moments(ve, g)
                            elif t == 2:
                                norm.scale(ve, g)
                                if null:
                                    norm.take_moments(ve, g, 1)
                            elif t == 3 and null:
                                norm.scale(ve, g, 1)
                        if t == TG - 1 and un.p == passes - 1:
                            ve_add(ve, un, n)

            def ve_add(ve, un, n):
                xg = norm.xg(un.g)
                ve.wait_ge(acc_ready, n + 1)
                if not null:
                    ve.wait_ge(norm.biased, un.g + 1)
                    V.scalar_tensor_tensor(out=xg, in0=acc, scalar=c.w["tg"][:, layer:layer + 1], in1=xg,
                                           op0=ALU.mult, op1=ALU.add).then_inc(added, 1)
                    return
                for t in range(TG):
                    last = V.bn_stats(c.st[:, t, :], acc[:, t, :])
                last.then_inc(fin_bn, 1)
                ve.wait_ge(fin_bn, un.g + 1)
                V.memset(c.pause[:, 0:1], 0.0)
                for t in range(TG):
                    last = V.bn_aggr(c.mv[:, t, :], c.st[:, t, :])
                last.then_inc(fin_mv, 1)
                ve.wait_ge(fin_rstd, un.g + 1)
                for t in range(TG):
                    last = V.tensor_scalar(y[:, t, :], acc[:, t, :], c.mv[:, t, 0:1], c.rstd[:, TG + t:TG + t + 1],
                                           ALU.subtract, ALU.mult)
                last.then_inc(fin_y, 1)
                ve.wait_ge(fin_y, un.g + 1)
                V.tensor_tensor(y, y, bc(c.w["rows"][:, 5, :], 1, TG), ALU.mult).then_inc(fin_yg, 1)
                ve.wait_ge(fin_yg, un.g + 1)
                V.tensor_tensor(xg, xg, y, ALU.add).then_inc(added, 1)

            pairs(ve, body)


def by_pairs(eng, n, body):
    if n > 2:
        with eng.Fori(0, n // 2 - 1) as it:
            body(it * 2, 0, False)
            body(it * 2 + 1, 1, False)
    body(n - 2, 0, True)
    body(n - 1, 1, True)


def dense(c, d, layer):
    nc = c.nc
    V, A, T, G = nc.vector, nc.scalar, nc.tensor, nc.gpsimd
    pre = f"f{layer}_"
    hidden = layer == 3
    n, gate = c.ngroup, 4 + layer
    w = c.carve()
    hn = w([TG, P])
    hT = [w([GT]), w([GT])]
    hid = [w([4, GT]), w([4, GT])] if hidden else None
    ps_t, acc = c.ps[:, 0, :], [c.ps[:, 1, :], c.ps[:, 2, :]]
    ps_h = [c.ps[:, 4 + j, :] for j in range(4)]
    norm = Norm(c, pre + "ln", hn, {1: 2, 3: 4}[layer])
    sem = lambda s: c.sem(pre + s)
    t_ready, t_out, h_ready, h_out, y_ready, added, stored = (
        sem(s) for s in ("t", "t_out", "h", "h_out", "y", "added", "stored"))

    with nc.Block() as block:
        if hidden:
            @block.sync
            def _(sp):
                out = d["out"].rearrange("(n p) c -> p n c", p=P)

                def send(g):
                    sp.wait_ge(added, g + 2)
                    sp.dma_start(out[:, bass.ds(g * TG, TG), :], norm.xg(g)).then_inc(stored, 16)
                with sp.Fori(0, n) as g:
                    send(g)
                sp.wait_ge(stored, 16 * n)

        @block.gpsimd
        def _(pool):
            with pool.Fori(0, n) as g:
                norm.pool(pool, g)

        @block.tensor
        def _(te):
            def transposes(g):
                te.wait_ge(norm.ready, g + 1)
                te.wait_ge(t_out, g)
                for t in range(TG):
                    last = T.transpose(ps_t[:, t * P:(t + 1) * P], hn[:, t, :], c.w["ident"][:, :])
                last.then_inc(t_ready, 1)

            def hidden_chunk(g, u, j):
                te.wait_ge(t_out, g + 1)
                te.wait_ge(h_out, g * 4 + j if j == 0 else g * 4 - 4 + j + 1) if not isinstance(g, int) or g else None
                T.matmul(ps_h[j], c.w["l3f_w1"][:, j * P:(j + 1) * P], hT[u], start=True, stop=True).then_inc(h_ready, 1)

            transposes(0), transposes(1)
            if hidden:
                for j in range(4):
                    hidden_chunk(0, 0, j)

            def body(g, u, last_pair):
                te.wait_ge(added, g + 1)
                for j in range(4 if hidden else 1):
                    if hidden and not (last_pair and u):
                        hidden_chunk(g + 1, 1 - u, j)
                    if hidden:
                        te.wait_ge(h_out, g * 4 + j + 1)
                    else:
                        te.wait_ge(t_out, g + 1)
                    for t in range(TG):
                        lhs = (hid[u][:, j, :] if hidden else hT[u])[:, t * P:(t + 1) * P]
                        last = T.matmul(acc[u][:, t * D:(t + 1) * D], lhs, c.w["l3f_w2"][:, j, :] if hidden else c.w["l1f_g"][:, :],
                                        start=(j == 0 and t == 0), stop=(j == (3 if hidden else 0)), skip_group_check=True)
                last.then_inc(y_ready, 1)
                if not last_pair:
                    transposes(g + 2)

            by_pairs(te, n, body)

        @block.scalar
        def _(act):
            def take_hT(g, u):
                act.wait_ge(t_ready, g + 1)
                A.activation(hT[u], ps_t, ACT.Copy).then_inc(t_out, 1)

            def gelu(g, u, j):
                act.wait_ge(h_ready, g * 4 + j + 1)
                A.activation(hid[u][:, j, :], ps_h[j], ACT.Gelu_apprx_tanh, bias=c.w["l3f_b1"][:, j:j + 1]).then_inc(h_out, 1)

            act.sem_inc(added, 1)
            take_hT(0, 0), take_hT(1, 1)
            if hidden:
                for j in range(4):
                    gelu(0, 0, j)

            def body(g, u, last_pair):
                if hidden and not (last_pair and u):
                    for j in range(4):
                        gelu(g + 1, 1 - u, j)
                if not last_pair:
                    take_hT(g + 2, u)

            by_pairs(act, n, body)

        @block.vector
        def _(ve):
            norm.vector(ve, 0)
            ve.wait_ge(t_ready, 1)
            norm.vector(ve, 1)

            def body(g, u, last_pair):
                if not last_pair:
                    ve.wait_ge(t_ready, g + 2)
                    norm.vector(ve, g + 2)
                ve.wait_ge(y_ready, g + 1)
                ve.wait_ge(norm.biased, g + 1)
                xg = norm.xg(g)
                V.scalar_tensor_tensor(out=xg, in0=acc[u].rearrange("p (t c) -> p t c", c=D),
                                       scalar=c.w["tg"][:, gate:gate + 1], in1=xg, op0=ALU.mult, op1=ALU.add).then_inc(added, 1)

            by_pairs(ve, n, body)


def experts(c, d):
    nc = c.nc
    V, A, T, G = nc.vector, nc.scalar, nc.tensor, nc.gpsimd
    n = c.ngroup
    WB = 512
    blocks = [(s, min(WB, W2N - s)) for s in range(0, W2N, WB)]
    NB = len(blocks)
    NS = TG * NB
    w = c.carve()
    hn = w([TG, P])
    hT = [w([GT]), w([GT])]
    sg, a = [w([WB]), w([WB])], [w([WB]), w([WB])]
    aT = [w([4, P]), w([4, P])]
    wts = [w([TG, NE2]), w([TG, NE2])]
    den, score, choice, rep, sel = (w([TG, NE2]) for _ in range(5))
    top, gt, eq = w([TG * 4, 8]), w([TG, 4, 4]), w([TG, 4, 4])
    gs, rank, t8, ws = w([TG, 4]), w([TG, 4]), w([TG, 8]), w([TG])
    ps_g, ps_u, ps_a = (tuple(c.ps[:, i + j, :] for j in range(2)) for i in (0, 2, 4))
    acc, ps_x = c.ps[:, 6, :], c.ps[:, 7, :]
    norm = Norm(c, "f2_ln", hn)
    sem = lambda s: c.sem("f2_" + s)
    x_ready, x_out, gu_ready, silu_ready, u_read, a_ready, at_ready, at_out, y_ready, added, link = (
        sem(s) for s in ("x", "x_out", "gu", "silu", "u_read", "a", "at", "at_out", "y", "added", "link"))
    LINKS = 16
    wts_ready, norm_link = sem("wts"), sem("norm_link")

    def ahead(g, u, s):
        return (g, u, s + 2) if s + 2 < NS else (g + 1, 1 - u, s + 2 - NS)

    with nc.Block() as block:
        @block.gpsimd
        def _(pool):
            with pool.Fori(0, n) as g:
                norm.pool(pool, g)

        @block.tensor
        def _(te):
            def transposes(g):
                te.wait_ge(norm.ready, g + 1)
                te.wait_ge(x_out, g * 2)
                for t in range(TG):
                    last = T.transpose(ps_x[:, t * P:(t + 1) * P], hn[:, t, :], c.w["ident"][:, :])
                last.then_inc(x_ready, 1)

            def router(g, u):
                te.wait_ge(x_out, g * 2 + 1)
                for t in range(TG):
                    last = T.matmul(ps_x[:, t * NE2:(t + 1) * NE2], hT[u][:, t * P:(t + 1) * P], c.w["l2f_wr"][:, :],
                                    start=True, stop=True)
                last.then_inc(x_ready, 1)

            def gate_up(g, u, s):
                t, (c0, width) = s // NB, blocks[s % NB]
                m = g * NS + s
                if not (isinstance(g, int) and g == 0 and s < 2):
                    te.wait_ge(u_read, m - 1)
                lhs = hT[u][:, t * P:(t + 1) * P]
                T.matmul(ps_g[s % 2][:, 0:width], lhs, c.w["l2f_g"][:, c0:c0 + width], start=True, stop=True)
                T.matmul(ps_u[s % 2][:, 0:width], lhs, c.w["l2f_u"][:, c0:c0 + width], start=True, stop=True).then_inc(gu_ready, 1)

            te.wait_ge(c.l2f_in, 48)
            transposes(0), router(0, 0)
            gate_up(0, 0, 0), gate_up(0, 0, 1)

            def body(g, u, last_pair):
                end = last_pair and u == 1
                for s in range(NS):
                    m, t, (c0, width) = g * NS + s, s // NB, blocks[s % NB]
                    te.wait_ge(a_ready, m + 1)
                    for j in range(width // P):
                        last = T.transpose(ps_a[s % 2][:, j * P:(j + 1) * P], a[s % 2][:, j * P:(j + 1) * P], c.w["ident"][:, :])
                    last.then_inc(at_ready, 1)
                    if not (end and s + 2 >= NS):
                        gate_up(*ahead(g, u, s))
                    if s == 1 and not end:
                        transposes(g + 1)
                    if s == 3 and not end:
                        router(g + 1, 1 - u)
                    te.wait_ge(at_out, m + 1)
                    if s == 0:
                        te.wait_ge(added, g + 1)
                    for j in range(width // P):
                        last = T.matmul(acc[:, t * D:(t + 1) * D], aT[s % 2][:, j, :], c.w["l2f_d"][:, c0 // P + j, :],
                                        start=(s % NB == 0 and j == 0), stop=(s % NB == NB - 1), skip_group_check=True)
                last.then_inc(y_ready, 1)

            by_pairs(te, n, body)

        @block.scalar
        def _(act):
            def take_hT(g, u):
                act.wait_ge(x_ready, g * 2 + 1)
                A.activation(hT[u], ps_x, ACT.Copy).then_inc(x_out, 1)

            def silu(g, s):
                width = blocks[s % NB][1]
                act.wait_ge(gu_ready, g * NS + s + 1)
                A.activation(sg[s % 2][:, 0:width], ps_g[s % 2][:, 0:width], ACT.Silu).then_inc(silu_ready, 1)

            def sigmoid_exp(g):
                act.wait_ge(x_ready, g * 2 + 2)
                A.activation(den.rearrange("p t e -> p (t e)"), ps_x[:, 0:TG * NE2], ACT.Exp, scale=-1.0).then_inc(x_out, 1)

            act.sem_inc(added, 1)
            take_hT(0, 0), sigmoid_exp(0), silu(0, 0), silu(0, 1)

            def body(g, u, last_pair):
                end = last_pair and u == 1
                for s in range(NS):
                    width = blocks[s % NB][1]
                    act.wait_ge(at_ready, g * NS + s + 1)
                    A.activation(aT[s % 2][:, 0:width // P, :].rearrange("p j q -> p (j q)"), ps_a[s % 2][:, 0:width],
                                 ACT.Copy).then_inc(at_out, 1)
                    if not (end and s + 2 >= NS):
                        g2, _, s2 = ahead(g, u, s)
                        silu(g2, s2)
                    if s == 1 and not end:
                        take_hT(g + 1, 1 - u)
                    if s == 3 and not end:
                        sigmoid_exp(g + 1)

            by_pairs(act, n, body)

        @block.vector
        def _(ve):
            def chained(g, i, ins):
                ins.then_inc(link, 1)
                ve.wait_ge(link, g * LINKS + i)

            def mults(g, u, s):
                width = blocks[s % NB][1]
                m = g * NS + s
                ve.wait_ge(silu_ready, m + 1)
                out = a[s % 2][:, 0:width]
                first = V.tensor_tensor(out, sg[s % 2][:, 0:width], ps_u[s % 2][:, 0:width], ALU.mult)
                first.then_inc(u_read, 1)
                ve.wait_ge(u_read, m + 1)
                e0 = blocks[s % NB][0] // I2
                if width == WB:
                    if s % NS == 0:
                        ve.wait_ge(wts_ready, g + 1)
                    o3 = out.rearrange("p (e i) -> p e i", i=I2)
                    V.tensor_tensor(o3, o3, bc(wts[u][:, s // NB, e0:e0 + WB // I2], 2, I2), ALU.mult).then_inc(a_ready, 1)
                else:
                    V.memset(c.pause[:, 1:2], 0.0).then_inc(a_ready, 1)

            def routing(g, u, part):
                ch = lambda i, ins: chained(g, i, ins)
                if part == 0:
                    ve.wait_ge(x_out, g * 2 + 2)
                    ch(1, V.tensor_scalar(den, den, 1.0, None, ALU.add))
                    V.reciprocal(score, den).then_inc(link, 1)
                elif part == 1:
                    ve.wait_ge(link, g * LINKS + 2)
                    V.tensor_tensor(choice, score, bc(c.w["l2f_bias"][:, :], 1, TG), ALU.add).then_inc(link, 1)
                elif part == 2:
                    ve.wait_ge(link, g * LINKS + 3)
                    V.memset(c.pause[:, 0:1], 0.0)
                    for i in range(TG * 4):
                        last = V.max(top[:, i, :], choice[:, i // 4, (i % 4) * 8:(i % 4) * 8 + 8])
                    ch(4, last)
                    t4 = top.rearrange("p (t q) k -> p t q k", t=TG)
                    V.tensor_tensor(gs, t4[:, :, :, 0], t4[:, :, :, 1], ALU.add).then_inc(link, 1)
                elif part == 3:
                    ve.wait_ge(link, g * LINKS + 5)
                    mine, other = bc(gs, 3, 4), bc(gs, 2, 4)
                    V.tensor_tensor(gt, other, mine, ALU.is_gt)
                    V.tensor_tensor(eq, other, mine, ALU.is_equal).then_inc(link, 1)
                elif part == 4:
                    ve.wait_ge(link, g * LINKS + 6)
                    ch(7, V.tensor_tensor(eq, eq, bc(c.w["tri4"][:, 0:4, :], 1, TG), ALU.mult))
                    V.tensor_tensor(gt, gt, eq, ALU.add).then_inc(link, 1)
                elif part == 5:
                    ve.wait_ge(link, g * LINKS + 8)
                    ch(9, V.tensor_reduce(rank, gt, AX.X, ALU.add))
                    V.tensor_scalar(rank, rank, 1.5, None, ALU.is_lt).then_inc(link, 1)
                elif part == 6:
                    ve.wait_ge(link, g * LINKS + 10)
                    c4 = choice.rearrange("p t (q k) -> p t q k", k=8)
                    ch(11, V.tensor_tensor(c4, c4, bc(rank, 3, 8), ALU.mult))
                    V.memset(c.pause[:, 0:1], 0.0)
                    for t in range(TG):
                        last = V.max(t8[:, t, :], choice[:, t, :])
                    last.then_inc(link, 1)
                elif part == 7:
                    ve.wait_ge(link, g * LINKS + 12)
                    V.memset(c.pause[:, 0:1], 0.0)
                    for t in range(TG):
                        last = V.match_replace(rep[:, t, :], t8[:, t, :], choice[:, t, :], -1e30)
                    last.then_inc(link, 1)
                elif part == 8:
                    ve.wait_ge(link, g * LINKS + 13)
                    V.tensor_tensor(sel, rep, choice, ALU.not_equal).then_inc(link, 1)
                elif part == 9:
                    ve.wait_ge(link, g * LINKS + 14)
                    ch(15, V.tensor_tensor(wts[u], sel, score, ALU.mult))
                    V.tensor_reduce(ws, wts[u], AX.X, ALU.add).then_inc(link, 1)
                elif part == 10:
                    ve.wait_ge(link, g * LINKS + 16)
                    V.tensor_scalar(ws, ws, 1e-20, None, ALU.add).then_inc(norm_link, 1)
                    ve.wait_ge(norm_link, g * 3 + 1)
                    V.reciprocal(ws, ws).then_inc(norm_link, 1)
                elif part == 11:
                    ve.wait_ge(norm_link, g * 3 + 2)
                    V.tensor_scalar(ws, ws, 2.5, None, ALU.mult).then_inc(norm_link, 1)
                elif part == 12:
                    ve.wait_ge(norm_link, g * 3 + 3)
                    V.tensor_tensor(wts[u], wts[u], bc(ws, 2, NE2), ALU.mult).then_inc(wts_ready, 1)

            norm.vector(ve, 0)
            for part in range(13):
                routing(0, 0, part)
            norm.vector(ve, 1)
            mults(0, 0, 0), mults(0, 0, 1)

            def body(g, u, last_pair):
                end = last_pair and u == 1
                for s in range(NS):
                    if not (end and s + 2 >= NS):
                        mults(*ahead(g, u, s))
                    if 5 <= s < 18 and not end:
                        routing(g + 1, 1 - u, s - 5)
                    if s == 4 and not last_pair:
                        ve.wait_ge(x_ready, g * 2 + 3)
                        norm.vector(ve, g + 2)
                ve.wait_ge(y_ready, g + 1)
                xg = norm.xg(g)
                V.scalar_tensor_tensor(out=xg, in0=acc.rearrange("p (t c) -> p t c", c=D), scalar=c.w["tg"][:, 6:7], in1=xg,
                                       op0=ALU.mult, op1=ALU.add).then_inc(added, 1)

            by_pairs(ve, n, body)


def gated_attention(c, d):
    nc = c.nc
    V, A, T, G = nc.vector, nc.scalar, nc.tensor, nc.gpsimd
    n = c.ngroup
    ZW, NZ = 2 * QKV, NE0 // 2
    w = c.carve()
    hn = w([TG, P])
    hT = [w([GT]), w([GT])]
    rw = [w([TG, NE0]), w([TG, NE0])]
    part_sum = [w([QKV]), w([QKV])]
    qvk0 = [w([4 * DH]), w([4 * DH])]
    qkT, sm, ex, pT = w([2 * P]), w([P]), w([P]), w([P])
    nmx, esum, rec, rwn = w([1]), w([1]), w([1]), w([NE0])
    mixed, mT = w([NE0, DH]), w([NE0 // 2, P])
    sq, n2, rn, rn_wait = w([P]), w([TG]), w([TG]), w([TG])
    lg, gated, active, l2, key, first, fb = (w([TG, NE0]) for _ in range(7))
    cnt, m1, m2, km = w([TG]), w([TG]), w([TG]), w([TG])
    ps_z = [c.ps[:, j, 0:ZW] for j in range(4)]
    ps_x, ps_y, ps_m, acc = (c.ps[:, 4 + j, :] for j in range(4))
    norm = Norm(c, "f0_ln", hn)
    sem = lambda s: c.sem("f0_" + s)
    z_ready, z_read, summed, qkv_ready = sem("z"), sem("z_read"), sem("sum"), sem("qkv")
    qkt_ready, qkt_out, s_ready, s_read, nmx_ready, exp_ready = (
        sem(s) for s in ("qkt", "qkt_out", "s", "s_read", "nmx", "exp"))
    pt_ready, pt_out, pv_ready, rec_ready, rwn_ready, mixed_ready = (
        sem(s) for s in ("pt", "pt_out", "pv", "rec", "rwn", "mixed"))
    m_ready, m_out, y_ready, added = (sem(s) for s in ("m", "m_out", "y", "added"))
    mt_ready, mt_out, r_ready, r_read, n2_ready, rn_ready, rw_ready, link = (
        sem(s) for s in ("mt", "mt_out", "r", "r_read", "n2", "rn", "rw", "link"))
    gexp = sem("gexp")
    LINKS = 18

    def nxt(g, u, t):
        return (g, u, t + 1) if t < TG - 1 else (g + 1, 1 - u, 0)

    with nc.Block() as block:
        @block.gpsimd
        def _(pool):
            def row_norms(g):
                pool.wait_ge(n2_ready, g * TG + TG)
                G.tensor_tensor(rn_wait, c.zero[:, 0:TG], c.zero[:, 0:TG], ALU.add)
                G.tensor_scalar(rn, n2, 1e-24, None, ALU.max).then_inc(rn_ready, 1)
                pool.wait_ge(rn_ready, g * 2 + 1)
                G.tensor_tensor(rn, rn, c.w["half"][:, 0:TG], ALU.pow).then_inc(rn_ready, 1)

            norm.pool(pool, 0), row_norms(0), norm.pool(pool, 1)
            if n > 2:
                with pool.Fori(0, n - 2) as g:
                    row_norms(g + 1), norm.pool(pool, g + 2)
            row_norms(n - 1)

        @block.tensor
        def _(te):
            def transposes(g):
                te.wait_ge(norm.ready, g + 1)
                for t in range(TG):
                    last = T.transpose(ps_m[:, t * P:(t + 1) * P], hn[:, t, :], c.w["ident"][:, :])
                last.then_inc(m_ready, 1)

            def router(g, u):
                te.wait_ge(m_out, g + 1)
                for t in range(TG):
                    last = T.matmul(ps_y[:, t * NE0:(t + 1) * NE0], hT[u][:, t * P:(t + 1) * P], c.w["l0f_sim"][:, :],
                                    start=True, stop=True)
                last.then_inc(r_ready, 1)

            def project(g, u, t, j):
                if not (isinstance(g, int) and g == 0 and t == 0 and j < 4):
                    te.wait_ge(z_read, (g * TG + t) * NE0 + 2 * j - 6)
                T.matmul(ps_z[j % 4], hT[u][:, t * P:(t + 1) * P], c.w["l0f_w"][:, j * ZW:(j + 1) * ZW],
                         start=True, stop=True).then_inc(z_ready, 1)

            transposes(0), router(0, 0)
            for j in range(NZ):
                project(0, 0, 0, j)

            def body(g, u, last_pair):
                for t in range(TG):
                    end = last_pair and u == 1 and t == TG - 1
                    m = g * TG + t
                    z = nxt(g, u, t)
                    te.wait_ge(qkv_ready, m + 1)
                    T.transpose(ps_x[:, 0:P], qvk0[t % 2][:, 0:P], c.w["ident"][:, :])
                    T.transpose(ps_x[:, P:2 * P], qvk0[t % 2][:, P:2 * P], c.w["ident"][:, :]).then_inc(qkt_ready, 1)
                    if not end:
                        project(*z, 0), project(*z, 1)
                    te.wait_ge(qkt_out, m + 1)
                    T.matmul(ps_x[:, 2 * P:3 * P], qkT[:, 0:P], qkT[:, P:2 * P], start=True, stop=True)\
                        .then_inc(s_ready, 1)
                    if not end:
                        project(*z, 2), project(*z, 3)
                    if t == 0 and not (last_pair and u == 1):
                        te.wait_ge(mt_out, m * 2 + 1)
                        transposes(g + 1)
                    te.wait_ge(exp_ready, m + 1)
                    T.transpose(ps_x[:, 3 * P:4 * P], ex, c.w["ident"][:, :]).then_inc(pt_ready, 1)
                    if not end:
                        project(*z, 4), project(*z, 5)
                    te.wait_ge(pt_out, m + 1)
                    if t in (0, 2):
                        te.wait_ge(r_read, g + 1 if t == 0 else (g + 1 if last_pair and u == 1 else g + 2))
                    T.matmul(ps_y[:, 0:DH], pT, qvk0[t % 2][:, DH:2 * DH], start=True, stop=True).then_inc(pv_ready, 1)
                    if not end:
                        project(*z, 6)
                    te.wait_ge(mixed_ready, m + 1)
                    if t == 0:
                        te.wait_ge(m_out, g + 1 if last_pair and u == 1 else g + 2)
                    te.wait_ge(mt_out, m * 2 + 1)
                    for q in range(2):
                        if q:
                            if not end:
                                project(*z, 7)
                            te.wait_ge(mt_out, m * 2 + 2)
                        for j in range(4):
                            e = (q * 4 + j) * 2
                            last = T.transpose(ps_m[:, j * P:(j + 1) * P], mixed[:, e:e + 2, :].rearrange("p e i -> p (e i)"),
                                               c.w["ident"][:, :])
                        last.then_inc(mt_ready, 1)
                    if t == 1 and not (last_pair and u == 1):
                        router(g + 1, 1 - u)
                    if t == 0:
                        te.wait_ge(added, g + 1)
                    for j in range(8):
                        if j % 4 == 0:
                            te.wait_ge(mt_out, m * 2 + j // 4 + 2)
                        last = T.matmul(acc[:, t * D:(t + 1) * D], mT[:, j, :], c.w["l0f_o"][:, j, :], start=(j == 0), stop=(j == 7))
                last.then_inc(y_ready, 1)

            by_pairs(te, n, body)

        @block.scalar
        def _(act):
            def take_hT(g, u):
                act.wait_ge(m_ready, g + 1)
                A.activation(hT[u], ps_m, ACT.Copy).then_inc(m_out, 1)
                for t in range(TG):
                    if t:
                        act.wait_ge(n2_ready, g * TG + t)
                    else:
                        act.wait_ge(norm.ready, g + 1)
                    A.activation(sq, hn[:, t, :], ACT.Square, accum_out=n2[:, t:t + 1]).then_inc(n2_ready, 1)

            def gate_exp(g):
                act.wait_ge(link, g * LINKS + 15)
                A.activation(gated, gated, ACT.Exp).then_inc(gexp, 1)

            act.sem_inc(mt_out, 1), act.sem_inc(mt_ready, 1), act.sem_inc(added, 1)
            take_hT(0, 0), gate_exp(0)

            def body(g, u, last_pair):
                for t in range(TG):
                    m = g * TG + t
                    act.wait_ge(qkt_ready, m + 1)
                    A.activation(qkT, ps_x[:, 0:2 * P], ACT.Copy).then_inc(qkt_out, 1)
                    if t == 0 and not (last_pair and u == 1):
                        take_hT(g + 1, 1 - u)
                    act.wait_ge(nmx_ready, m + 1)
                    A.activation(ex, sm, ACT.Exp, bias=nmx[:, 0:1], accum_out=esum[:, 0:1]).then_inc(exp_ready, 1)
                    act.wait_ge(pt_ready, m + 1)
                    A.activation(pT, ps_x[:, 3 * P:4 * P], ACT.Copy).then_inc(pt_out, 1)
                    for q in range(2):
                        act.wait_ge(mt_ready, m * 2 + q + 2)
                        A.activation(mT[:, 4 * q:4 * q + 4, :].rearrange("p j q -> p (j q)"), ps_m, ACT.Copy).then_inc(mt_out, 1)
                    if t == 2 and not (last_pair and u == 1):
                        gate_exp(g + 1)

            by_pairs(act, n, body)

        @block.vector
        def _(ve):
            def routing(g, u, part):
                at = g * LINKS

                def after(i):
                    ve.wait_ge(link, at + i)

                if part == 0:
                    ve.wait_ge(r_ready, g + 1)
                    ve.wait_ge(rn_ready, g * 2 + 2)
                    V.tensor_tensor(lg, ps_y[:, 0:TG * NE0].rearrange("p (t e) -> p t e", e=NE0), bc(rn, 2, NE0),
                                    ALU.mult).then_inc(r_read, 1)
                    ve.wait_ge(r_read, g + 1)
                    V.tensor_tensor(lg, lg, bc(c.w["l0f_sig"][:, :], 1, TG), ALU.subtract).then_inc(link, 1)
                elif part == 1:
                    after(1)
                    V.tensor_scalar(gated, lg, 0.0, None, ALU.max)
                    V.tensor_scalar(active, lg, 0.0, None, ALU.is_gt)
                    V.tensor_reduce(m1, lg, AX.X, ALU.max).then_inc(link, 1)
                elif part == 2:
                    after(2)
                    V.tensor_reduce(cnt, active, AX.X, ALU.add)
                    V.tensor_tensor(key, lg, bc(m1, 2, NE0), ALU.is_equal).then_inc(link, 1)
                    after(3)
                    V.tensor_tensor(key, key, bc(c.w["iota16"][:, :], 1, TG), ALU.mult).then_inc(link, 1)
                elif part == 3:
                    after(4)
                    V.tensor_reduce(km, key, AX.X, ALU.max).then_inc(link, 1)
                    after(5)
                    V.tensor_tensor(first, key, bc(km, 2, NE0), ALU.is_equal).then_inc(link, 1)
                elif part == 4:
                    after(6)
                    V.scalar_tensor_tensor(out=l2, in0=first, scalar=-1e30, in1=lg, op0=ALU.mult, op1=ALU.add).then_inc(link, 1)
                    after(7)
                    V.tensor_reduce(m2, l2, AX.X, ALU.max).then_inc(link, 1)
                elif part == 5:
                    after(8)
                    V.tensor_tensor(key, l2, bc(m2, 2, NE0), ALU.is_equal).then_inc(link, 1)
                    after(9)
                    V.tensor_tensor(key, key, bc(c.w["iota16"][:, :], 1, TG), ALU.mult).then_inc(link, 1)
                elif part == 6:
                    after(10)
                    V.tensor_reduce(km, key, AX.X, ALU.max).then_inc(link, 1)
                    after(11)
                    V.tensor_tensor(fb, key, bc(km, 2, NE0), ALU.is_equal).then_inc(link, 1)
                    V.tensor_scalar(cnt, cnt, 0.0, None, ALU.is_equal)
                elif part == 7:
                    after(12)
                    V.tensor_tensor(fb, fb, first, ALU.add).then_inc(link, 1)
                    V.tensor_reduce(m1, gated, AX.X, ALU.max)
                    after(13)
                    V.tensor_tensor(fb, fb, bc(cnt, 2, NE0), ALU.mult).then_inc(link, 1)
                elif part == 8:
                    after(14)
                    V.tensor_tensor(active, active, fb, ALU.add)
                    V.tensor_tensor(gated, gated, bc(m1, 2, NE0), ALU.subtract).then_inc(link, 1)
                elif part == 9:
                    ve.wait_ge(gexp, g + 1)
                    V.tensor_tensor(gated, gated, active, ALU.mult).then_inc(link, 1)
                    after(16)
                    V.tensor_reduce(cnt, gated, AX.X, ALU.add).then_inc(link, 1)
                elif part == 10:
                    after(17)
                    V.reciprocal(cnt, cnt).then_inc(link, 1)
                    after(18)
                    V.tensor_tensor(rw[u], gated, bc(cnt, 2, NE0), ALU.mult).then_inc(rw_ready, 1)

            def add_up(g, u, t, j):
                m = g * TG + t
                if j == 0 and t == 0:
                    ve.wait_ge(rw_ready, g + 1)
                ve.wait_ge(z_ready, m * NZ + j + 1)
                for e in range(2):
                    z, r = ps_z[j % 4][:, e * QKV:(e + 1) * QKV], rw[u][:, t, 2 * j + e:2 * j + e + 1]
                    if j == 0:
                        V.tensor_scalar(part_sum[e], z, r, None, ALU.mult).then_inc(z_read, 1)
                    else:
                        ve.wait_ge(z_read, m * NE0 + 2 * j + e - 1)
                        V.scalar_tensor_tensor(out=part_sum[e], in0=z, scalar=r, in1=part_sum[e],
                                               op0=ALU.mult, op1=ALU.add).then_inc(z_read, 1)
                if j == NZ - 1:
                    ve.wait_ge(z_read, m * NE0 + NE0)
                    V.tensor_tensor(qvk0[t % 2][:, 0:QKV], part_sum[0], part_sum[1], ALU.add).then_inc(qkv_ready, 1)

            V.memset(qvk0[0][:, QKV:], 0.0)
            V.memset(qvk0[1][:, QKV:], 0.0)
            norm.vector(ve, 0)
            for part in range(11):
                routing(0, 0, part)
            norm.vector(ve, 1)
            for j in range(NZ):
                add_up(0, 0, 0, j)

            def body(g, u, last_pair):
                more = not (last_pair and u == 1)
                for t in range(TG):
                    end = not more and t == TG - 1
                    m = g * TG + t
                    z = nxt(g, u, t)

                    def sums(*js):
                        if not end:
                            for j in js:
                                add_up(*z, j)
                    sums(0)
                    ve.wait_ge(s_ready, m + 1)
                    V.scalar_tensor_tensor(out=sm, in0=ps_x[:, 2 * P:3 * P], scalar=DH ** -0.5, in1=c.w["causal"][:, :],
                                           op0=ALU.mult, op1=ALU.add).then_inc(s_read, 1)
                    sums(1)
                    ve.wait_ge(s_read, m + 1)
                    V.tensor_reduce(nmx, sm, AX.X, ALU.max, negate=True).then_inc(nmx_ready, 1)
                    sums(2, 3)
                    if t == 2 and more:
                        for part in (0, 1, 2, 3, 4):
                            routing(g + 1, 1 - u, part)
                    ve.wait_ge(exp_ready, m + 1)
                    V.reciprocal(rec, esum).then_inc(rec_ready, 1)
                    sums(4)
                    ve.wait_ge(rec_ready, m + 1)
                    V.tensor_scalar(rwn, rw[u][:, t, :], rec[:, 0:1], None, ALU.mult).then_inc(rwn_ready, 1)
                    sums(5)
                    ve.wait_ge(pv_ready, m + 1)
                    ve.wait_ge(rwn_ready, m + 1)
                    ve.wait_ge(mt_ready, m * 2 + 1)
                    V.tensor_tensor(mixed, bc(ps_y[:, 0:DH], 1, NE0), bc(rwn, 2, DH), ALU.mult).then_inc(mixed_ready, 1)
                    if t == 2 and more:
                        for part in (5, 6, 7, 8):
                            routing(g + 1, 1 - u, part)
                    sums(6, 7)
                    if t == 2 and more:
                        for part in (9, 10):
                            routing(g + 1, 1 - u, part)
                    if t == 3 and not last_pair:
                        ve.wait_ge(n2_ready, g * TG + 2 * TG)
                        norm.vector(ve, g + 2)
                ve.wait_ge(y_ready, g + 1)
                xg = norm.xg(g)
                V.scalar_tensor_tensor(out=xg, in0=acc.rearrange("p (t c) -> p t c", c=D), scalar=c.w["tg"][:, 4:5], in1=xg,
                                       op0=ALU.mult, op1=ALU.add).then_inc(added, 1)

            by_pairs(ve, n, body)


def program(nc, d, layers=range(8)):
    ctx = ExitStack()
    with ctx:
        c = Chip(nc, ctx)
        c.ntile = d["x"].shape[0] // P
        c.ngroup = c.ntile // TG
        c.work = c.sbuf("work", [P, 26 * 1024])
        c.ps = ctx.enter_context(nc.psum_tensor("ps", [P, 8, 512], FP))
        c.st = c.sbuf("st", [P, TG, 6])
        c.mv = c.sbuf("mv", [P, TG, 2])
        c.rstd = c.sbuf("rstd", [P, 2 * TG])
        c.zero = c.sbuf("zero", [P, 512])
        c.mask = c.sbuf("mask", [P, c.ntile, S], U8)
        c.pause = c.sbuf("pause", [1, 2])
        c.l2f_in = c.sem("l2f_in")
        c.own = []
        setup(c, d)
        for layer in layers:
            if layer % 2 == 0:
                attention(c, d, layer // 2)
            elif layer == 1:
                gated_attention(c, d)
            elif layer in (3, 7):
                dense(c, d, layer // 2)
            elif layer == 5:
                experts(c, d)
            nc.clear_and_free_semaphores(c.own)
            c.own = []
            nc.all_engine_barrier()
        if 7 not in layers:
            store(c, d)


def store(c, d):
    out = c.sem("out")
    with c.nc.Block() as block:
        @block.sync
        def _(sp):
            sp.dma_start(d["out"].rearrange("(n p) c -> p n c", p=P), c.w["x"][:, :, :]).then_inc(out, 16)
            sp.wait_ge(out, 16)


def layouts(i):
    f = np.float32
    ca = np.ascontiguousarray
    a = {}
    nb = i["x"].shape[0]
    a["x"] = i["x"].reshape(nb * S, D)
    a["ctxT"] = ca(i["ctx_768"].reshape(nb * S, DC).T)
    for name, key in (("mask0", "mask_BxS2_bk0"), ("mask1", "mask_BxS2_bf1")):
        m = i[key].reshape(nb // 2, 2, 1, S).transpose(1, 2, 0, 3)
        a[name] = ca(np.broadcast_to(m, (2, S, nb // 2, S)).reshape(P, nb // 2, S))
    rep = lambda v: np.broadcast_to(np.asarray(v).reshape(1, -1), (P, np.asarray(v).size))
    chunks = lambda w: ca(w.reshape(-1, P, w.shape[-1]).transpose(1, 0, 2))
    a["gates"] = ca(rep(np.concatenate([i["g_xattn"], i["g_ffn"]])))
    a["rows"] = ca(np.stack([rep(i[k]) for k in ("L0_xattn_b_o", "L1_xattn_bo", "L1_ffn_bias", "L2_xattn_bo", "L3_ffn_b2",
                                                 "L3_xattn_g_out", "L2_xattn_bv")], 1))
    a["l0_wq"], a["l0_wk"], a["l0_wv"], a["l0_wo"] = i["L0_xattn_W_q"], i["L0_xattn_W_k"], i["L0_xattn_W_v"], chunks(i["L0_xattn_W_o"])
    a["l1_wq"], a["l1_wk"], a["l1_wv"], a["l1_wo"] = i["L1_xattn_Wq"], i["L1_xattn_Wk"], i["L1_xattn_Wv"], chunks(i["L1_xattn_Wo"])
    a["l2_wq"], a["l2_wk"], a["l2_wv"], a["l2_wo"] = (i["L2_xattn_W" + k] for k in "qkvo")
    a["l2_bcol"] = ca(np.stack([i["L2_xattn_bq"], i["L2_xattn_bk"]], 1))
    a["l3_wq"] = i["L3_xattn_Wq"]
    a["l3_wk"], a["l3_wv"] = ca(i["L3_xattn_Wkv"][:, :1024]), ca(i["L3_xattn_Wkv"][:, 1024:])
    a["l3_wo"] = chunks(i["L3_xattn_Wout"])
    a["gncol"] = i["L3_xattn_g_norm"].reshape(P, 1)
    a["nullk"] = ca(rep(i["L3_xattn_null_kv"][0]))
    a["nvcol"] = ca(np.concatenate([i["L3_xattn_null_kv"][1]] * 2).reshape(P, 1))
    p = np.arange(P)
    a["nvsel"] = (np.arange(16)[None, None, :] == (2 * np.arange(8)[None, :, None] + p[:, None, None] // DH)).astype(f)
    a["hm"] = (p[:, None] // 8 == np.arange(16)[None, :]).astype(f)
    a["ident"] = np.eye(P, dtype=f)
    a["causal"] = np.where((p[:, None] // S == p[None, :] // S) & (p[None, :] <= p[:, None]), 0, NEG).astype(f)
    a["iota16"] = np.broadcast_to(16.0 - np.arange(16, dtype=f), (P, 16)).copy()
    a["tri4"] = np.broadcast_to((np.arange(4)[None, :] < np.arange(4)[:, None]).astype(f), (P, 4, 4)).copy()
    ang = 2 * np.pi * ((p[:, None] * p[None, :]) % P) / P
    a["dftc"], a["dfts"] = np.cos(ang).astype(f), np.sin(ang).astype(f)
    a["wr"], a["wi"] = i["L1_ffn_w_freq_real"], i["L1_ffn_w_freq_imag"]
    a["l0f_w"] = ca(np.concatenate([i[f"L0_ffn_{k}_proj"] for k in "qvk"], 2).transpose(1, 0, 2).reshape(P, NE0 * QKV))
    a["l0f_o"] = chunks(i["L0_ffn_o_proj"].reshape(NE0 * DH, D))
    a["sim"] = i["L0_ffn_sim_matrix"]
    a["gates0"] = ca(rep(i["L0_ffn_gates"]))
    a["l2f_wr"] = ca(i["L2_ffn_gate_w"].T)
    a["l2f_bias"] = ca(rep(i["L2_ffn_gate_bias"]))
    for n, k in (("g", "gate"), ("u", "up")):
        a["l2f_" + n] = ca(np.concatenate([i[f"L2_ffn_expert_{k}"].reshape(NE2 * I2, D), i[f"L2_ffn_shared_{k}"]], 0).T)
    down = i["L2_ffn_expert_down"].transpose(0, 2, 1).reshape(NE2 * I2, D)
    a["l2f_d"] = chunks(np.concatenate([down, i["L2_ffn_shared_down"].T], 0))
    a["u1t"], a["v1"] = ca(i["L3_ffn_U1"].T), i["L3_ffn_V1"]
    a["u2t"], a["v2"] = ca(i["L3_ffn_U2"].T), i["L3_ffn_V2"]
    a["l3f_b1"] = ca(i["L3_ffn_b1"].reshape(4, P).T)
    return {k: ca(v) for k, v in a.items()}


def kernel(**inputs):
    import concourse.bacc as bacc
    from concourse.bass_utils import run_bass_kernel_spmd

    arrays = layouts({k: np.asarray(v) for k, v in inputs.items()})
    nc = bacc.Bacc("TRN2", target_bir_lowering=False, num_devices=1)
    d = {n: nc.dram_tensor("in_" + n, a.shape, mybir.dt.from_np(a.dtype), kind="ExternalInput").ap()
         for n, a in arrays.items()}
    d["out"] = nc.dram_tensor("out", arrays["x"].shape, FP, kind="ExternalOutput").ap()
    program(nc, d)
    r = run_bass_kernel_spmd(nc, [{"in_" + n: a for n, a in arrays.items()}], core_ids=[0])
    return r.results[0]["out"].reshape(inputs["x"].shape)
```

```python
import concourse.bass as bass
from concourse import mybir
from contextlib import ExitStack
import numpy as np

FP = mybir.dt.float32
FR = mybir.dt.float32r
U8 = mybir.dt.uint8
ALU = mybir.AluOpType
ACT = mybir.ActivationFunctionType
AX = mybir.AxisListType

P = 128
S = 64
D = 128
DC = 96
TG = 4
GT = TG * P
HP = 8
DH = 64
NE0 = 16
QKV = 3 * DH
NE2, I2 = 32, 64
W2N = NE2 * I2 + P
CLAMP = 1e4
NEG = -3.0e38
LN_EPS = 1e-5


def bc(ap, axis, n):
    shape = list(ap.shape)
    shape.insert(axis, n)
    return ap.unsqueeze(axis).broadcast_to(shape)


class Chip:

    def __init__(self, nc, ctx):
        self.nc, self.ctx, self.own, self.w = nc, ctx, [], {}

    def sbuf(self, name, shape, dt=FP):
        return self.ctx.enter_context(self.nc.sbuf_tensor(name, shape, dt))

    def sem(self, name):
        s = self.nc.alloc_semaphore(name=name)
        self.own.append(s)
        return s

    def open_work(self, n, parts=0):
        self.scope = ExitStack()
        self.opened += 1
        self.work = self.scope.enter_context(self.nc.sbuf_tensor(f"work{self.opened}", [P, n], FP))
        if parts:
            self.parts = self.scope.enter_context(self.nc.sbuf_tensor(f"parts{self.opened}", [P, parts], FR))

    def close_work(self):
        self.scope.close()

    def carve(self, area=None):
        at = [0]
        area = self.work if area is None else area

        def take(shape):
            n = int(np.prod(shape))
            t = area[:, at[0]:at[0] + n]
            at[0] += n
            assert at[0] <= area.shape[1], at
            names = "abcd"[:len(shape)]
            if len(shape) == 1:
                return t
            sizes = {m: k for m, k in zip(names[1:], shape[1:])}
            return t.rearrange(f"p ({' '.join(names)}) -> p {' '.join(names)}", **sizes)
        return take


def setup(c, d):
    nc = c.nc
    V, A, T, G = nc.vector, nc.scalar, nc.tensor, nc.gpsimd
    names = []

    def res(name, shape, dt=FP):
        t = c.sbuf(name, shape, dt)
        c.w[name] = t
        return t

    ntile = c.ntile
    res("x", [P, ntile, D])
    res("ident", [P, P])
    res("tg", [P, 8])
    early = res("early", [P, 8 * 4 * D + NE0 * QKV + NE0 * DH // P * D])
    at = [0]

    def place(name, shape, parts=P):
        n = int(np.prod(shape))
        t = early[0:parts, at[0]:at[0] + n]
        c.w[name] = t if len(shape) == 1 else t.rearrange("p (a b) -> p a b", b=shape[-1])
        at[0] += n

    for n in ("l0", "l1"):
        place(n + "_wq", [HP * DH]), place(n + "_wk", [HP * DH], DC), place(n + "_wv", [HP * DH], DC)
        place(n + "_wo", [4, D])
    place("l0f_w", [NE0 * QKV]), place("l0f_o", [NE0 * DH // P, D])
    at[0] = 0
    place("l2f_g", [W2N]), place("l2f_u", [W2N]), place("l2f_d", [W2N // P, D])
    res("l3_wq", [P, 2 * HP * DH])
    res("l3_wk", [DC, 2 * HP * DH])
    res("l3_wv", [DC, 2 * HP * DH])
    res("l3_wo", [P, 8, D])
    res("l2_wq", [P, D]), res("l2_wk", [DC, D]), res("l2_wv", [DC, D]), res("l2_wo", [P, D])
    for n in ("l2_wq", "l2_wk", "l2_wv", "l2_wo", "l3_wk", "l3_wv"):
        c.w[n] = c.w[n][:, :]
    res("l2_bcol", [P, 2])
    res("rows", [P, 7, D])
    res("hm", [P, 16])
    res("nullk", [P, DH])
    res("nvsel", [P, 8, 16])
    res("nvcol", [P, 1])
    res("gncol", [P, 1])
    res("l3_wnull", [P, 16])
    res("l3_nwo", [16, D])
    res("l1f_g", [P, D])
    res("l3f_w1", [P, 512])
    res("l3f_w2", [P, 4, D])
    res("l3f_b1", [P, 4])
    res("eps", [P, TG])
    res("half", [P, 16])
    res("l0f_sim", [P, NE0])
    res("l0f_sig", [P, NE0])
    res("causal", [P, P])
    res("iota16", [P, NE0])
    res("l2f_wr", [P, NE2])
    res("l2f_bias", [P, NE2])
    res("tri4", [P, 4, 4])
    c.open_work(26 * 1024)
    scr = c.work[:, 0:9 * 512].rearrange("p (n w) -> p n w", w=512)
    dftc, dfts, wr, wi = (scr[:, i, 0:D] for i in range(4))
    a1, a2, cn, sn = (scr[:, 4 + i, 0:D] for i in range(4))
    nsc = scr[:, 8, 0:D]
    u1t = c.work[0:32, 9 * 512:9 * 512 + D]
    v1 = c.work[0:32, 10 * 512:11 * 512]
    u2t = c.work[0:32, 11 * 512:12 * 512]
    v2 = c.work[0:32, 12 * 512:12 * 512 + D]
    nkprod = c.work[:, 13 * 512:15 * 512]
    simsq = c.work[:, 15 * 512:15 * 512 + 16]
    simn2 = c.work[:, 15 * 512 + 16:15 * 512 + 32]
    ones = c.work[:, 15 * 512 + 128:15 * 512 + 256]

    loads_small, loads_x, loads_big = [], [], []
    loads_small += [(c.w["ident"][:, :], d["ident"]), (c.w["tg"][:, :], d["gates"]), (c.w["rows"][:, :, :], d["rows"]),
                    (c.w["hm"][:, :], d["hm"]), (c.w["nullk"][:, :], d["nullk"]), (c.w["nvsel"][:, :, :], d["nvsel"]),
                    (c.w["nvcol"][:, :], d["nvcol"]), (c.w["gncol"][:, :], d["gncol"]), (c.w["l2_bcol"][:, :], d["l2_bcol"]),
                    (c.w["l3f_b1"][:, :], d["l3f_b1"]),
                    (dftc, d["dftc"]), (dfts, d["dfts"]), (wr, d["wr"]), (wi, d["wi"]),
                    (u1t, d["u1t"]), (v1, d["v1"]), (u2t, d["u2t"]), (v2, d["v2"]),
                    (c.w["l0f_sim"][:, :], d["sim"]), (c.w["l0f_sig"][:, :], d["gates0"]),
                    (c.w["causal"][:, :], d["causal"]), (c.w["iota16"][:, :], d["iota16"]),
                    (c.w["l2f_wr"][:, :], d["l2f_wr"]), (c.w["l2f_bias"][:, :], d["l2f_bias"]), (c.w["tri4"][:, :, :], d["tri4"]),
                    (c.w["l3_wq"][:, :], d["l3_wq"]), (c.w["l3_wo"][:, :, :], d["l3_wo"])]
    for n in ("l0_wq", "l0_wk", "l0_wv"):
        loads_big.append((c.w[n], d[n]))
    loads_big.append((c.w["l0_wo"], d["l0_wo"]))
    loads_big += [(c.w["l0f_w"], d["l0f_w"]), (c.w["l0f_o"], d["l0f_o"])]
    for n in ("l1_wq", "l1_wk", "l1_wv", "l2_wq", "l2_wk", "l2_wv", "l2_wo", "l3_wk", "l3_wv"):
        loads_big.append((c.w[n], d[n]))
    loads_big += [(c.w["l1_wo"], d["l1_wo"])]

    ld_small, ld_x, ld_big = c.sem("ld_small"), c.sem("ld_x"), c.sem("ld_big")
    xv = d["x"].rearrange("(n p) c -> p n c", p=P)
    consts, chain, pe, evac, ppow, vchain = (c.sem("su_" + n) for n in ("consts", "act", "pe", "evac", "pow", "dve"))
    with nc.Block() as block:
        @block.sync
        def _(sp):
            for dst, src in loads_small:
                sp.dma_start(dst, src).then_inc(ld_small, 16)
            sp.wait_ge(ld_small, 16 * len(loads_small))
            sp.wait_ge(ld_x, 16)
            sp.wait_ge(ld_big, 16 * len(loads_big))

        @block.scalar
        def _(act):
            act.dma_start(c.w["x"][:, :, :], xv).then_inc(ld_x, 16)
            for dst, src in loads_big:
                act.dma_start(dst, src).then_inc(ld_big, 16)
            act.wait_ge(ld_small, 16 * len(loads_small))
            A.activation(c.w["tg"][:, :], c.w["tg"][:, :], ACT.Tanh).then_inc(chain, 1)
            A.activation(c.w["l0f_sig"][:, :], c.w["l0f_sig"][:, :], ACT.Exp, scale=-1.0).then_inc(chain, 1)

        @block.gpsimd
        def _(pool):
            G.memset(ones, 1.0).then_inc(consts, 1)
            G.memset(c.w["half"][:, :], -0.5).then_inc(consts, 1)
            G.memset(c.zero[:, :], 0.0)
            G.memset(c.w["eps"][:, :], LN_EPS)
            pool.wait_ge(consts, 2)
            pool.wait_ge(vchain, 2)
            G.tensor_tensor(simn2, simn2, c.w["half"][:, :], ALU.pow).then_inc(ppow, 1)

        @block.tensor
        def _(te):
            te.wait_ge(ld_small, 16 * len(loads_small))
            te.wait_ge(vchain, 1)
            te.wait_ge(consts, 1)
            pa, pb, pw, pn = c.ps[:, 0, :], c.ps[:, 1, :], c.ps[:, 2, :], c.ps[:, 3, :]
            T.matmul(c.ps[:, 6, 0:16], ones, simsq, start=True, stop=True).then_inc(pe, 1)
            te.wait_ge(evac, 1)
            T.matmul(pa[:, 0:D], wr, dftc, start=True, stop=False)
            T.matmul(pa[:, 0:D], wi, dfts, start=False, stop=True)
            T.matmul(pb[:, 0:D], wr, dfts, start=True, stop=False)
            T.matmul(pb[:, 0:D], wi, nsc, start=False, stop=True).then_inc(pe, 1)
            T.matmul(pw, u1t, v1, start=True, stop=True)
            for j in range(4):
                T.matmul(pn[:, j * D:(j + 1) * D], u2t[:, j * P:(j + 1) * P], v2, start=True, stop=True)
            te.wait_ge(evac, 2)
            for j in range(8):
                last = T.matmul(c.ps[0:16, 4, 0:D], c.w["nvsel"][:, j, :], c.w["l3_wo"][:, j, :], start=(j == 0), stop=(j == 7))
            last.then_inc(pe, 1)
            te.wait_ge(evac, 4)
            T.matmul(c.ps[:, 5, 0:D], a1, cn, start=True, stop=False)
            T.matmul(c.ps[:, 5, 0:D], a2, sn, start=False, stop=True).then_inc(pe, 1)

        @block.vector
        def _(ve):
            ve.wait_ge(ld_small, 16 * len(loads_small))
            V.tensor_tensor(simsq, c.w["l0f_sim"][:, :], c.w["l0f_sim"][:, :], ALU.mult).then_inc(vchain, 1)
            V.tensor_scalar(nsc, dftc, -1.0, None, ALU.mult).then_inc(evac, 1)
            V.tensor_scalar(c.w["nvsel"][:, :, :], c.w["nvsel"][:, :, :], c.w["nvcol"][:, 0:1], None, ALU.mult).then_inc(evac, 1)
            V.tensor_scalar(cn, dftc, 1.0 / D, None, ALU.mult).then_inc(evac, 1)
            V.tensor_scalar(sn, dfts, 1.0 / D, None, ALU.mult)
            ve.wait_ge(pe, 1)
            V.tensor_scalar(simn2, c.ps[:, 6, 0:16], 1e-24, None, ALU.max).then_inc(vchain, 1)
            V.tensor_scalar(c.w["l3_wq"][:, :], c.w["l3_wq"][:, :], c.w["gncol"][:, 0:1], None, ALU.mult).then_inc(vchain, 1)
            ve.wait_ge(vchain, 3)
            V.tensor_tensor(nkprod.rearrange("p (h d) -> p h d", d=DH), c.w["l3_wq"][:, :].rearrange("p (h d) -> p h d", d=DH),
                            bc(c.w["nullk"][:, :], 1, 16), ALU.mult).then_inc(vchain, 1)
            ve.wait_ge(vchain, 4)
            V.tensor_reduce(c.w["l3_wnull"][:, :], nkprod.rearrange("p (h d) -> p h d", d=DH), AX.X, ALU.add)
            ve.wait_ge(ppow, 1)
            V.tensor_tensor(c.w["l0f_sim"][:, :], c.w["l0f_sim"][:, :], simn2, ALU.mult)
            ve.wait_ge(chain, 2)
            V.tensor_scalar(c.w["l0f_sig"][:, :], c.w["l0f_sig"][:, :], 1.0, None, ALU.add).then_inc(vchain, 1)
            ve.wait_ge(vchain, 5)
            V.reciprocal(c.w["l0f_sig"][:, :], c.w["l0f_sig"][:, :])
            for row, gate in ((0, 0), (1, 1), (2, 5), (3, 2), (4, 7), (5, 3)):
                V.tensor_scalar(c.w["rows"][:, row, :], c.w["rows"][:, row, :], c.w["tg"][:, gate:gate + 1], None, ALU.mult)
            ve.wait_ge(pe, 2)
            V.tensor_copy(a1, c.ps[:, 0, 0:D])
            V.tensor_copy(a2, c.ps[:, 1, 0:D]).then_inc(evac, 1)
            ve.wait_ge(pe, 3)
            V.tensor_copy(c.w["l3f_w1"][:, :], c.ps[:, 2, :])
            V.tensor_copy(c.w["l3f_w2"][:, :, :].rearrange("p j c -> p (j c)"), c.ps[:, 3, :])
            V.tensor_copy(c.w["l3_nwo"][:, :], c.ps[0:16, 4, 0:D])
            ve.wait_ge(pe, 4)
            V.tensor_copy(c.w["l1f_g"][:, :], c.ps[:, 5, 0:D])


class Norm:

    def __init__(self, c, name, hn, bias_row=None, twice=False):
        self.c, self.hn, self.bias_row, self.twice = c, hn, bias_row, twice
        self.n = 2 if twice else 1
        self.stats = c.st
        self.moments, self.rstd_ready, self.eps_added, self.biased, self.ready, self.bn = (
            c.sem(f"{name}_{n}") for n in ("moments", "rstd", "eps", "biased", "hn", "bn"))
        self.mid = c.sem(f"{name}_mid") if twice else None

    def xg(self, g):
        return self.c.w["x"][:, bass.ds(g * TG, TG), :]

    def vector(self, ve, g):
        for r in range(self.n):
            self.take_moments(ve, g, r), self.scale(ve, g, r)

    def take_moments(self, ve, g, r=0):
        c, V = self.c, self.c.nc.vector
        e = g * self.n + r
        if r:
            ve.wait_ge(self.mid, g + 1)
        for t in range(TG):
            src = c.w["x"][:, bass.ds(g * TG + t, 1), :] if r == 0 else self.hn[:, t, :]
            last = V.bn_stats(c.st[:, t, :], src[:, 0, :] if r == 0 else src)
        last.then_inc(self.bn, 1)
        ve.wait_ge(self.bn, e + 1)
        V.memset(c.pause[:, 0:1], 0.0)
        for t in range(TG):
            last = V.bn_aggr(c.mv[:, t, :], c.st[:, t, :])
        last.then_inc(self.moments, 1)

    def scale(self, ve, g, r=0):
        c, V = self.c, self.c.nc.vector
        e = g * self.n + r
        ve.wait_ge(self.rstd_ready, e + 1)
        for t in range(TG):
            src = c.w["x"][:, bass.ds(g * TG + t, 1), :][:, 0, :] if r == 0 else self.hn[:, t, :]
            last = V.tensor_scalar(self.hn[:, t, :], src, c.mv[:, t, 0:1], c.rstd[:, t:t + 1],
                                   ALU.subtract, ALU.mult)
        last.then_inc(self.mid if self.twice and r == 0 else self.ready, 1)

    def pool(self, pool, g):
        c, G = self.c, self.c.nc.gpsimd
        for r in range(self.n):
            e = g * self.n + r
            pool.wait_ge(self.moments, e + 1)
            G.tensor_tensor(c.rstd[:, 0:TG], c.mv[:, :, 1], c.w["eps"][:, 0:TG], ALU.add).then_inc(self.eps_added, 1)
            pool.wait_ge(self.eps_added, e + 1)
            G.tensor_tensor(c.rstd[:, 0:TG], c.rstd[:, 0:TG], c.w["half"][:, 0:TG], ALU.pow).then_inc(self.rstd_ready, 1)
        if self.bias_row is not None:
            pool.wait_ge(self.ready, g + 1)
            G.tensor_tensor(self.xg(g), self.xg(g), bc(c.w["rows"][:, self.bias_row, :], 1, TG), ALU.add).then_inc(self.biased, 1)


def split_high(c, high, x):
    return c.nc.vector.tensor_copy(high, x)


def split_low(c, low, x, high):
    return c.nc.vector.tensor_tensor(low, x, high.bitcast(FP), ALU.subtract)


def product3(c, out, lhs, rhs):
    (lh, ll), (rh, rl) = lhs, rhs
    T = c.nc.tensor
    T.matmul(out, lh, rh, start=True, stop=False)
    T.matmul(out, lh, rl, start=False, stop=False)
    return T.matmul(out, ll, rh, start=False, stop=True)


class Unit:

    def __init__(self, it, u, passes):
        self.it, self.u, self.passes = it, u, passes
        self.k = it * 2 + u
        self.p = u if passes == 2 else 0
        self.g = it if passes == 2 else self.k

    def next(self):
        return Unit(self.it + 1, 0, self.passes) if self.u else Unit(self.it, 1, self.passes)


def attention(c, d, layer):
    nc = c.nc
    V, A, T, G = nc.vector, nc.scalar, nc.tensor, nc.gpsimd
    narrow = layer == 2
    null = layer == 3
    masked = layer in (0, 3)
    passes = 2 if layer >= 2 else 1
    units = c.ngroup * passes
    pre = f"a{layer}_"
    scale = 8 ** -0.5 if narrow else DH ** -0.5
    wq, wk, wv, wo = (c.w[f"l{layer}_w{n}"] for n in "qkvo")
    bias_row = {0: 0, 1: 1, 2: 3, 3: None}[layer]

    w = c.carve()
    hn, hT = w([TG, P]), w([GT])
    ctx = [w([GT // S, 2, S] if narrow else [GT]) for _ in range(2)]
    loads = 2 if narrow else 1
    qT = [w([1 if narrow else HP // 2, GT]) for _ in range(2)]
    kz = [w([HP, GT] if narrow else [HP // 2, GT // S, 2, S]) for _ in range(2)]
    sc = w([HP, S])
    pr = [w([HP, S]), w([HP, S])]
    mx, den = w([HP]), w([HP])
    rec = [w([HP]), w([HP])]
    if narrow:
        kT = w([GT])
        vz = [w([GT // S, HP // 2, 16]) for _ in range(2)]
        ptT = w([HP // 2, P])
        o, oT = w([TG, D]), w([1, P])
    else:
        vv = [w([TG, HP * DH]) for _ in range(2)]
        pbd = w([HP, P])
        ptT = w([HP, P])
        oT = w([HP // 2, P])
    if masked:
        mask = c.mask
        nm = [w([TG, S]), w([TG, S])]
    if null:
        s0 = [w([TG, HP]), w([TG, HP])]
        e0, r0, r0T, y = [w([HP]), w([HP])], w([TG, 2 * HP]), w([GT]), w([TG, D])

    bank = {"A": c.ps[:, 0, :], "B": c.ps[:, 1, :]}
    ps_s = c.ps[:, 2, :].rearrange("p (h k) -> p h k", k=S)
    ps_t = c.ps[:, 4:6, :].rearrange("p a (h k) -> p (a h) k", k=P)
    parts = 1 if narrow else 2
    ps_o = c.ps[:, 6, :].rearrange("p (j q) -> p j q", q=P)
    acc = c.ps[:, 7, :].rearrange("p (t c) -> p t c", c=D)

    norm = Norm(c, pre + "ln", hn, bias_row, twice=null)
    sem = lambda n: c.sem(pre + n)
    zeroed, mask_in = sem("zeroed"), sem("mask_in")
    ctx_in = [sem("ctx0"), sem("ctx1")]
    full = {"A": sem("fullA"), "B": sem("fullB")}
    done = {"A": sem("doneA"), "B": sem("doneB")}
    s_ready, s_out, max_ready, sub_ready, exp_ready = (sem(n) for n in ("s", "s_out", "max", "sub", "exp"))
    sum_ready, rec_ready, pbd_ready, pt_ready, pt_out = (sem(n) for n in ("sum", "rec", "pbd", "pt", "pt_out"))
    o_ready, o_out, acc_ready, added = (sem(n) for n in ("o", "o_out", "acc", "added"))
    nm_ready = sem("nm") if masked else None
    if narrow:
        kz_ready, q_copied, ot_ready, ot_out = sem("kz"), sem("q_copied"), sem("ot"), sem("ot_out")
    if null:
        null_max, e0_ready, den_ready, r0_ready, fin_bn, fin_mv, fin_eps, fin_rstd, fin_y, fin_yg = (
            sem(n) for n in ("nmax", "e0", "den", "r0", "fbn", "fmv", "feps", "frstd", "fy", "fyg"))

    def steps_of(u):
        t = [("T", 0)] if u % passes == 0 else []
        if narrow:
            return [[("v", 0)], [("v", 1)], [("T", 0), ("q", 0), ("k", 0)] if u == 1 else [], []]
        qk = [(kind, j) for j in range(4) for kind in "qk"]
        v = [("v", j) for j in range(TG)]
        return [t + qk[0:4], qk[4:8] + ([("z", 0)] if null else []), v[0:2], v[2:4]]

    def banked(steps):
        count, out = {"A": 0, "B": 0}, []
        for jobs in steps:
            row = []
            for kind, j in jobs:
                b = {"T": "A", "z": "B", "r": "A"}.get(kind) or (
                    {"q": "B", "k": "A"}.get(kind) or ("AB" if narrow else "BA")[j % 2])
                row.append((kind, j, b, count[b]))
                count[b] += 1
            out.append((row, dict(count)))
        return out, count

    r = [("r", 0)] if null else []
    first = [("T", 0), ("q", 0), ("k", 0), ("v", 0), ("v", 1)] if narrow else sum(steps_of(0), [])
    table_first, base = banked([first])
    s1, s2 = steps_of(1), steps_of(2)
    table, per = banked(s1 + s2[:3] + [r + s2[3]])
    table_last, _ = banked((s1[:2] + [[], []] if narrow else s1) + [[], [], [], r])

    def target(job, un):
        if job[0] == "r":
            return un
        return un.next().next() if narrow and job[0] in "Tqk" else un.next()

    def before(b, i, it):
        return i if it is None else base[b] + it * per[b] + i

    def takes(kind, j):
        return V if kind == "z" or (narrow and kind == "v") else A

    def te_job(te, job, it, un):
        kind, j, b, i = job
        u, p, out = un.u, un.p, bank[job[2]]
        te.wait_ge(done[b], before(b, i, it))
        if kind == "T":
            te.wait_ge(norm.ready, un.g + 1)
            for t in range(TG):
                last = T.transpose(out[:, t * P:(t + 1) * P], hn[:, t, :], c.w["ident"][:, :])
        elif kind == "q":
            if j == 0 and un.p == 0:
                te.wait_ge(done["A"], before("A", i_T(it, un), it) + 1)
            col = j * P + (0 if narrow else p * HP * DH)
            last = T.matmul(out, wq[:, col:col + P], hT, start=True, stop=True)
        elif kind == "k":
            if j == 0:
                te.wait_ge(ctx_in[u], (un.it + 1) * 16 * loads)
            col = j * P + (0 if narrow else p * HP * DH)
            cx = ctx[u][0:DC, :, 0, :] if narrow else ctx[u][0:DC, :]
            last = T.matmul(out, wk[:, col:col + P], cx, start=True, stop=True)
        elif kind == "z":
            for t in range(TG):
                last = T.matmul(out[:, t * HP:(t + 1) * HP], hT[:, t * P:(t + 1) * P],
                                c.w["l3_wnull"][:, p * HP:(p + 1) * HP], start=True, stop=True)
        elif kind == "v" and narrow:
            te.wait_ge(ctx_in[u], (un.it + 1) * 16 * loads)
            for i in range(4):
                s = 4 * j + i
                last = T.matmul(out[:, i * P:(i + 1) * P], ctx[u][0:DC, s, :, :].rearrange("p e k -> p (e k)"), wv,
                                start=True, stop=True)
        elif kind == "v":
            last = T.matmul(out, ctx[u][0:DC, j * P:(j + 1) * P], wv[:, p * HP * DH:(p + 1) * HP * DH],
                            start=True, stop=True)
        elif kind == "r":
            te.wait_ge(r0_ready, un.g * 2 * TG + 2 * TG)
            for t in range(TG):
                last = T.transpose(out[0:2 * HP, t * P:(t + 1) * P], r0[:, t, :], c.w["ident"][:, :])
        last.then_inc(full[b], 1)

    def i_T(it, un):
        rows = table_first if it is None else table
        s = 0 if it is None else 2 if narrow else TG * (1 - un.u)
        return next(i for kind, _, _, i in rows[s][0] if kind == "T")

    def te_scores(te, n, un, t):
        if masked or narrow:
            te.wait_ge(s_out, n)
        elif not (isinstance(n, int) and n == 0):
            te.wait_ge(sub_ready, n)
        for j in range(1 if narrow else HP // 2):
            for b in range(2):
                half, s = slice(b * S, b * S + S), 2 * t + b
                q = qT[un.u][:, j, s * S:(s + 1) * S]
                if narrow:
                    last = T.matmul(ps_s[half, :, :], q, kz[un.u][:, :, s * S:(s + 1) * S], start=True, stop=True)
                else:
                    last = T.matmul(ps_s[half, 2 * j:2 * j + 2, :], q, kz[un.u][:, j, s, :, :], start=True, stop=True)
        last.then_inc(s_ready, 1)

    def te_wait_unit(te, it, un, row):
        if narrow:
            te.wait_ge(kz_ready, un.k * 4 + 4)
            if un.p == 1:
                te.wait_ge(q_copied, un.g + 1)
            return
        cnt = (table_first if it is None else table)[row][1]
        for b in "AB":
            te.wait_ge(done[b], before(b, cnt[b], it))

    def two_on(un, t):
        return (un, t + 2) if t < 2 else (un.next(), t - 2)

    def te_turn(te, n, t):
        te.wait_ge(o_out, n + 2)
        T.transpose(c.ps[:, 3, 0:P], o[:, t, :], c.w["ident"][:, :]).then_inc(ot_ready, 1)

    def te_out(te, un, t):
        te.wait_ge(ot_out, un.g * TG + t + 1)
        if t == 0:
            te.wait_ge(added, un.g + 1)
        T.matmul(acc[:, t, :], oT[:, 0, :], wo, start=(t == 0), stop=True, skip_group_check=True).then_inc(acc_ready, 1)

    def act_turned(act, un, t):
        act.wait_ge(ot_ready, un.g * TG + t + 1)
        A.activation(oT[:, 0, :], c.ps[:, 3, 0:P], ACT.Copy).then_inc(ot_out, 1)

    def te_step(te, it, un, t, last_pair):
        rows = table_last if last_pair else table
        n = it * 8 + (4 * un.u + t)
        end = last_pair and un.u == 1

        def scores_ahead():
            if t < 2 or not end:
                if t == 2:
                    te_wait_unit(te, it, un.next(), 4 * un.u + 1)
                te_scores(te, n + 2, *two_on(un, t))

        if narrow:
            scores_ahead()
        te.wait_ge(pt_out, n * parts + 1)
        if narrow:
            te.wait_ge(exp_ready, n + 1)
            for j in range(HP // 2):
                tr = T.transpose(ps_t[:, j, :], pr[t % 2][:, 2 * j:2 * j + 2, :].rearrange("p h k -> p (h k)"), c.w["ident"][:, :])
            tr.then_inc(pt_ready, 1)
        else:
            te.wait_ge(pbd_ready, n + 1)
            for h in range(HP):
                tr = T.transpose(ps_t[:, h, :], pbd[:, h, :], c.w["ident"][:, :])
                if h % 4 == 3:
                    tr.then_inc(pt_ready, 1)
        jobs = rows[4 * un.u + t][0]
        if jobs and jobs[0][0] in "Tr":
            te_job(te, jobs[0], it, target(jobs[0], un))
            jobs = jobs[1:]
        if not narrow:
            scores_ahead()
        if narrow and un.p == 1 and t:
            te_turn(te, n - 1, t - 1)
        if narrow:
            for job in jobs:
                te_job(te, job, it, target(job, un))
            jobs = []
        te.wait_ge(pt_out, n * parts + parts + 1)
        te.wait_ge(o_out, n + 1)
        if narrow:
            for b in range(2):
                half = slice(b * S, b * S + S)
                for j in range(HP // 2):
                    last = T.matmul(ps_o[half, 0, 16 * j:16 * j + 16], ptT[:, j, half], vz[un.u][:, 2 * t + b, j, :],
                                    start=True, stop=True)
        else:
            for h in range(HP):
                half = slice(DH * (h % 2), DH * (h % 2) + DH)
                last = T.matmul(ps_o[half, h // 2, :], vv[un.u][:, t, h * DH:(h + 1) * DH], ptT[:, h, :],
                                start=True, stop=True)
        last.then_inc(o_ready, 1)
        for job in jobs:
            te_job(te, job, it, target(job, un))
        if t == TG - 1 and not end:
            cnt = rows[4 * un.u + t][1]
            te_v_wait = [(b, before(b, cnt[b], it)) for b in "AB"]
        if narrow:
            if un.p == 1 and t:
                te_out(te, un, t - 1)
            if un.p == 1 and t == TG - 1:
                te_turn(te, n, t), te_out(te, un, t)
            if t == TG - 1 and not end:
                for b, v in te_v_wait:
                    te.wait_ge(done[b], v)
            return
        te.wait_ge(o_out, n + 2)
        if t == 0 and un.p == 0:
            te.wait_ge(added, un.g + 1)
        for j in range(HP // 2):
            last = T.matmul(acc[:, t, :], oT[:, j, :], wo[:, un.p * 4 + j, :], start=(un.p == 0 and t == 0 and j == 0),
                            stop=(j == HP // 2 - 1 and un.p == passes - 1), skip_group_check=True)
        if null and un.p == 1 and t == TG - 1:
            _, _, b, i = rows[4 * un.u + t][0][0]
            te.wait_ge(done[b], before(b, i, it) + 1)
            for tt in range(TG):
                last = T.matmul(acc[:, tt, :], r0T[0:2 * HP, tt * P:(tt + 1) * P], c.w["l3_nwo"][:, :],
                                start=False, stop=True, skip_group_check=True)
        last.then_inc(acc_ready, 1)
        if t == TG - 1 and not end:
            for b, v in te_v_wait:
                te.wait_ge(done[b], v)

    def take(eng, who, job, it, un):
        kind, j, b, i = job
        src, u, p = bank[b], un.u, un.p
        on_act = who is A
        copy = (lambda o, s: A.activation(o, s, ACT.Copy)) if on_act else (lambda o, s: V.tensor_copy(o, s))
        eng.wait_ge(full[b], before(b, i, it) + 1)
        if kind == "T":
            last = copy(hT, src)
        elif kind == "q" and narrow:
            if it is not None:
                eng.wait_ge(q_copied, un.g)
            last = A.activation(qT[u][:, 0, :], src, ACT.Identity, bias=c.w["l2_bcol"][:, 0:1])
        elif kind == "q":
            last = copy(qT[u][:, j, :], src)
        elif kind == "k" and narrow:
            if it is not None:
                eng.wait_ge(kz_ready, un.k * 4)
            last = A.activation(kT, src, ACT.Identity, bias=c.w["l2_bcol"][:, 1:2])
        elif kind == "k":
            sk = src.rearrange("p (s k) -> p s k", k=S)
            copy(kz[u][0:DH, j, :, 0, :], sk[0:DH])
            last = copy(kz[u][DH:P, j, :, 1, :], sk[DH:P])
        elif kind == "z":
            last = V.tensor_scalar(s0[u].rearrange("p t h -> p (t h)"), src[:, 0:TG * HP], scale, None, ALU.mult)
        elif kind == "v" and narrow:
            for e in range(2):
                rows = slice(e * S, e * S + S)
                head = lambda ap: ap.rearrange("p s (a e d) -> p s a e d", e=2, d=8)[:, :, p * HP // 2:(p + 1) * HP // 2, e, :]
                last = V.tensor_tensor(vz[u][rows, 4 * j:4 * j + 4, :, 8 * e:8 * e + 8],
                                       head(src[rows, :].rearrange("p (s f) -> p s f", f=P)),
                                       head(bc(c.w["rows"][rows, 6, :], 1, 4)), ALU.add)
        elif kind == "v":
            last = copy(vv[u][:, j, :], src)
        elif kind == "r":
            last = copy(r0T[0:2 * HP, :], src[0:2 * HP, :])
        last.then_inc(done[b], 1)

    def taken(kind, pair):
        rows, s = (table_first, 0) if pair is None else (table, 2)
        _, _, b, i = next(job for job in rows[s][0] if job[0] == kind)
        return done[b], before(b, i, pair) + 1, per[b]

    def mask_keys(eng, pair, un, quarters, back=False):
        s, v, step = taken("k", pair)
        eng.wait_ge(s, v - step if back else v)
        for quarter in quarters:
            for h in (2 * quarter, 2 * quarter + 1):
                hm = c.w["hm"][:, un.p * HP + h:un.p * HP + h + 1]
                if quarter < 3:
                    last = A.activation(kz[un.u][:, h, :], kT, ACT.Copy, scale=hm)
                else:
                    last = V.tensor_scalar(kz[un.u][:, h, :], kT, hm, None, ALU.mult)
            last.then_inc(kz_ready, 1)

    def copy_q(act, pair):
        s, v, _ = taken("q", pair)
        act.wait_ge(s, v)
        A.activation(qT[1], qT[0], ACT.Copy).then_inc(q_copied, 1)

    def act_exp(act, n, t):
        act.wait_ge(sub_ready, n + 1)
        if null:
            A.activation(e0[t % 2], e0[t % 2], ACT.Exp)
        A.activation(pr[t % 2], sc, ACT.Exp, scale=1.0 if masked else scale).then_inc(exp_ready, 1)

    def ve_max(ve, n, un, t):
        if masked and t == 0:
            ve.wait_ge(nm_ready, un.k + 1)
        ve.wait_ge(s_ready, n + 1)
        if not (isinstance(n, int) and n == 0):
            ve.wait_ge(exp_ready, n)
        src = sc
        if masked:
            V.scalar_tensor_tensor(out=sc, in0=ps_s, scalar=scale, in1=bc(nm[un.u][:, t, :], 1, HP),
                                   op0=ALU.mult, op1=ALU.add).then_inc(s_out, 1)
        elif narrow:
            V.tensor_scalar(sc, ps_s, CLAMP / scale, -CLAMP / scale, ALU.min, ALU.max).then_inc(s_out, 1)
        else:
            src = ps_s
        if masked or narrow:
            ve.wait_ge(s_out, n + 1)
        V.tensor_reduce(mx, src, AX.X, ALU.max).then_inc(max_ready, 1)
        ve.wait_ge(max_ready, n + 1)
        if null:
            V.tensor_tensor(mx, mx, s0[un.u][:, t, :], ALU.max).then_inc(null_max, 1)
            ve.wait_ge(null_max, n + 1)
            V.tensor_tensor(e0[t % 2], s0[un.u][:, t, :], mx, ALU.subtract)
        V.tensor_tensor(sc, src, bc(mx, 2, S), ALU.subtract).then_inc(sub_ready, 1)

    def ve_probs(ve, n, un, t, it=None):
        ve.wait_ge(exp_ready, n + 1)
        if narrow and it is not None:
            ve.wait_ge(rec_ready, n)
        V.tensor_reduce(den, pr[t % 2], AX.X, ALU.add).then_inc(sum_ready, 1)
        ve.wait_ge(sum_ready, n + 1)
        if null:
            V.tensor_tensor(den, den, e0[t % 2], ALU.add).then_inc(den_ready, 1)
            ve.wait_ge(den_ready, n + 1)
        r = rec[t % 2]
        V.reciprocal(r, den).then_inc(rec_ready, 1)
        if narrow:
            return
        ve.wait_ge(rec_ready, n + 1)
        ve.wait_ge(pt_ready, n * 2)
        for b in range(2):
            half = slice(b * S, b * S + S)
            last = V.tensor_tensor(pbd[half, :, half], pr[t % 2][half, :, :], bc(r[half, :], 2, S), ALU.mult)
        last.then_inc(pbd_ready, 1)
        if null:
            if it is not None and t == 0 and un.p == 0:
                ve.wait_ge(full["A"], before("A", table[7][0][0][3], it) + 1)
            V.tensor_tensor(r0[:, t, un.p * HP:(un.p + 1) * HP], e0[t % 2], r, ALU.mult).then_inc(r0_ready, 1)

    def take_o(ve, n, un, t):
        ve.wait_ge(o_ready, n + 1)
        ve.wait_ge(rec_ready, n + 1)
        hd = lambda ap: ap.rearrange("p (h d) -> p h d", d=8)
        V.tensor_tensor(hd(o[:, t, un.p * 64:un.p * 64 + 64]), hd(ps_o[:, 0, 0:64]), bc(rec[t % 2], 2, 8),
                        ALU.mult).then_inc(o_out, 1)

    def ve_mask(ve, un):
        tiles = mask[:, bass.ds(un.g * TG, TG), :]
        V.tensor_scalar(nm[un.u], tiles, 1.0, -NEG, ALU.subtract, ALU.mult).then_inc(nm_ready, 1)

    def pairs(eng, body, n=units // 2):
        if n > 1:
            with eng.Fori(0, n - 1) as it:
                body(it, False)
        body(n - 1, True)

    with nc.Block() as block:
        @block.sync
        def _(sp):
            def load(un):
                src = d["ctxT"][:, bass.ds(un.g * GT, GT)]
                if not narrow:
                    sp.dma_start(ctx[un.u][0:DC, :], src).then_inc(ctx_in[un.u], 16)
                    return
                for e in range(loads):
                    sp.dma_start(ctx[un.u][0:DC, :, e, :], src.rearrange("c (s k) -> c s k", k=S)).then_inc(ctx_in[un.u], 16)

            def vdone(it, row):
                jobs = (table_first if it is None else table)[row][0]
                kind, j, b, i = [job for job in jobs if job[0] == "v"][-1]
                sp.wait_ge(full[b], before(b, i, it) + 1)

            if layer == 0:
                sp.dma_start(mask[:, :, :], d["mask0"]).then_inc(mask_in, 16)
            elif layer == 3:
                sp.dma_start(mask[:, :, :], d["mask1"]).then_inc(mask_in, 16)
            if layer == 2:
                for dst, src in ((c.w["l2f_g"], d["l2f_g"]), (c.w["l2f_u"], d["l2f_u"]), (c.w["l2f_d"], d["l2f_d"])):
                    sp.dma_start(dst, src).then_inc(c.l2f_in, 16)
            load(Unit(0, 0, passes)), load(Unit(0, 1, passes))
            vdone(None, 0)
            load(Unit(1, 0, passes))

            def reload(it, u):
                vdone(it, 4 * u + (1 if narrow else 3))
                load(Unit(it, u, passes).next().next().next())

            if units > 4:
                with sp.Fori(0, (units - 4) // 2) as it:
                    reload(it, 0), reload(it, 1)
            reload((units - 4) // 2, 0)

        @block.gpsimd
        def _(pool):
            norm.pool(pool, 0)
            if passes == 1:
                norm.pool(pool, 1)

            def body(it, last_pair):
                for u in range(2):
                    if passes == 1 and not last_pair:
                        norm.pool(pool, it * 2 + u + 2)
                    if passes == 2 and u == 0 and not last_pair:
                        norm.pool(pool, it + 1)
                if null:
                    pool.wait_ge(fin_mv, it + 1)
                    G.tensor_tensor(c.rstd[:, TG:2 * TG], c.mv[:, :, 1], c.w["eps"][:, 0:TG], ALU.add).then_inc(fin_eps, 1)
                    pool.wait_ge(fin_eps, it + 1)
                    G.tensor_tensor(c.rstd[:, TG:2 * TG], c.rstd[:, TG:2 * TG], c.w["half"][:, 0:TG], ALU.pow)\
                        .then_inc(fin_rstd, 1)

            pairs(pool, body)

        @block.tensor
        def _(te):
            te.wait_ge(zeroed, 2)
            for job in table_first[0][0]:
                te_job(te, job, None, Unit(0, 0, passes))
            te_wait_unit(te, None, Unit(0, 0, passes), 0)
            te_scores(te, 0, Unit(0, 0, passes), 0)
            te_scores(te, 1, Unit(0, 0, passes), 1)

            def body(it, last_pair):
                for u in range(2):
                    for t in range(TG):
                        te_step(te, it, Unit(it, u, passes), t, last_pair)

            pairs(te, body)

        @block.scalar
        def _(act):
            act.sem_inc(pt_out, 1), act.sem_inc(o_out, 1), act.sem_inc(added, 1)
            if not narrow:
                for k0 in kz:
                    last = A.activation(k0.rearrange("p j s e k -> p j (s e k)"), bc(bc(c.zero[:, 0:GT], 1, 2), 1, HP // 2), ACT.Copy)
                last.then_inc(zeroed, 1)
            else:
                act.sem_inc(zeroed, 1)
            act.wait_ge(zeroed, 2)
            for job in table_first[0][0]:
                if takes(*job[:2]) is A:
                    take(act, A, job, None, Unit(0, 0, passes))
            if narrow:
                mask_keys(act, None, Unit(0, 0, passes), (0, 1, 2)), copy_q(act, None)
            for t in range(2):
                act_exp(act, t, t)
            if narrow:
                mask_keys(act, None, Unit(0, 1, passes), (0, 1))

            def body(it, last_pair):
                rows = table_last if last_pair else table
                for u in range(2):
                    for t in range(TG):
                        un, n = Unit(it, u, passes), it * 8 + (4 * u + t)
                        more = t < 2 or not (last_pair and u)
                        for a in range(parts):
                            act.wait_ge(pt_ready, n * parts + a + 1)
                            A.activation(ptT[:, 4 * a:4 * a + 4, :], ps_t[:, 4 * a:4 * a + 4, :], ACT.Copy).then_inc(pt_out, 1)
                        mine = [job for job in rows[4 * u + t][0] if takes(*job[:2]) is A]
                        if mine and mine[0][0] in "Tr":
                            take(act, A, mine[0], it, target(mine[0], un))
                            mine = mine[1:]
                        if not narrow:
                            act.wait_ge(o_ready, n + 1)
                            A.activation(oT, ps_o, ACT.Copy).then_inc(o_out, 1)
                        if narrow and un.p == 1 and t:
                            act_turned(act, un, t - 1)
                        for job in mine:
                            take(act, A, job, it, target(job, un))
                        if more:
                            act_exp(act, n + 2, t)
                        if narrow and t == 0 and not (last_pair and u):
                            mask_keys(act, it, un.next(), (2,), back=u == 0)
                        if narrow and t == 2 and u and not last_pair:
                            copy_q(act, it)
                        if narrow and un.p == 1 and t == TG - 1:
                            act_turned(act, un, t)
                        if narrow and t >= 2 and not last_pair:
                            mask_keys(act, it, un.next().next(), (t - 2,))

            pairs(act, body)

        @block.vector
        def _(ve):
            if narrow:
                V.memset(vz[0], 0.0)
                V.memset(vz[1], 0.0).then_inc(zeroed, 1)
            else:
                V.memset(pbd, 0.0).then_inc(zeroed, 1)
            norm.vector(ve, 0)
            ve.wait_ge(zeroed, 2)
            if masked:
                ve.wait_ge(mask_in, 16)
                ve_mask(ve, Unit(0, 0, passes))
            for job in table_first[0][0]:
                if takes(*job[:2]) is V:
                    take(ve, V, job, None, Unit(0, 0, passes))
            if narrow:
                mask_keys(ve, None, Unit(0, 0, passes), (3,))
            if passes == 1:
                ve.wait_ge(full["A"], 1)
                norm.vector(ve, 1)
            ve_max(ve, 0, Unit(0, 0, passes), 0), ve_max(ve, 1, Unit(0, 0, passes), 1)
            ve_probs(ve, 0, Unit(0, 0, passes), 0)

            def body(it, last_pair):
                rows = table_last if last_pair else table
                for u in range(2):
                    for t in range(TG):
                        un, n = Unit(it, u, passes), it * 8 + (4 * u + t)
                        end = last_pair and u == 1
                        if narrow and t:
                            for job in rows[4 * u + t - 1][0]:
                                if job[0] == "v":
                                    take(ve, V, job, it, target(job, un))
                        if t < TG - 1:
                            ve_probs(ve, n + 1, un, t + 1, it)
                        elif not end:
                            ve_probs(ve, n + 1, un.next(), 0, it)
                        if t < 2 or not end:
                            if t == 2 and masked:
                                ve_mask(ve, un.next())
                            ve_max(ve, n + 2, *two_on(un, t))
                        if narrow:
                            if t == 0 and not end:
                                mask_keys(ve, it, un.next(), (3,), back=u == 0)
                        if not narrow:
                            for job in rows[4 * u + t][0]:
                                if takes(*job[:2]) is V:
                                    take(ve, V, job, it, target(job, un))
                        if narrow:
                            take_o(ve, n, un, t)
                        if not last_pair and (passes == 1 or u == 0):
                            g = it * 2 + u + 2 if passes == 1 else it + 1
                            if t == (0 if narrow else 1):
                                norm.take_moments(ve, g)
                            elif t == (1 if narrow else 2):
                                norm.scale(ve, g)
                                if null:
                                    norm.take_moments(ve, g, 1)
                            elif t == 3 and null:
                                norm.scale(ve, g, 1)
                        if t == TG - 1 and un.p == passes - 1:
                            ve_add(ve, un, n)

            def ve_add(ve, un, n):
                xg = norm.xg(un.g)
                ve.wait_ge(acc_ready, un.g * TG + TG if narrow else n + 1)
                if not null:
                    ve.wait_ge(norm.biased, un.g + 1)
                    V.scalar_tensor_tensor(out=xg, in0=acc, scalar=c.w["tg"][:, layer:layer + 1], in1=xg,
                                           op0=ALU.mult, op1=ALU.add).then_inc(added, 1)
                    return
                for t in range(TG):
                    last = V.bn_stats(c.st[:, t, :], acc[:, t, :])
                last.then_inc(fin_bn, 1)
                ve.wait_ge(fin_bn, un.g + 1)
                V.memset(c.pause[:, 0:1], 0.0)
                for t in range(TG):
                    last = V.bn_aggr(c.mv[:, t, :], c.st[:, t, :])
                last.then_inc(fin_mv, 1)
                ve.wait_ge(fin_rstd, un.g + 1)
                for t in range(TG):
                    last = V.tensor_scalar(y[:, t, :], acc[:, t, :], c.mv[:, t, 0:1], c.rstd[:, TG + t:TG + t + 1],
                                           ALU.subtract, ALU.mult)
                last.then_inc(fin_y, 1)
                ve.wait_ge(fin_y, un.g + 1)
                V.tensor_tensor(y, y, bc(c.w["rows"][:, 5, :], 1, TG), ALU.mult).then_inc(fin_yg, 1)
                ve.wait_ge(fin_yg, un.g + 1)
                V.tensor_tensor(xg, xg, y, ALU.add).then_inc(added, 1)

            pairs(ve, body)


def by_pairs(eng, n, body):
    if n > 2:
        with eng.Fori(0, n // 2 - 1) as it:
            body(it * 2, 0, False)
            body(it * 2 + 1, 1, False)
    body(n - 2, 0, True)
    body(n - 1, 1, True)


def dense(c, d, layer):
    nc = c.nc
    V, A, T, G = nc.vector, nc.scalar, nc.tensor, nc.gpsimd
    pre = f"f{layer}_"
    hidden = layer == 3
    n, gate = c.ngroup, 4 + layer
    w = c.carve()
    hn = w([TG, P])
    hT = [w([GT]), w([GT])]
    hid = [w([4, GT]), w([4, GT])] if hidden else None
    ps_t, acc = c.ps[:, 0, :], [c.ps[:, 1, :], c.ps[:, 2, :]]
    ps_h = [c.ps[:, 4 + j, :] for j in range(4)]
    norm = Norm(c, pre + "ln", hn, {1: 2, 3: 4}[layer])
    sem = lambda s: c.sem(pre + s)
    t_ready, t_out, h_ready, h_out, y_ready, added, stored = (
        sem(s) for s in ("t", "t_out", "h", "h_out", "y", "added", "stored"))

    with nc.Block() as block:
        if hidden:
            @block.sync
            def _(sp):
                out = d["out"].rearrange("(n p) c -> p n c", p=P)

                def send(g):
                    sp.wait_ge(added, g + 2)
                    sp.dma_start(out[:, bass.ds(g * TG, TG), :], norm.xg(g)).then_inc(stored, 16)
                with sp.Fori(0, n) as g:
                    send(g)
                sp.wait_ge(stored, 16 * n)

        @block.gpsimd
        def _(pool):
            with pool.Fori(0, n) as g:
                norm.pool(pool, g)

        @block.tensor
        def _(te):
            def transposes(g):
                te.wait_ge(norm.ready, g + 1)
                te.wait_ge(t_out, g)
                for t in range(TG):
                    last = T.transpose(ps_t[:, t * P:(t + 1) * P], hn[:, t, :], c.w["ident"][:, :])
                last.then_inc(t_ready, 1)

            def hidden_chunk(g, u, j):
                te.wait_ge(t_out, g + 1)
                if not (isinstance(g, int) and g == 0):
                    te.wait_ge(h_out, g * 4 if j == 0 else g * 4 + j - 3)
                T.matmul(ps_h[j], c.w["l3f_w1"][:, j * P:(j + 1) * P], hT[u], start=True, stop=True).then_inc(h_ready, 1)

            transposes(0), transposes(1)
            if hidden:
                for j in range(4):
                    hidden_chunk(0, 0, j)

            def body(g, u, last_pair):
                te.wait_ge(added, g + 1)
                for j in range(4 if hidden else 1):
                    if hidden and not (last_pair and u):
                        hidden_chunk(g + 1, 1 - u, j)
                    if hidden:
                        te.wait_ge(h_out, g * 4 + j + 1)
                    else:
                        te.wait_ge(t_out, g + 1)
                    for t in range(TG):
                        lhs = (hid[u][:, j, :] if hidden else hT[u])[:, t * P:(t + 1) * P]
                        last = T.matmul(acc[u][:, t * D:(t + 1) * D], lhs, c.w["l3f_w2"][:, j, :] if hidden else c.w["l1f_g"][:, :],
                                        start=(j == 0 and t == 0), stop=(j == (3 if hidden else 0)), skip_group_check=True)
                last.then_inc(y_ready, 1)
                if not last_pair:
                    transposes(g + 2)

            by_pairs(te, n, body)

        @block.scalar
        def _(act):
            def take_hT(g, u):
                act.wait_ge(t_ready, g + 1)
                A.activation(hT[u], ps_t, ACT.Copy).then_inc(t_out, 1)

            def gelu(g, u, j):
                act.wait_ge(h_ready, g * 4 + j + 1)
                A.activation(hid[u][:, j, :], ps_h[j], ACT.Gelu_apprx_tanh, bias=c.w["l3f_b1"][:, j:j + 1]).then_inc(h_out, 1)

            act.sem_inc(added, 1)
            take_hT(0, 0), take_hT(1, 1)
            if hidden:
                for j in range(4):
                    gelu(0, 0, j)

            def body(g, u, last_pair):
                if hidden and not (last_pair and u):
                    for j in range(4):
                        gelu(g + 1, 1 - u, j)
                if not last_pair:
                    take_hT(g + 2, u)

            by_pairs(act, n, body)

        @block.vector
        def _(ve):
            norm.vector(ve, 0)
            ve.wait_ge(t_ready, 1)
            norm.vector(ve, 1)

            def body(g, u, last_pair):
                if not last_pair:
                    ve.wait_ge(t_ready, g + 2)
                    norm.vector(ve, g + 2)
                ve.wait_ge(y_ready, g + 1)
                ve.wait_ge(norm.biased, g + 1)
                xg = norm.xg(g)
                V.scalar_tensor_tensor(out=xg, in0=acc[u].rearrange("p (t c) -> p t c", c=D),
                                       scalar=c.w["tg"][:, gate:gate + 1], in1=xg, op0=ALU.mult, op1=ALU.add).then_inc(added, 1)

            by_pairs(ve, n, body)


def experts(c, d):
    nc = c.nc
    V, A, T, G = nc.vector, nc.scalar, nc.tensor, nc.gpsimd
    n = c.ngroup
    WB = 512
    blocks = [(s, min(WB, W2N - s)) for s in range(0, W2N, WB)]
    NB = len(blocks)
    NS = TG * NB
    w = c.carve()
    hn = w([TG, P])
    hT = [w([GT]), w([GT])]
    r = c.carve(c.parts)
    hTh, hTl = [r([GT]), r([GT])], [r([GT]), r([GT])]
    wgh, wgl, wuh, wul = (r([W2N]) for _ in range(4))
    sg, a = [w([WB]), w([WB])], [w([WB]), w([WB])]
    aT = [w([4, P]), w([4, P])]
    wts = [w([TG, NE2]), w([TG, NE2])]
    den, score, choice, rep, sel = (w([TG, NE2]) for _ in range(5))
    top, gt, eq = w([TG * 4, 8]), w([TG, 4, 4]), w([TG, 4, 4])
    gs, rank, t8, ws = w([TG, 4]), w([TG, 4]), w([TG, 8]), w([TG])
    ps_g, ps_u, ps_a = (tuple(c.ps[:, i + j, :] for j in range(2)) for i in (0, 2, 4))
    acc, ps_x = c.ps[:, 6, :], c.ps[:, 7, :]
    norm = Norm(c, "f2_ln", hn)
    sem = lambda s: c.sem("f2_" + s)
    x_ready, x_out, gu_ready, silu_ready, u_read, a_ready, at_ready, at_out, y_ready, added, link = (
        sem(s) for s in ("x", "x_out", "gu", "silu", "u_read", "a", "at", "at_out", "y", "added", "link"))
    LINKS = 16
    wts_ready, norm_link = sem("wts"), sem("norm_link")
    high_ready, low_ready, w_high, w_low = sem("high"), sem("low"), sem("w_high"), sem("w_low")

    def ahead(g, u, s):
        return (g, u, s + 2) if s + 2 < NS else (g + 1, 1 - u, s + 2 - NS)

    with nc.Block() as block:
        @block.gpsimd
        def _(pool):
            with pool.Fori(0, n) as g:
                norm.pool(pool, g)

        @block.tensor
        def _(te):
            def transposes(g):
                te.wait_ge(norm.ready, g + 1)
                te.wait_ge(x_out, g * 2)
                for t in range(TG):
                    last = T.transpose(ps_x[:, t * P:(t + 1) * P], hn[:, t, :], c.w["ident"][:, :])
                last.then_inc(x_ready, 1)

            def router(g, u):
                te.wait_ge(x_out, g * 2 + 1)
                for t in range(TG):
                    last = T.matmul(ps_x[:, t * NE2:(t + 1) * NE2], hT[u][:, t * P:(t + 1) * P], c.w["l2f_wr"][:, :],
                                    start=True, stop=True)
                last.then_inc(x_ready, 1)

            def gate_up(g, u, s):
                t, (c0, width) = s // NB, blocks[s % NB]
                m = g * NS + s
                if not (isinstance(g, int) and g == 0 and s < 2):
                    te.wait_ge(u_read, m - 1)
                if s == 0:
                    te.wait_ge(low_ready, g + 1)
                rows, cols = slice(t * P, (t + 1) * P), slice(c0, c0 + width)
                lhs = hTh[u][:, rows], hTl[u][:, rows]
                product3(c, ps_g[s % 2][:, 0:width], lhs, (wgh[:, cols], wgl[:, cols]))
                product3(c, ps_u[s % 2][:, 0:width], lhs, (wuh[:, cols], wul[:, cols])).then_inc(gu_ready, 1)

            te.wait_ge(c.l2f_in, 48)
            transposes(0), router(0, 0)
            te.wait_ge(w_low, 2)
            gate_up(0, 0, 0), gate_up(0, 0, 1)

            def body(g, u, last_pair):
                end = last_pair and u == 1
                for s in range(NS):
                    m, t, (c0, width) = g * NS + s, s // NB, blocks[s % NB]
                    te.wait_ge(a_ready, m + 1)
                    for j in range(width // P):
                        last = T.transpose(ps_a[s % 2][:, j * P:(j + 1) * P], a[s % 2][:, j * P:(j + 1) * P], c.w["ident"][:, :])
                    last.then_inc(at_ready, 1)
                    if not (end and s + 2 >= NS):
                        gate_up(*ahead(g, u, s))
                    if s == 1 and not end:
                        transposes(g + 1)
                    if s == 3 and not end:
                        router(g + 1, 1 - u)
                    te.wait_ge(at_out, m + 1)
                    if s == 0:
                        te.wait_ge(added, g + 1)
                    for j in range(width // P):
                        last = T.matmul(acc[:, t * D:(t + 1) * D], aT[s % 2][:, j, :], c.w["l2f_d"][:, c0 // P + j, :],
                                        start=(s % NB == 0 and j == 0), stop=(s % NB == NB - 1), skip_group_check=True)
                last.then_inc(y_ready, 1)

            by_pairs(te, n, body)

        @block.scalar
        def _(act):
            def take_hT(g, u):
                act.wait_ge(x_ready, g * 2 + 1)
                A.activation(hT[u], ps_x, ACT.Copy).then_inc(x_out, 1)

            def silu(g, s):
                width = blocks[s % NB][1]
                act.wait_ge(gu_ready, g * NS + s + 1)
                A.activation(sg[s % 2][:, 0:width], ps_g[s % 2][:, 0:width], ACT.Silu).then_inc(silu_ready, 1)

            def sigmoid_exp(g):
                act.wait_ge(x_ready, g * 2 + 2)
                A.activation(den.rearrange("p t e -> p (t e)"), ps_x[:, 0:TG * NE2], ACT.Exp, scale=-1.0).then_inc(x_out, 1)

            act.sem_inc(added, 1)
            take_hT(0, 0), sigmoid_exp(0), silu(0, 0), silu(0, 1)

            def body(g, u, last_pair):
                end = last_pair and u == 1
                for s in range(NS):
                    width = blocks[s % NB][1]
                    act.wait_ge(at_ready, g * NS + s + 1)
                    A.activation(aT[s % 2][:, 0:width // P, :].rearrange("p j q -> p (j q)"), ps_a[s % 2][:, 0:width],
                                 ACT.Copy).then_inc(at_out, 1)
                    if not (end and s + 2 >= NS):
                        g2, _, s2 = ahead(g, u, s)
                        silu(g2, s2)
                    if s == 1 and not end:
                        take_hT(g + 1, 1 - u)
                    if s == 3 and not end:
                        sigmoid_exp(g + 1)

            by_pairs(act, n, body)

        @block.vector
        def _(ve):
            def chained(g, i, ins):
                ins.then_inc(link, 1)
                ve.wait_ge(link, g * LINKS + i)

            def mults(g, u, s):
                width = blocks[s % NB][1]
                m = g * NS + s
                ve.wait_ge(silu_ready, m + 1)
                out = a[s % 2][:, 0:width]
                first = V.tensor_tensor(out, sg[s % 2][:, 0:width], ps_u[s % 2][:, 0:width], ALU.mult)
                first.then_inc(u_read, 1)
                ve.wait_ge(u_read, m + 1)
                e0 = blocks[s % NB][0] // I2
                if width == WB:
                    if s % NS == 0:
                        ve.wait_ge(wts_ready, g + 1)
                    o3 = out.rearrange("p (e i) -> p e i", i=I2)
                    V.tensor_tensor(o3, o3, bc(wts[u][:, s // NB, e0:e0 + WB // I2], 2, I2), ALU.mult).then_inc(a_ready, 1)
                else:
                    V.memset(c.pause[:, 1:2], 0.0).then_inc(a_ready, 1)

            def routing(g, u, part):
                ch = lambda i, ins: chained(g, i, ins)
                if part == 0:
                    ve.wait_ge(x_out, g * 2 + 2)
                    ch(1, V.tensor_scalar(den, den, 1.0, None, ALU.add))
                    V.reciprocal(score, den).then_inc(link, 1)
                elif part == 1:
                    ve.wait_ge(link, g * LINKS + 2)
                    V.tensor_tensor(choice, score, bc(c.w["l2f_bias"][:, :], 1, TG), ALU.add).then_inc(link, 1)
                elif part == 2:
                    ve.wait_ge(link, g * LINKS + 3)
                    V.memset(c.pause[:, 0:1], 0.0)
                    for i in range(TG * 4):
                        last = V.max(top[:, i, :], choice[:, i // 4, (i % 4) * 8:(i % 4) * 8 + 8])
                    ch(4, last)
                    t4 = top.rearrange("p (t q) k -> p t q k", t=TG)
                    V.tensor_tensor(gs, t4[:, :, :, 0], t4[:, :, :, 1], ALU.add).then_inc(link, 1)
                elif part == 3:
                    ve.wait_ge(link, g * LINKS + 5)
                    mine, other = bc(gs, 3, 4), bc(gs, 2, 4)
                    V.tensor_tensor(gt, other, mine, ALU.is_gt)
                    V.tensor_tensor(eq, other, mine, ALU.is_equal).then_inc(link, 1)
                elif part == 4:
                    ve.wait_ge(link, g * LINKS + 6)
                    ch(7, V.tensor_tensor(eq, eq, bc(c.w["tri4"][:, 0:4, :], 1, TG), ALU.mult))
                    V.tensor_tensor(gt, gt, eq, ALU.add).then_inc(link, 1)
                elif part == 5:
                    ve.wait_ge(link, g * LINKS + 8)
                    ch(9, V.tensor_reduce(rank, gt, AX.X, ALU.add))
                    V.tensor_scalar(rank, rank, 1.5, None, ALU.is_lt).then_inc(link, 1)
                elif part == 6:
                    ve.wait_ge(link, g * LINKS + 10)
                    c4 = choice.rearrange("p t (q k) -> p t q k", k=8)
                    ch(11, V.tensor_tensor(c4, c4, bc(rank, 3, 8), ALU.mult))
                    V.memset(c.pause[:, 0:1], 0.0)
                    for t in range(TG):
                        last = V.max(t8[:, t, :], choice[:, t, :])
                    last.then_inc(link, 1)
                elif part == 7:
                    ve.wait_ge(link, g * LINKS + 12)
                    V.memset(c.pause[:, 0:1], 0.0)
                    for t in range(TG):
                        last = V.match_replace(rep[:, t, :], t8[:, t, :], choice[:, t, :], -1e30)
                    last.then_inc(link, 1)
                elif part == 8:
                    ve.wait_ge(link, g * LINKS + 13)
                    V.tensor_tensor(sel, rep, choice, ALU.not_equal).then_inc(link, 1)
                elif part == 9:
                    ve.wait_ge(link, g * LINKS + 14)
                    ch(15, V.tensor_tensor(wts[u], sel, score, ALU.mult))
                    V.tensor_reduce(ws, wts[u], AX.X, ALU.add).then_inc(link, 1)
                elif part == 10:
                    ve.wait_ge(link, g * LINKS + 16)
                    V.tensor_scalar(ws, ws, 1e-20, None, ALU.add).then_inc(norm_link, 1)
                    ve.wait_ge(norm_link, g * 3 + 1)
                    V.reciprocal(ws, ws).then_inc(norm_link, 1)
                elif part == 11:
                    ve.wait_ge(norm_link, g * 3 + 2)
                    V.tensor_scalar(ws, ws, 2.5, None, ALU.mult).then_inc(norm_link, 1)
                elif part == 12:
                    ve.wait_ge(norm_link, g * 3 + 3)
                    V.tensor_tensor(wts[u], wts[u], bc(ws, 2, NE2), ALU.mult).then_inc(wts_ready, 1)

            def split(g, u):
                ve.wait_ge(x_out, g * 2 + 1)
                split_high(c, hTh[u], hT[u]).then_inc(high_ready, 1)
                ve.wait_ge(high_ready, g + 1)
                split_low(c, hTl[u], hT[u], hTh[u]).then_inc(low_ready, 1)

            norm.vector(ve, 0)
            ve.wait_ge(c.l2f_in, 48)
            split_high(c, wgh, c.w["l2f_g"])
            split_high(c, wuh, c.w["l2f_u"]).then_inc(w_high, 1)
            ve.wait_ge(w_high, 1)
            split_low(c, wgl, c.w["l2f_g"], wgh).then_inc(w_low, 1)
            split_low(c, wul, c.w["l2f_u"], wuh).then_inc(w_low, 1)
            split(0, 0)
            for part in range(13):
                routing(0, 0, part)
            norm.vector(ve, 1)
            mults(0, 0, 0), mults(0, 0, 1)

            def body(g, u, last_pair):
                end = last_pair and u == 1
                for s in range(NS):
                    if not (end and s + 2 >= NS):
                        mults(*ahead(g, u, s))
                    if 5 <= s < 18 and not end:
                        routing(g + 1, 1 - u, s - 5)
                    if s == 2 and not end:
                        split(g + 1, 1 - u)
                    if s == 4 and not last_pair:
                        ve.wait_ge(x_ready, g * 2 + 3)
                        norm.vector(ve, g + 2)
                ve.wait_ge(y_ready, g + 1)
                xg = norm.xg(g)
                V.scalar_tensor_tensor(out=xg, in0=acc.rearrange("p (t c) -> p t c", c=D), scalar=c.w["tg"][:, 6:7], in1=xg,
                                       op0=ALU.mult, op1=ALU.add).then_inc(added, 1)

            by_pairs(ve, n, body)


def gated_attention(c, d):
    nc = c.nc
    V, A, T, G = nc.vector, nc.scalar, nc.tensor, nc.gpsimd
    n = c.ngroup
    ZW, NZ = 2 * QKV, NE0 // 2
    w = c.carve()
    hn = w([TG, P])
    hT = [w([GT]), w([GT])]
    r = c.carve(c.parts)
    hTh, hTl = [r([GT]), r([GT])], [r([GT]), r([GT])]
    wh, wl = r([NE0 * QKV]), r([NE0 * QKV])
    rw = [w([TG, NE0]), w([TG, NE0])]
    part_sum = [[w([QKV]), w([QKV])] for _ in range(2)]
    qvk0 = [w([4 * DH]), w([4 * DH])]
    qkT, sm, ex, pT = w([2 * P]), w([P]), w([P]), w([P])
    nmx, esum, rec, rwn = w([1]), w([1]), w([1]), w([NE0])
    mixed, mT = w([NE0, DH]), w([NE0 // 2, P])
    sq, n2, rn, rn_wait = w([P]), w([TG]), w([TG]), w([TG])
    lg, gated, active, l2, key, first, fb = (w([TG, NE0]) for _ in range(7))
    cnt, m1, m2, km = w([TG]), w([TG]), w([TG]), w([TG])
    ps_z = [c.ps[:, j, 0:ZW] for j in range(4)]
    ps_x, ps_y, ps_m, acc = (c.ps[:, 4 + j, :] for j in range(4))
    norm = Norm(c, "f0_ln", hn)
    sem = lambda s: c.sem("f0_" + s)
    z_ready, z_read, qkv_ready = sem("z"), sem("z_read"), sem("qkv")
    qkt_ready, qkt_out, s_ready, s_read, nmx_ready, exp_ready = (
        sem(s) for s in ("qkt", "qkt_out", "s", "s_read", "nmx", "exp"))
    pt_ready, pt_out, pv_ready, rec_ready, rwn_ready, mixed_ready = (
        sem(s) for s in ("pt", "pt_out", "pv", "rec", "rwn", "mixed"))
    m_ready, m_out, y_ready, added = (sem(s) for s in ("m", "m_out", "y", "added"))
    mt_ready, mt_out, r_ready, r_read, n2_ready, rn_ready, rw_ready, link = (
        sem(s) for s in ("mt", "mt_out", "r", "r_read", "n2", "rn", "rw", "link"))
    high_ready, low_ready, w_high, w_low = sem("high"), sem("low"), sem("w_high"), sem("w_low")
    gexp, first_read = sem("gexp"), sem("first")
    ADDS = NE0 - 2
    LINKS = 18

    def nxt(g, u, t):
        return (g, u, t + 1) if t < TG - 1 else (g + 1, 1 - u, 0)

    with nc.Block() as block:
        @block.gpsimd
        def _(pool):
            def row_norms(g):
                pool.wait_ge(n2_ready, g * TG + TG)
                G.tensor_tensor(rn_wait, c.zero[:, 0:TG], c.zero[:, 0:TG], ALU.add)
                G.tensor_scalar(rn, n2, 1e-24, None, ALU.max).then_inc(rn_ready, 1)
                pool.wait_ge(rn_ready, g * 2 + 1)
                G.tensor_tensor(rn, rn, c.w["half"][:, 0:TG], ALU.pow).then_inc(rn_ready, 1)

            norm.pool(pool, 0), row_norms(0), norm.pool(pool, 1)
            if n > 2:
                with pool.Fori(0, n - 2) as g:
                    row_norms(g + 1), norm.pool(pool, g + 2)
            row_norms(n - 1)

        @block.tensor
        def _(te):
            def transposes(g):
                te.wait_ge(norm.ready, g + 1)
                for t in range(TG):
                    last = T.transpose(ps_m[:, t * P:(t + 1) * P], hn[:, t, :], c.w["ident"][:, :])
                last.then_inc(m_ready, 1)

            def router(g, u):
                te.wait_ge(m_out, g + 1)
                for t in range(TG):
                    last = T.matmul(ps_y[:, t * NE0:(t + 1) * NE0], hT[u][:, t * P:(t + 1) * P], c.w["l0f_sim"][:, :],
                                    start=True, stop=True)
                last.then_inc(r_ready, 1)

            def project(g, u, t, j):
                m = g * TG + t
                if j == 4:
                    te.wait_ge(first_read, m * 2 + 2)
                elif j > 4 or not (isinstance(g, int) and g == 0 and t == 0):
                    te.wait_ge(z_read, m * ADDS + 2 * (j - 4) if j > 4 else m * ADDS - ADDS + 2 * (j + 4))
                if t == 0 and j == 0:
                    te.wait_ge(low_ready, g + 1)
                rows, cols = slice(t * P, (t + 1) * P), slice(j * ZW, (j + 1) * ZW)
                product3(c, ps_z[j % 4], (hTh[u][:, rows], hTl[u][:, rows]), (wh[:, cols], wl[:, cols])).then_inc(z_ready, 1)

            transposes(0), router(0, 0)
            te.wait_ge(w_low, 1)
            for j in range(NZ):
                project(0, 0, 0, j)

            def turn_mixed(g, t, q, last):
                m = g * TG + t
                te.wait_ge(mixed_ready, m + 1)
                if t == 0 and q == 0:
                    te.wait_ge(m_out, g + 1 if last else g + 2)
                te.wait_ge(mt_out, m * 2 + q + 1)
                for j in range(4):
                    e = (q * 4 + j) * 2
                    tr = T.transpose(ps_m[:, j * P:(j + 1) * P], mixed[:, e:e + 2, :].rearrange("p e i -> p (e i)"),
                                     c.w["ident"][:, :])
                tr.then_inc(mt_ready, 1)

            def back(g, t):
                m = g * TG + t
                if t == 0:
                    te.wait_ge(added, g + 1)
                for j in range(8):
                    if j % 4 == 0:
                        te.wait_ge(mt_out, m * 2 + j // 4 + 2)
                    out = T.matmul(acc[:, t * D:(t + 1) * D], mT[:, j, :], c.w["l0f_o"][:, j, :], start=(j == 0), stop=(j == 7))
                if t == TG - 1:
                    out.then_inc(y_ready, 1)

            def body(g, u, last_pair):
                last = last_pair and u == 1
                for t in range(TG):
                    end = last and t == TG - 1
                    m = g * TG + t
                    z = nxt(g, u, t)
                    before = (g, t - 1, last) if t else (g - 1, TG - 1, False) if u else None

                    def make(*js):
                        if not end:
                            for j in js:
                                project(*z, j)

                    make(0, 1)
                    te.wait_ge(qkv_ready, m + 1)
                    T.transpose(ps_x[:, 0:P], qvk0[t % 2][:, 0:P], c.w["ident"][:, :])
                    T.transpose(ps_x[:, P:2 * P], qvk0[t % 2][:, P:2 * P], c.w["ident"][:, :]).then_inc(qkt_ready, 1)
                    if before:
                        turn_mixed(before[0], before[1], 0, before[2])
                    make(2)
                    te.wait_ge(qkt_out, m + 1)
                    T.matmul(ps_x[:, 2 * P:3 * P], qkT[:, 0:P], qkT[:, P:2 * P], start=True, stop=True)\
                        .then_inc(s_ready, 1)
                    if t == 2 and not last:
                        router(g + 1, 1 - u)
                    if before:
                        turn_mixed(before[0], before[1], 1, before[2])
                    make(3, 4)
                    te.wait_ge(exp_ready, m + 1)
                    T.transpose(ps_x[:, 3 * P:4 * P], ex, c.w["ident"][:, :]).then_inc(pt_ready, 1)
                    make(5)
                    te.wait_ge(pt_out, m + 1)
                    if t in (0, 2):
                        te.wait_ge(r_read, g + 1 if t == 0 else (g + 1 if last else g + 2))
                    T.matmul(ps_y[:, 0:DH], pT, qvk0[t % 2][:, DH:2 * DH], start=True, stop=True).then_inc(pv_ready, 1)
                    make(6, 7)
                    if before:
                        back(*before[:2])
                    if t == 0 and not last:
                        te.wait_ge(mt_out, m * 2 + 1)
                        transposes(g + 1)
                    if u == 1 and t == TG - 1:
                        turn_mixed(g, t, 0, last), turn_mixed(g, t, 1, last), back(g, t)

            by_pairs(te, n, body)

        @block.scalar
        def _(act):
            def take_hT(g, u):
                act.wait_ge(m_ready, g + 1)
                A.activation(hT[u], ps_m, ACT.Copy).then_inc(m_out, 1)

            def squares(g):
                for t in range(TG):
                    if t:
                        act.wait_ge(n2_ready, g * TG + t)
                    else:
                        act.wait_ge(norm.ready, g + 1)
                    A.activation(sq, hn[:, t, :], ACT.Square, accum_out=n2[:, t:t + 1]).then_inc(n2_ready, 1)

            def take_mixed(m):
                for q in range(2):
                    act.wait_ge(mt_ready, m * 2 + q + 2)
                    A.activation(mT[:, 4 * q:4 * q + 4, :].rearrange("p j q -> p (j q)"), ps_m, ACT.Copy).then_inc(mt_out, 1)

            def gate_exp(g):
                act.wait_ge(link, g * LINKS + 15)
                A.activation(gated, gated, ACT.Exp).then_inc(gexp, 1)

            act.sem_inc(mt_out, 1), act.sem_inc(mt_ready, 1), act.sem_inc(added, 1)
            def first_sums(g, u, t):
                m = g * TG + t
                if t == 0:
                    act.wait_ge(rw_ready, g + 1)
                act.wait_ge(z_ready, m * NZ + 1)
                for e in range(2):
                    A.activation(part_sum[t % 2][e], ps_z[0][:, e * QKV:(e + 1) * QKV], ACT.Copy,
                                 scale=rw[u][:, t, e:e + 1]).then_inc(first_read, 1)

            take_hT(0, 0), squares(0), gate_exp(0), first_sums(0, 0, 0)

            def body(g, u, last_pair):
                for t in range(TG):
                    m = g * TG + t
                    if not (last_pair and u == 1 and t == TG - 1):
                        first_sums(*nxt(g, u, t))
                    act.wait_ge(qkt_ready, m + 1)
                    A.activation(qkT, ps_x[:, 0:2 * P], ACT.Copy).then_inc(qkt_out, 1)
                    if t or u:
                        take_mixed(m - 1)
                    act.wait_ge(nmx_ready, m + 1)
                    A.activation(ex, sm, ACT.Exp, bias=nmx[:, 0:1], accum_out=esum[:, 0:1]).then_inc(exp_ready, 1)
                    act.wait_ge(pt_ready, m + 1)
                    A.activation(pT, ps_x[:, 3 * P:4 * P], ACT.Copy).then_inc(pt_out, 1)
                    if t == 0 and not (last_pair and u == 1):
                        take_hT(g + 1, 1 - u)
                    if t == 1 and not (last_pair and u == 1):
                        squares(g + 1)
                    if u == 1 and t == TG - 1:
                        take_mixed(m)
                    if t == 2 and not (last_pair and u == 1):
                        gate_exp(g + 1)

            by_pairs(act, n, body)

        @block.vector
        def _(ve):
            def routing(g, u, part):
                at = g * LINKS

                def after(i):
                    ve.wait_ge(link, at + i)

                if part == 0:
                    ve.wait_ge(r_ready, g + 1)
                    ve.wait_ge(rn_ready, g * 2 + 2)
                    V.tensor_tensor(lg, ps_y[:, 0:TG * NE0].rearrange("p (t e) -> p t e", e=NE0), bc(rn, 2, NE0),
                                    ALU.mult).then_inc(r_read, 1)
                    ve.wait_ge(r_read, g + 1)
                    V.tensor_tensor(lg, lg, bc(c.w["l0f_sig"][:, :], 1, TG), ALU.subtract).then_inc(link, 1)
                elif part == 1:
                    after(1)
                    V.tensor_scalar(gated, lg, 0.0, None, ALU.max)
                    V.tensor_scalar(active, lg, 0.0, None, ALU.is_gt)
                    V.tensor_reduce(m1, lg, AX.X, ALU.max).then_inc(link, 1)
                elif part == 2:
                    after(2)
                    V.tensor_reduce(cnt, active, AX.X, ALU.add)
                    V.tensor_tensor(key, lg, bc(m1, 2, NE0), ALU.is_equal).then_inc(link, 1)
                    after(3)
                    V.tensor_tensor(key, key, bc(c.w["iota16"][:, :], 1, TG), ALU.mult).then_inc(link, 1)
                elif part == 3:
                    after(4)
                    V.tensor_reduce(km, key, AX.X, ALU.max).then_inc(link, 1)
                    after(5)
                    V.tensor_tensor(first, key, bc(km, 2, NE0), ALU.is_equal).then_inc(link, 1)
                elif part == 4:
                    after(6)
                    V.scalar_tensor_tensor(out=l2, in0=first, scalar=-1e30, in1=lg, op0=ALU.mult, op1=ALU.add).then_inc(link, 1)
                    after(7)
                    V.tensor_reduce(m2, l2, AX.X, ALU.max).then_inc(link, 1)
                elif part == 5:
                    after(8)
                    V.tensor_tensor(key, l2, bc(m2, 2, NE0), ALU.is_equal).then_inc(link, 1)
                    after(9)
                    V.tensor_tensor(key, key, bc(c.w["iota16"][:, :], 1, TG), ALU.mult).then_inc(link, 1)
                elif part == 6:
                    after(10)
                    V.tensor_reduce(km, key, AX.X, ALU.max).then_inc(link, 1)
                    after(11)
                    V.tensor_tensor(fb, key, bc(km, 2, NE0), ALU.is_equal).then_inc(link, 1)
                    V.tensor_scalar(cnt, cnt, 0.0, None, ALU.is_equal)
                elif part == 7:
                    after(12)
                    V.tensor_tensor(fb, fb, first, ALU.add).then_inc(link, 1)
                    V.tensor_reduce(m1, gated, AX.X, ALU.max)
                    after(13)
                    V.tensor_tensor(fb, fb, bc(cnt, 2, NE0), ALU.mult).then_inc(link, 1)
                elif part == 8:
                    after(14)
                    V.tensor_tensor(active, active, fb, ALU.add)
                    V.tensor_tensor(gated, gated, bc(m1, 2, NE0), ALU.subtract).then_inc(link, 1)
                elif part == 9:
                    ve.wait_ge(gexp, g + 1)
                    V.tensor_tensor(gated, gated, active, ALU.mult).then_inc(link, 1)
                    after(16)
                    V.tensor_reduce(cnt, gated, AX.X, ALU.add).then_inc(link, 1)
                elif part == 10:
                    after(17)
                    V.reciprocal(cnt, cnt).then_inc(link, 1)
                    after(18)
                    V.tensor_tensor(rw[u], gated, bc(cnt, 2, NE0), ALU.mult).then_inc(rw_ready, 1)

            def add_up(g, u, t, j):
                m = g * TG + t
                if j == 1 and t == 0:
                    ve.wait_ge(rw_ready, g + 1)
                ve.wait_ge(z_ready, m * NZ + j + 1)
                for e in range(2):
                    z, r = ps_z[j % 4][:, e * QKV:(e + 1) * QKV], rw[u][:, t, 2 * j + e:2 * j + e + 1]
                    if j == 1:
                        ve.wait_ge(first_read, m * 2 + e + 1)
                    else:
                        ve.wait_ge(z_read, m * ADDS + 2 * j + e - 3)
                    V.scalar_tensor_tensor(out=part_sum[t % 2][e], in0=z, scalar=r, in1=part_sum[t % 2][e],
                                           op0=ALU.mult, op1=ALU.add).then_inc(z_read, 1)
                if j == NZ - 1:
                    ve.wait_ge(z_read, m * ADDS + ADDS)
                    V.tensor_tensor(qvk0[t % 2][:, 0:QKV], part_sum[t % 2][0], part_sum[t % 2][1], ALU.add).then_inc(qkv_ready, 1)

            V.memset(qvk0[0][:, QKV:], 0.0)
            V.memset(qvk0[1][:, QKV:], 0.0)
            def split(g, u):
                ve.wait_ge(m_out, g + 1)
                split_high(c, hTh[u], hT[u]).then_inc(high_ready, 1)
                ve.wait_ge(high_ready, g + 1)
                split_low(c, hTl[u], hT[u], hTh[u]).then_inc(low_ready, 1)

            norm.vector(ve, 0)
            split_high(c, wh, c.w["l0f_w"]).then_inc(w_high, 1)
            ve.wait_ge(w_high, 1)
            split_low(c, wl, c.w["l0f_w"], wh).then_inc(w_low, 1)
            split(0, 0)
            for part in range(11):
                routing(0, 0, part)
            norm.vector(ve, 1)
            for j in range(1, NZ):
                add_up(0, 0, 0, j)

            def body(g, u, last_pair):
                more = not (last_pair and u == 1)
                for t in range(TG):
                    end = not more and t == TG - 1
                    m = g * TG + t
                    z = nxt(g, u, t)

                    def sums(*js):
                        if not end:
                            for j in js:
                                add_up(*z, j)
                    sums(1)
                    ve.wait_ge(s_ready, m + 1)
                    V.scalar_tensor_tensor(out=sm, in0=ps_x[:, 2 * P:3 * P], scalar=DH ** -0.5, in1=c.w["causal"][:, :],
                                           op0=ALU.mult, op1=ALU.add).then_inc(s_read, 1)
                    sums(2)
                    ve.wait_ge(s_read, m + 1)
                    V.tensor_reduce(nmx, sm, AX.X, ALU.max, negate=True).then_inc(nmx_ready, 1)
                    sums(3)
                    if t == 1 and more:
                        split(g + 1, 1 - u)
                    if t == 2 and more:
                        for part in (0, 1, 2, 3, 4):
                            routing(g + 1, 1 - u, part)
                    ve.wait_ge(exp_ready, m + 1)
                    V.reciprocal(rec, esum).then_inc(rec_ready, 1)
                    sums(4)
                    if t == 3 and not last_pair:
                        norm.take_moments(ve, g + 2)
                    ve.wait_ge(rec_ready, m + 1)
                    V.tensor_scalar(rwn, rw[u][:, t, :], rec[:, 0:1], None, ALU.mult).then_inc(rwn_ready, 1)
                    sums(5)
                    ve.wait_ge(pv_ready, m + 1)
                    ve.wait_ge(rwn_ready, m + 1)
                    ve.wait_ge(mt_ready, m * 2 + 1)
                    V.tensor_tensor(mixed, bc(ps_y[:, 0:DH], 1, NE0), bc(rwn, 2, DH), ALU.mult).then_inc(mixed_ready, 1)
                    if t == 2 and more:
                        for part in (5, 6, 7, 8):
                            routing(g + 1, 1 - u, part)
                    sums(6, 7)
                    if t == 2 and more:
                        for part in (9, 10):
                            routing(g + 1, 1 - u, part)
                    if t == 3 and not last_pair:
                        ve.wait_ge(n2_ready, g * TG + 2 * TG)
                        norm.scale(ve, g + 2)
                    if u == 1 and t == 0:
                        add(g - 1)
                if u == 1:
                    add(g)

            def add(g):
                ve.wait_ge(y_ready, g + 1)
                xg = norm.xg(g)
                V.scalar_tensor_tensor(out=xg, in0=acc.rearrange("p (t c) -> p t c", c=D), scalar=c.w["tg"][:, 4:5], in1=xg,
                                       op0=ALU.mult, op1=ALU.add).then_inc(added, 1)

            by_pairs(ve, n, body)


def program(nc, d, layers=range(8)):
    ctx = ExitStack()
    with ctx:
        c = Chip(nc, ctx)
        c.ntile = d["x"].shape[0] // P
        c.ngroup = c.ntile // TG
        c.ps = ctx.enter_context(nc.psum_tensor("ps", [P, 8, 512], FP))
        c.st = c.sbuf("st", [P, TG, 6])
        c.mv = c.sbuf("mv", [P, TG, 2])
        c.rstd = c.sbuf("rstd", [P, 2 * TG])
        c.zero = c.sbuf("zero", [P, 512])
        c.mask = c.sbuf("mask", [P, c.ntile, S], U8)
        c.pause = c.sbuf("pause", [1, 2])
        c.l2f_in = c.sem("l2f_in")
        c.own, c.opened = [], 0
        setup(c, d)
        c.close_work()
        for layer in layers:
            parts = {1: 4 * GT + 2 * NE0 * QKV, 5: 4 * GT + 4 * W2N}.get(layer, 0)
            c.open_work(12 * 1024 if parts else 26 * 1024, parts)
            if layer % 2 == 0:
                attention(c, d, layer // 2)
            elif layer == 1:
                gated_attention(c, d)
            elif layer in (3, 7):
                dense(c, d, layer // 2)
            elif layer == 5:
                experts(c, d)
            nc.clear_and_free_semaphores(c.own)
            c.own = []
            nc.all_engine_barrier()
            c.close_work()
        if 7 not in layers:
            store(c, d)


def store(c, d):
    out = c.sem("out")
    with c.nc.Block() as block:
        @block.sync
        def _(sp):
            sp.dma_start(d["out"].rearrange("(n p) c -> p n c", p=P), c.w["x"][:, :, :]).then_inc(out, 16)
            sp.wait_ge(out, 16)


def layouts(i):
    f = np.float32
    ca = np.ascontiguousarray
    a = {}
    nb = i["x"].shape[0]
    a["x"] = i["x"].reshape(nb * S, D)
    a["ctxT"] = ca(i["ctx_768"].reshape(nb * S, DC).T)
    for name, key in (("mask0", "mask_BxS2_bk0"), ("mask1", "mask_BxS2_bf1")):
        m = i[key].reshape(nb // 2, 2, 1, S).transpose(1, 2, 0, 3)
        a[name] = ca(np.broadcast_to(m, (2, S, nb // 2, S)).reshape(P, nb // 2, S))
    rep = lambda v: np.broadcast_to(np.asarray(v).reshape(1, -1), (P, np.asarray(v).size))
    chunks = lambda w: ca(w.reshape(-1, P, w.shape[-1]).transpose(1, 0, 2))
    a["gates"] = ca(rep(np.concatenate([i["g_xattn"], i["g_ffn"]])))
    a["rows"] = ca(np.stack([rep(i[k]) for k in ("L0_xattn_b_o", "L1_xattn_bo", "L1_ffn_bias", "L2_xattn_bo", "L3_ffn_b2",
                                                 "L3_xattn_g_out", "L2_xattn_bv")], 1))
    a["l0_wq"], a["l0_wk"], a["l0_wv"], a["l0_wo"] = i["L0_xattn_W_q"], i["L0_xattn_W_k"], i["L0_xattn_W_v"], chunks(i["L0_xattn_W_o"])
    a["l1_wq"], a["l1_wk"], a["l1_wv"], a["l1_wo"] = i["L1_xattn_Wq"], i["L1_xattn_Wk"], i["L1_xattn_Wv"], chunks(i["L1_xattn_Wo"])
    a["l2_wq"], a["l2_wk"], a["l2_wv"], a["l2_wo"] = (i["L2_xattn_W" + k] for k in "qkvo")
    a["l2_bcol"] = ca(np.stack([i["L2_xattn_bq"], i["L2_xattn_bk"]], 1))
    a["l3_wq"] = i["L3_xattn_Wq"]
    a["l3_wk"], a["l3_wv"] = ca(i["L3_xattn_Wkv"][:, :1024]), ca(i["L3_xattn_Wkv"][:, 1024:])
    a["l3_wo"] = chunks(i["L3_xattn_Wout"])
    a["gncol"] = i["L3_xattn_g_norm"].reshape(P, 1)
    a["nullk"] = ca(rep(i["L3_xattn_null_kv"][0]))
    a["nvcol"] = ca(np.concatenate([i["L3_xattn_null_kv"][1]] * 2).reshape(P, 1))
    p = np.arange(P)
    a["nvsel"] = (np.arange(16)[None, None, :] == (2 * np.arange(8)[None, :, None] + p[:, None, None] // DH)).astype(f)
    a["hm"] = (p[:, None] // 8 == np.arange(16)[None, :]).astype(f)
    a["ident"] = np.eye(P, dtype=f)
    a["causal"] = np.where((p[:, None] // S == p[None, :] // S) & (p[None, :] <= p[:, None]), 0, NEG).astype(f)
    a["iota16"] = np.broadcast_to(16.0 - np.arange(16, dtype=f), (P, 16)).copy()
    a["tri4"] = np.broadcast_to((np.arange(4)[None, :] < np.arange(4)[:, None]).astype(f), (P, 4, 4)).copy()
    ang = 2 * np.pi * ((p[:, None] * p[None, :]) % P) / P
    a["dftc"], a["dfts"] = np.cos(ang).astype(f), np.sin(ang).astype(f)
    a["wr"], a["wi"] = i["L1_ffn_w_freq_real"], i["L1_ffn_w_freq_imag"]
    a["l0f_w"] = ca(np.concatenate([i[f"L0_ffn_{k}_proj"] for k in "qvk"], 2).transpose(1, 0, 2).reshape(P, NE0 * QKV))
    a["l0f_o"] = chunks(i["L0_ffn_o_proj"].reshape(NE0 * DH, D))
    a["sim"] = i["L0_ffn_sim_matrix"]
    a["gates0"] = ca(rep(i["L0_ffn_gates"]))
    a["l2f_wr"] = ca(i["L2_ffn_gate_w"].T)
    a["l2f_bias"] = ca(rep(i["L2_ffn_gate_bias"]))
    for n, k in (("g", "gate"), ("u", "up")):
        a["l2f_" + n] = ca(np.concatenate([i[f"L2_ffn_expert_{k}"].reshape(NE2 * I2, D), i[f"L2_ffn_shared_{k}"]], 0).T)
    down = i["L2_ffn_expert_down"].transpose(0, 2, 1).reshape(NE2 * I2, D)
    a["l2f_d"] = chunks(np.concatenate([down, i["L2_ffn_shared_down"].T], 0))
    a["u1t"], a["v1"] = ca(i["L3_ffn_U1"].T), i["L3_ffn_V1"]
    a["u2t"], a["v2"] = ca(i["L3_ffn_U2"].T), i["L3_ffn_V2"]
    a["l3f_b1"] = ca(i["L3_ffn_b1"].reshape(4, P).T)
    return {k: ca(v) for k, v in a.items()}


def kernel(**inputs):
    import concourse.bacc as bacc
    from concourse.bass_utils import run_bass_kernel_spmd

    arrays = layouts({k: np.asarray(v) for k, v in inputs.items()})
    nc = bacc.Bacc("TRN2", target_bir_lowering=False, num_devices=1)
    d = {n: nc.dram_tensor("in_" + n, a.shape, mybir.dt.from_np(a.dtype), kind="ExternalInput").ap()
         for n, a in arrays.items()}
    d["out"] = nc.dram_tensor("out", arrays["x"].shape, FP, kind="ExternalOutput").ap()
    program(nc, d)
    r = run_bass_kernel_spmd(nc, [{"in_" + n: a for n, a in arrays.items()}], core_ids=[0])
    return r.results[0]["out"].reshape(inputs["x"].shape)
```
